# Optimizing a Trainium2 kernel written in Bass

```python
import numpy as np
import jax
import jax.numpy as jnp

def _softmax(x, axis=-1):
    return jax.nn.softmax(x, axis=axis)

def _gelu(x):
    return jax.nn.gelu(x, approximate=True)

def _silu(x):
    return jax.nn.silu(x)

def _sigmoid(x):
    return jax.nn.sigmoid(x)

def _layernorm(x, axis=-1, eps=1e-05):
    m = jnp.mean(x, axis=axis, keepdims=True)
    v = jnp.var(x, axis=axis, keepdims=True)
    return (x - m) / jnp.sqrt(v + eps)

def _scatter_add(tgt, idx, src, axis=0):
    return tgt.at[idx].add(src)

def _segment_sum(src, seg, n):
    return jax.ops.segment_sum(src, seg, n)
kernel_name = 'mk_gps_d1_gnn_r16_23a3ef'

def setup_inputs(seed: int=0):
    np.random.seed(seed)
    _w = jnp.asarray

    def _rec_inputs():
        import jax
        import jax.numpy as jnp
        _gk = jax.random.key(seed)
        x = -0.000364 + 1 * jax.random.normal(jax.random.fold_in(_gk, 1), (625, 768), jnp.float32)
        src = jax.random.randint(jax.random.fold_in(_gk, 2), (10000,), 0, 625, jnp.int32)
        dst = jnp.minimum((625 * jax.random.uniform(jax.random.fold_in(_gk, 3), (10000,)) ** 2.0).astype(jnp.int32), 9999)
        _o = jnp.argsort(dst, stable=True)
        src = src[_o]
        dst = dst[_o]
        edge_type_8 = jax.random.randint(jax.random.fold_in(_gk, 12), (10000,), 0, 8, jnp.int32)
        return (x, src, dst, edge_type_8)
    x, src, dst, edge_type_8 = _rec_inputs()

    def _L0_gnn_setup():
        import jax, jax.numpy as jnp
        import numpy as np
        N, IN, OUT, R, E = (1250, 768, 768, 8, 20000)

        def _rgcn_conv(x, src, dst, etype, W, root, b):
            num_nodes = x.shape[0]
            num_rel = W.shape[0]
            x_src = x[src]
            seg = dst * num_rel + etype
            sums = jax.ops.segment_sum(x_src, seg, num_segments=num_nodes * num_rel)
            cnt = jax.ops.segment_sum(jnp.ones((src.shape[0],), dtype=x.dtype), seg, num_segments=num_nodes * num_rel)
            mean = sums / jnp.maximum(cnt, 1.0)[:, None]
            mean = mean.reshape(num_nodes, num_rel, -1)
            out = jnp.einsum('nri,rio->no', mean, W)
            return out + x @ root + b
        key = jax.random.key(seed)
        ks = jax.random.split(key, 9)
        x = jax.random.normal(ks[0], (N, IN), dtype=jnp.float32)
        edge_index = jax.random.randint(ks[1], (2, E), 0, N, dtype=jnp.int64)
        edge_type = jax.random.randint(ks[2], (E,), 0, R, dtype=jnp.int64)
        s1 = 1.0 / np.sqrt(IN)
        s2 = 1.0 / np.sqrt(OUT)
        W1 = jax.random.normal(ks[3], (R, IN, OUT), dtype=jnp.float32) * s1
        root1 = jax.random.normal(ks[4], (IN, OUT), dtype=jnp.float32) * s1
        b1 = jnp.zeros((OUT,), dtype=jnp.float32)
        W2 = jax.random.normal(ks[5], (R, OUT, OUT), dtype=jnp.float32) * s2
        root2 = jax.random.normal(ks[6], (OUT, OUT), dtype=jnp.float32) * s2
        b2 = jnp.zeros((OUT,), dtype=jnp.float32)
        return {'x': x, 'edge_index': edge_index, 'edge_type': edge_type, 'W1': W1, 'root1': root1, 'b1': b1, 'W2': W2, 'root2': root2, 'b2': b2}
    _L0_gnn_all = _L0_gnn_setup()
    _L0_gnn_in = {k: v for k, v in _L0_gnn_all.items() if k in ('W1', 'root1', 'b1', 'W2', 'root2', 'b2')}
    del _L0_gnn_all

    def _L0_mix_setup():
        import jax, jax.numpy as jnp
        import numpy as np
        DIM = 768
        HEADS = 12
        HEAD_DIM = DIM // HEADS
        EPS = 1e-06
        LN_EPS = 1e-05

        def _elu1(t):
            return jax.nn.elu(t) + 1.0
        key = jax.random.key(seed)
        k1, k2, k3, k4 = jax.random.split(key, 4)
        x = jax.random.normal(k1, (8, 256, DIM), dtype=jnp.float32)
        ln_gamma = jnp.ones((DIM,), dtype=jnp.float32)
        ln_beta = jnp.zeros((DIM,), dtype=jnp.float32)
        w_qkv = jax.random.normal(k2, (3 * DIM, DIM), dtype=jnp.float32) * (1.0 / np.sqrt(DIM))
        w_proj = jax.random.normal(k3, (DIM, DIM), dtype=jnp.float32) * (1.0 / np.sqrt(DIM))
        b_proj = jax.random.normal(k4, (DIM,), dtype=jnp.float32) * 0.01
        return {'x': x, 'ln_gamma': ln_gamma, 'ln_beta': ln_beta, 'w_qkv': w_qkv, 'w_proj': w_proj, 'b_proj': b_proj}
    _L0_mix_all = _L0_mix_setup()
    _L0_mix_in = {k: v for k, v in _L0_mix_all.items() if k in ('ln_gamma', 'ln_beta', 'w_qkv', 'w_proj', 'b_proj')}
    del _L0_mix_all

    def _L0_ffn_setup():
        import math
        import jax, jax.numpy as jnp
        import numpy as np
        B, L, D = (8, 256, 768)
        E = 16
        TOP_K = 2
        F_EXP = 4 * D
        F_SH = F_EXP * 2 // 4
        key = jax.random.key(seed)
        ks = jax.random.split(key, 8)
        s = lambda fan_in: 1.0 / math.sqrt(fan_in)
        return {'hidden_states': jax.random.normal(ks[0], (B, L, D), jnp.float32), 'gate_weight': jax.random.uniform(ks[1], (E, D), jnp.float32, -s(D), s(D)), 'Wg': jax.random.uniform(ks[2], (E, F_EXP, D), jnp.float32, -s(D), s(D)), 'Wu': jax.random.uniform(ks[3], (E, F_EXP, D), jnp.float32, -s(D), s(D)), 'Wd': jax.random.uniform(ks[4], (E, D, F_EXP), jnp.float32, -s(F_EXP), s(F_EXP)), 'Ws_g': jax.random.uniform(ks[5], (F_SH, D), jnp.float32, -s(D), s(D)), 'Ws_u': jax.random.uniform(ks[6], (F_SH, D), jnp.float32, -s(D), s(D)), 'Ws_d': jax.random.uniform(ks[7], (D, F_SH), jnp.float32, -s(F_SH), s(F_SH))}
    _L0_ffn_all = _L0_ffn_setup()
    _L0_ffn_in = {k: v for k, v in _L0_ffn_all.items() if k in ('gate_weight', 'Wg', 'Wu', 'Wd', 'Ws_g', 'Ws_u', 'Ws_d')}
    del _L0_ffn_all
    return {'x': x, 'src': src, 'dst': dst, 'edge_type_8': edge_type_8, 'L0_gnn_W1': _L0_gnn_in['W1'], 'L0_gnn_root1': _L0_gnn_in['root1'], 'L0_gnn_b1': _L0_gnn_in['b1'], 'L0_gnn_W2': _L0_gnn_in['W2'], 'L0_gnn_root2': _L0_gnn_in['root2'], 'L0_gnn_b2': _L0_gnn_in['b2'], 'L0_mix_ln_gamma': _L0_mix_in['ln_gamma'], 'L0_mix_ln_beta': _L0_mix_in['ln_beta'], 'L0_mix_w_qkv': _L0_mix_in['w_qkv'], 'L0_mix_w_proj': _L0_mix_in['w_proj'], 'L0_mix_b_proj': _L0_mix_in['b_proj'], 'L0_ffn_gate_weight': _L0_ffn_in['gate_weight'], 'L0_ffn_Wg': _L0_ffn_in['Wg'], 'L0_ffn_Wu': _L0_ffn_in['Wu'], 'L0_ffn_Wd': _L0_ffn_in['Wd'], 'L0_ffn_Ws_g': _L0_ffn_in['Ws_g'], 'L0_ffn_Ws_u': _L0_ffn_in['Ws_u'], 'L0_ffn_Ws_d': _L0_ffn_in['Ws_d']}

def reference(x, src, dst, edge_type_8, L0_gnn_W1, L0_gnn_root1, L0_gnn_b1, L0_gnn_W2, L0_gnn_root2, L0_gnn_b2, L0_mix_ln_gamma, L0_mix_ln_beta, L0_mix_w_qkv, L0_mix_w_proj, L0_mix_b_proj, L0_ffn_gate_weight, L0_ffn_Wg, L0_ffn_Wu, L0_ffn_Wd, L0_ffn_Ws_g, L0_ffn_Ws_u, L0_ffn_Ws_d):
    import jax
    import jax.numpy as jnp

    def _L0_gnn_ref(x, edge_index, edge_type, W1, root1, b1, W2, root2, b2):
        import jax, jax.numpy as jnp
        import numpy as np
        N, IN, OUT, R, E = (1250, 768, 768, 8, 20000)

        def _rgcn_conv(x, src, dst, etype, W, root, b):
            num_nodes = x.shape[0]
            num_rel = W.shape[0]
            x_src = x[src]
            seg = dst * num_rel + etype
            sums = jax.ops.segment_sum(x_src, seg, num_segments=num_nodes * num_rel)
            cnt = jax.ops.segment_sum(jnp.ones((src.shape[0],), dtype=x.dtype), seg, num_segments=num_nodes * num_rel)
            mean = sums / jnp.maximum(cnt, 1.0)[:, None]
            mean = mean.reshape(num_nodes, num_rel, -1)
            out = jnp.einsum('nri,rio->no', mean, W)
            return out + x @ root + b
        src, dst = (edge_index[0], edge_index[1])
        h = _rgcn_conv(x, src, dst, edge_type, W1, root1, b1)
        h = jax.nn.relu(h)
        out = _rgcn_conv(h, src, dst, edge_type, W2, root2, b2)
        return out

    def _L0_mix_ref(x, ln_gamma, ln_beta, w_qkv, w_proj, b_proj):
        import jax, jax.numpy as jnp
        import numpy as np
        DIM = 768
        HEADS = 12
        HEAD_DIM = DIM // HEADS
        EPS = 1e-06
        LN_EPS = 1e-05

        def _elu1(t):
            return jax.nn.elu(t) + 1.0
        bsz, n, dim = x.shape
        mu = jnp.mean(x, axis=-1, keepdims=True)
        var = jnp.mean(jnp.square(x - mu), axis=-1, keepdims=True)
        y = (x - mu) * jax.lax.rsqrt(var + LN_EPS) * ln_gamma + ln_beta
        qkv = jnp.einsum('bnd,ed->bne', y, w_qkv)
        qkv = qkv.reshape(bsz, n, 3, HEADS, HEAD_DIM)
        qkv = jnp.transpose(qkv, (2, 0, 3, 1, 4))
        q, k, v = (_elu1(qkv[0]), _elu1(qkv[1]), qkv[2])
        kv = jnp.einsum('bhnd,bhne->bhde', k, v)
        k_sum = jnp.sum(k, axis=2)
        z = 1.0 / (jnp.einsum('bhnd,bhd->bhn', q, k_sum) + EPS)
        out = jnp.einsum('bhnd,bhde->bhne', q, kv) * z[..., None]
        out = jnp.transpose(out, (0, 2, 1, 3)).reshape(bsz, n, dim)
        return jnp.einsum('bnd,ed->bne', out, w_proj) + b_proj

    def _L0_ffn_ref(hidden_states, gate_weight, Wg, Wu, Wd, Ws_g, Ws_u, Ws_d):
        import math
        import jax, jax.numpy as jnp
        import numpy as np
        B, L, D = (8, 256, 768)
        E = 16
        TOP_K = 2
        F_EXP = 4 * D
        F_SH = F_EXP * 2 // 4
        b, l, d = hidden_states.shape
        n = b * l
        x = hidden_states.reshape(n, d)
        scores = jax.nn.sigmoid(x @ gate_weight.T)
        capacity = math.ceil(n / E * TOP_K)
        topk_score, topk_ids = jax.lax.top_k(scores.T, capacity)
        xg = x[topk_ids]
        gate = jax.nn.silu(jnp.einsum('ecd,efd->ecf', xg, Wg))
        up = jnp.einsum('ecd,efd->ecf', xg, Wu)
        out = jnp.einsum('ecf,edf->ecd', gate * up, Wd)
        out = out * topk_score[..., None]
        y = jnp.zeros((n, d), x.dtype).at[topk_ids.reshape(-1)].add(out.reshape(-1, d))
        y = y.reshape(b, l, d)
        shared = jax.nn.silu(hidden_states @ Ws_g.T) * (hidden_states @ Ws_u.T) @ Ws_d.T
        return y + shared
    edge_index = jnp.stack([src, dst])
    xn = _layernorm(x, axis=-1)
    x = x + _L0_gnn_ref(xn, edge_index, edge_type_8, L0_gnn_W1, L0_gnn_root1, L0_gnn_b1, L0_gnn_W2, L0_gnn_root2, L0_gnn_b2) + _L0_mix_ref(xn[None], L0_mix_ln_gamma, L0_mix_ln_beta, L0_mix_w_qkv, L0_mix_w_proj, L0_mix_b_proj)[0]
    x = x + _L0_ffn_ref(_layernorm(x, axis=-1)[None], L0_ffn_gate_weight, L0_ffn_Wg, L0_ffn_Wu, L0_ffn_Wd, L0_ffn_Ws_g, L0_ffn_Ws_u, L0_ffn_Ws_d)[0]
    return x

_drawn_inputs = setup_inputs


def setup_inputs(seed=0):
    import zlib

    import numpy as np

    out = dict(_drawn_inputs(seed))
    spreads = {'L0_gnn_b1': (0.0, 0.1),
     'L0_gnn_b2': (0.0, 0.3),
     'L0_mix_ln_gamma': (1.0, 0.6),
     'L0_mix_ln_beta': (0.0, 0.305)}
    factors = {'L0_mix_b_proj': 22.282}
    for name, (base, spread) in spreads.items():
        noise = np.random.default_rng([zlib.crc32(name.encode()), seed]).standard_normal(out[name].shape)
        drawn = base * np.exp(spread * noise) if base else spread * noise
        out[name] = jnp.asarray(drawn.astype(out[name].dtype))
    for name, factor in factors.items():
        out[name] = (out[name] * factor).astype(out[name].dtype)
    return out
```

```python
from contextlib import ExitStack

import numpy as np
import concourse.bass as bass
from concourse import mybir

F32 = mybir.dt.float32
F32R = mybir.dt.float32r
I32 = mybir.dt.int32
U32 = mybir.dt.uint32
BF16 = mybir.dt.bfloat16
ALU = mybir.AluOpType
ACT = mybir.ActivationFunctionType
AX = mybir.AxisListType

P = 128
N = 625
D = 768
R = 8
E = 10000
NT, TN = 5, 125
KT = D // P
NC, HC = 628, 314
HD = D // 2
NE, CAP = 16, 79
CS = 80
FE, FS = 3072, 1536
EB = E // TN
GB = 4
NG = EB // GB
ROWS = R * NC
TABLE = 128 * 24544
DUMP = N * ROWS
ZC = TABLE // P // 8
LATER = 2048.0
PIECE = KT * P
NRAW, NSPL = 6, 3
NQ, QT = 8, 3
CHUNK = QT * D
NRING, NR1 = 8, 4
EC = 3 * NQ
SF = FS // NE
ROUNDS = CS // 8
MJ = 24
EPS_LN = 1e-5
EPS_Z = 1e-6


def build(nc, a, out):
    outer = ExitStack()
    with outer:
        def sb(name, shape, dt=F32, stack=outer):
            return stack.enter_context(nc.sbuf_tensor(name, shape, dt))

        def sem(name):
            return outer.enter_context(nc.semaphore(name))

        table = nc.dram_tensor("edge_table", (TABLE, 1), F32).ap()
        keys_dram = nc.dram_tensor("edge_keys", (EB, TN), F32).ap()
        mix_dram = nc.dram_tensor("mix_spill", (P, KT * NC), F32).ap()
        xf_dram = nc.dram_tensor("ffn_input", (N, D), F32).ap()

        ps = outer.enter_context(nc.psum_tensor("ps", [P, 4, 1024], F32))
        psh = ps.rearrange("p k (h c) -> p k h c", h=2)

        ident = sb("ident", [P, P])
        ones = sb("ones", [P, P])
        onesr = sb("onesr", [P, P], F32R)
        eps_ln = sb("eps_ln", [P, 1])
        vecs = sb("vecs", [P, 5, KT])
        acc = sb("acc", [P, KT, NC])
        ring = sb("ring", [P, NR1, CHUNK])

        phase_a = ExitStack()
        sa = lambda name, shape, dt=F32: sb(name, shape, dt, phase_a)
        xh = sa("xh", [TN, NT, D], F32R)
        xl = sa("xl", [TN, NT, D], F32R)
        band = sa("band", [P, (2 * GB - 1) * TN])
        ecol = sa("ecol", [TN, 3, EB], I32)
        ef = sa("ef", [TN, 3, EB])
        key = sa("key", [TN, EB])
        to_dump = sa("to_dump", [TN, EB])
        dump_cell = sa("dump_cell", [P, 1])
        keyT = sa("keyT", [EB, TN])
        keyrow = sa("keyrow", [TN, 2, GB * TN])
        eq = sa("eq", [TN, GB, GB * TN], BF16)
        cnt4 = sa("cnt4", [TN, 2, GB])
        later4 = sa("later4", [TN, GB])
        off4 = sa("off4", [TN, GB])
        idx4 = sa("idx4", [TN, 2, GB], I32)
        stats = sa("stats", [TN, 2, NT, 2, 6])
        mv = sa("mv", [TN, 2, NT, 2])
        rstd = sa("rstd", [TN, 2, NT])
        wraw = sa("wraw", [P, NRAW, PIECE])
        wh = sa("wh", [P, NSPL, PIECE], F32R)
        wl = sa("wl", [P, NSPL, PIECE], F32R)
        tmp = sa("tmp", [P, 2, 640])
        tmp2 = sa("tmp2", [P, 2, 640])
        inv = sa("inv", [P, NC])
        kv_bd = sa("kv_bd", [P, KT, P])
        ks_bd = sa("ks_bd", [P, KT, P])
        early = ExitStack()
        nat = sb("nat", [TN, NT, D], F32, early)
        kpc = sb("kpc", [TN, 2, NT, P], F32, early)
        vpc = sb("vpc", [TN, 2, NT, P], F32, early)
        early.close()
        cbuf = sa("cbuf", [TN, 2, NT * NC], F32R)
        sa("behind_cbuf", [TN, 160])
        early = ExitStack()
        xn = sb("xn", [TN, NT, D], F32, early)
        early.close()
        mh = sa("mh", [P, KT, NC], F32R)
        ml = sa("ml", [P, KT, NC], F32R)
        phase_a.close()
        phase_b = outer.enter_context(ExitStack())
        sbb = lambda name, shape, dt=F32: sb(name, shape, dt, phase_b)
        x2 = sbb("x2", [TN, NT, D])
        early = ExitStack()
        mixb = sb("mixb", [P, KT, NC], F32, early)
        early.close()
        early = ExitStack()
        xf = sb("xf", [TN, NT, D], F32, early)
        early.close()
        ring2 = sbb("ring2", [P, NRING - NR1, CHUNK])
        fh = sbb("fh", [P, KT, NC], F32R)
        fl = sbb("fl", [P, KT, NC], F32R)
        sraw = sbb("sraw", [P, 2 * KT * SF])
        sgh = sbb("sgh", [P, 2 * KT * SF], F32R)
        sgl = sbb("sgl", [P, 2 * KT * SF], F32R)
        draw = sbb("draw", [SF, D])
        sdh = sbb("sdh", [SF, D], F32R)
        sdl = sbb("sdl", [SF, D], F32R)
        hs = sbb("hs", [SF, NC])
        hsh = sbb("hsh", [SF, NC], F32R)
        hsl = sbb("hsl", [SF, NC], F32R)
        sgate = sbb("sgate", [SF, 2, HC])
        gate = sbb("gate", [P, 2, QT * CS])
        hid = sbb("hid", [P, NQ, QT, CS])
        xg = sbb("xg", [CS, D])
        xgT = sbb("xgT", [P, KT, CS])
        outT = sbb("outT", [P, KT, CS])
        oe = sbb("oe", [CS, D])
        oeh = sbb("oeh", [CS, D], F32R)
        oel = sbb("oel", [CS, D], F32R)
        onehot = sbb("onehot", [CS, NC], F32R)
        iota_n = sbb("iota_n", [CS, NC])
        gw = sbb("gw", [P, KT, NE])
        ez = sbb("ez", [NE, NC])
        score = sbb("score", [NE, 2, NC])
        top = sbb("top", [NE, CS])
        topi = sbb("topi", [NE, CS], U32)
        topf = sbb("topf", [NE, CS])
        slot_score = sbb("slot_score", [CS, NE])
        slot_tok = sbb("slot_tok", [CS, NE])
        slot_idx = sbb("slot_idx", [CS, NE], I32)
        stats3 = sbb("stats3", [TN, NT, 2, 6])
        mv3 = sbb("mv3", [TN, NT, 2])
        rstd3 = sbb("rstd3", [TN, NT])

        x_in = sem("x_in"); edges_in = sem("edges_in"); vecs_in = sem("vecs_in")
        const_step = sem("const_step"); const_ready = sem("const_ready")
        zeros_ready = sem("zeros_ready"); table_zero = sem("table_zero")
        dve_step = sem("dve_step"); sqrt_done = sem("sqrt_done"); tmp_zero = sem("tmp_zero"); stats_done = sem("stats_done")
        yn_ready = sem("yn_ready"); key_ready = sem("key_ready"); keyT_done = sem("keyT_done")
        keyT_ready = sem("keyT_ready"); keys_stored = sem("keys_stored")
        row_in = [sem("row_in0"), sem("row_in1")]
        compared = sem("compared"); group_ready = sem("group_ready"); scattered = sem("scattered")
        raw_in = [sem(f"raw_in{i}") for i in range(NRAW)]
        w_hi = sem("w_hi"); w_lo = sem("w_lo")
        c_in = [sem("c_in0"), sem("c_in1")]
        pe_done = sem("pe_done"); evac = sem("evac")
        hi_ready = sem("hi_ready"); lo_ready = sem("lo_ready")
        xh_done = sem("xh_done"); xl_ready = sem("xl_ready")
        min_ready = sem("min_ready"); exp_ready = sem("exp_ready"); recip_step = sem("recip_step")
        cnt_done = sem("cnt_done"); inv_step = sem("inv_step"); inv_ready = sem("inv_ready")
        h_ready = sem("h_ready"); mix_out = sem("mix_out"); mix_in = sem("mix_in")
        xraw_in = sem("xraw_in"); mix_added = sem("mix_added"); out_done = sem("out_done")

        used = sem("used")
        ring_in = [sem(f"ring_in{n}") for n in range(NRING)]
        xf_ready = sem("xf_ready"); xf_stored = sem("xf_stored"); gw_in = sem("gw_in")
        fh_ready = sem("fh_ready"); fl_ready = sem("fl_ready"); pads_zero = sem("pads_zero")
        ez_ready = sem("ez_ready"); top_ready = sem("top_ready"); idx_ready = sem("idx_ready")
        iota_ready = sem("iota_ready"); gathered = sem("gathered")
        sg_in = sem("sg_in"); sd_in = sem("sd_in")
        sg_hi = sem("sg_hi"); sg_lo = sem("sg_lo"); sd_hi = sem("sd_hi"); sd_lo = sem("sd_lo")
        shared_done = sem("shared_done"); silu_ready = sem("silu_ready"); hid_ready = sem("hid_ready")
        hs_hi = sem("hs_hi"); hs_lo = sem("hs_lo"); onehot_ready = sem("onehot_ready")
        down_copied = sem("down_copied"); oe_hi = sem("oe_hi"); oe_lo = sem("oe_lo")
        misc_done = sem("misc_done"); misc_evac = sem("misc_evac")

        J_Y = 0
        J_Q = J_Y + KT
        J_KV = J_Q + KT
        K_JOB = [J_KV] + [J_KV + 2 + 3 * (o - 1) for o in range(1, KT)]
        V_JOB = [j + 1 for j in K_JOB]
        P_JOB = [J_KV + 4 + 3 * o for o in range(KT - 1)] + [J_KV + 3 * KT - 1]
        J_ATT = J_KV + 3 * KT
        J_PROJ = J_ATT + 2 * KT
        J_XT = J_PROJ + KT
        J_ROOT1 = J_XT + 2 * KT
        J_REL1 = J_ROOT1 + KT
        RJ = 2 * KT
        J_HN = J_REL1 + R * RJ
        J_ROOT2 = J_HN + NT
        J_REL2 = J_ROOT2 + KT
        J_X2 = J_REL2 + R * RJ
        J_F = J_X2 + NT
        J_END = J_F + KT
        W_Q, W_KV = 0, KT
        W_PROJ = W_KV + 2 * KT
        W_ROOT1 = W_PROJ + KT
        W_REL1 = W_ROOT1 + KT
        W_ROOT2 = W_REL1 + R * KT
        W_REL2 = W_ROOT2 + KT
        W_END = W_REL2 + R * KT
        L_Y, L_ATT = 0, KT
        L_REL1 = 2 * KT
        L_H = L_REL1 + R * KT
        L_REL2 = L_H + KT

        def slot(j):
            return j % 3

        def piece(t, w):
            return t[:, w % NSPL, :].rearrange("p (k m) -> p k m", k=KT)

        def w_src(w):
            if w < W_KV:
                return a["wqkv"][w]
            if w < W_PROJ:
                o, v = divmod(w - W_KV, 2)
                return a["wqkv"][KT * (1 + v) + o]
            if w < W_ROOT1:
                return a["wproj"][w - W_PROJ]
            if w < W_REL1:
                return a["root1"][w - W_ROOT1]
            if w < W_REL2:
                return a["root2"][w - W_ROOT2]
            return a["wproj"][w - W_END]

        def halves(t):
            return t.rearrange("p (h c) -> p h c", h=2)

        def node_tiles(t):
            return t[:, 0:N].rearrange("p (t c) -> p t c", t=NT)

        bank = ps.rearrange("p k (h c) -> p (k h) c", h=2)
        M0 = 3
        M_TURN_X = 0
        M_SH = list(range(2, 10)) + [12, 13]
        M_TURN_O = 10
        M_SCATTER = 14

        def mbank(m):
            return 5 + m % 3

        order = [("g", 0), ("u", 0)]
        for q in range(1, NQ):
            order += [("g", q), ("u", q), ("d", q - 1)]
        order += [("d", NQ - 1)]
        chunk = {x: c for c, x in enumerate(order)}

        def ring_slot(c):
            c %= NRING
            return ring[:, c, :] if c < NR1 else ring2[:, c - NR1, :]

        block = outer.enter_context(nc.Block())

        @block.sync
        def _(sp):
            sp.dma_start(nat[:, :, :], a["x"].rearrange("(t p) d -> p t d", p=TN)).then_inc(x_in, 16)
            for n, e in enumerate(("type", "dst", "src")):
                sp.dma_start(ecol[:, n, :], a[e].rearrange("(p b) -> p b", b=EB)).then_inc(edges_in, 16)
            for n, v in enumerate(("gamma", "beta", "b_proj", "b1", "b2")):
                sp.dma_start(vecs[:, n, :], a[v]).then_inc(vecs_in, 16)

            def load_piece(w):
                if w >= NRAW:
                    sp.wait_ge(w_lo, w - NRAW + 1)
                sp.dma_start(wraw[:, w % NRAW, :], w_src(w)).then_inc(raw_in[w % NRAW], 16)

            def load_row(g):
                if g >= 2:
                    sp.wait_ge(group_ready, g - 1)
                src = keys_dram[g * GB:(g + 1) * GB, :].rearrange("b c -> (b c)").unsqueeze(0)
                sp.dma_start(keyrow[:, g % 2, :], src.broadcast_to([TN, GB * TN])).then_inc(row_in[g % 2], 16)

            for w in range(NRAW):
                load_piece(w)
            def first_chunk(c):
                m, q = order[c]
                sp.dma_start(ring_slot(c), a["W" + m][q]).then_inc(ring_in[c % NRING], 16)

            sp.wait_ge(keyT_ready, 1)
            sp.dma_start(keys_dram, keyT[:, :]).then_inc(keys_stored, 16)
            sp.wait_ge(keys_stored, 16)
            load_row(0)
            load_row(1)
            for w in range(NRAW, W_REL1):
                g = w - NRAW + 2
                if g < NG:
                    load_row(g)
                load_piece(w)
            sp.wait_ge(table_zero, 8 * 16)
            for c in range(NR1):
                first_chunk(c)
            sp.wait_ge(evac, J_PROJ + KT)
            sp.dma_start(mix_dram, acc[:, :, :].rearrange("p k n -> p (k n)")).then_inc(mix_out, 16)

            def relations(wt, base_j, base_w):
                with sp.Fori(0, R // 2) as i:
                    for u in range(2):
                        sp.wait_ge(pe_done, i * (2 * RJ) + (base_j + (u - 2) * RJ + KT))
                        src = table[0:DUMP, :].rearrange("(t p r n) o -> p r t (n o)", t=NT, p=TN, r=R)
                        sp.dma_start(cbuf[:, u, :].bitcast(F32).rearrange("p (t n) -> p t n", t=NT),
                                     src[:, bass.ds(i * 2 + u, 1), :, :].rearrange("p r t n -> p (r t) n")
                                     ).then_inc(c_in[u], 16)
                        for o in range(KT):
                            sp.wait_ge(w_lo, i * (2 * KT) + (base_w + u * KT + o - NRAW + 1))
                            sp.dma_start(wraw[:, o, :], wt[bass.ds(i * (2 * KT) + (u * KT + o), 1)].rearrange(
                                "a p f -> (a p) f")).then_inc(raw_in[o], 16)

            sp.wait_ge(scattered, 16 * EB)
            relations(a["W1"], J_REL1, W_REL1)
            for w in range(W_ROOT2, W_REL2):
                load_piece(w)
            relations(a["W2"], J_REL2, W_REL2)
            for w in range(W_END, W_END + NSPL):
                load_piece(w)
            sp.wait_ge(pe_done, J_X2 - KT)
            sp.wait_ge(mix_out, 16)
            sp.dma_start(mixb[:, :, :].rearrange("p k n -> p (k n)"), mix_dram).then_inc(mix_in, 16)
            sp.dma_start(x2[:, :, :], a["x"].rearrange("(t p) d -> p t d", p=TN)).then_inc(xraw_in, 16)
            sp.wait_ge(pe_done, J_X2)
            sp.wait_ge(w_lo, W_END + NSPL)
            sp.dma_start(gw[:, :, :], a["gate_weight"]).then_inc(gw_in, 16)

            def load_shared(e):
                sp.dma_start(sraw[:, :], a["Ws_gu"][bass.ds(e, 1)].rearrange("a p f -> (a p) f")
                             ).then_inc(sg_in, 16)

            def load_shared_down(e):
                sp.dma_start(draw[:, :], a["Ws_d"][bass.ds(e, 1)].rearrange("a p f -> (a p) f")
                             ).then_inc(sd_in, 16)

            load_shared(0)
            load_shared_down(0)
            sp.wait_ge(xf_ready, 1)
            sp.dma_start(xf_dram.rearrange("(t p) d -> p t d", p=TN), xf[:, :, :]).then_inc(xf_stored, 16)
            sp.wait_ge(xf_stored, 16)
            sp.wait_ge(pe_done, J_END)
            for c in range(NR1, NRING):
                first_chunk(c)
            sp.wait_ge(sg_lo, 1)
            load_shared(1)
            sp.wait_ge(sd_lo, 1)
            load_shared_down(1)
            for c in range(NRING, EC):
                sp.wait_ge(used, c - NRING + 1)
                first_chunk(c)
            with sp.Fori(1, NE) as e:
                for c, (m, q) in enumerate(order):
                    sp.wait_ge(used, e * EC + (c - NRING + 1))
                    sp.dma_start(ring_slot(c), a["W" + m][bass.ds(e * NQ + q, 1)].rearrange("a p f -> (a p) f")
                                 ).then_inc(ring_in[c % NRING], 16)
                    if c == NR1:
                        sp.wait_ge(sg_lo, e + 1)
                        load_shared((e + 1) % NE)
                    if c == NRING + 1:
                        sp.wait_ge(sd_lo, e + 1)
                        load_shared_down((e + 1) % NE)
            sp.wait_ge(sg_in, 16 * (NE + 1))
            sp.wait_ge(sd_in, 16 * (NE + 1))
            sp.wait_ge(misc_evac, M0 + MJ * NE)
            sp.dma_start(out.rearrange("(t p) d -> p t d", p=TN), x2[:, :, :]).then_inc(out_done, 16)
            sp.wait_ge(out_done, 16)

        @block.gpsimd
        def _(pool):
            zeros = ring[:, :, :].rearrange("p s c -> p (s c)")[:, 0:ZC]
            pool.memset(zeros, 0.0).then_inc(zeros_ready, 1)
            pool.memset(ident[:, :], 0.0).then_inc(const_step, 1)
            pool.memset(band[:, :], 1.0).then_inc(const_step, 1)
            pool.memset(ones[:, :], 1.0).then_inc(const_step, 1)
            pool.memset(onesr[:, :].bitcast(F32), 1.0).then_inc(const_step, 1)
            pool.memset(eps_ln[:, :], EPS_LN).then_inc(const_step, 1)
            pool.memset(kv_bd[:, :, :], 0.0).then_inc(const_step, 1)
            pool.memset(ks_bd[:, :, :], 0.0).then_inc(const_step, 1)
            pool.wait_ge(const_step, 7)
            pool.affine_select(out=ident[:, :], in_=ident[:, :], compare_op=ALU.not_equal, fill=1.0, base=0,
                               pattern=[[-1, P]], channel_multiplier=1).then_inc(const_ready, 1)
            pool.affine_select(out=band[:, :], in_=band[:, :], compare_op=ALU.is_ge, fill=LATER,
                               base=(GB - 1) * TN, pattern=[[-1, (2 * GB - 1) * TN]],
                               channel_multiplier=1).then_inc(const_ready, 1)
            pool.iota(dump_cell[:, :], pattern=[[0, 1]], base=DUMP, channel_multiplier=1,
                      allow_small_or_imprecise_dtypes=True).then_inc(const_ready, 1)
            pool.wait_ge(table_zero, 8 * 16)
            for g in range(NG):
                pool.wait_ge(group_ready, g + 1)
                if g >= 1:
                    pool.wait_ge(scattered, 16 * GB * g)
                for b in range(GB):
                    pool.indirect_dma_start(
                        out=table, out_offset=bass.IndirectOffsetOnAxis(ap=idx4[:, g % 2, b:b + 1], axis=0),
                        in_=cnt4[:, g % 2, b:b + 1], in_offset=None, compute_op=ALU.add
                    ).then_inc(scattered, 16)
            pool.wait_ge(pe_done, J_X2)
            pool.wait_ge(lo_ready, L_REL2 + R * KT)
            pool.wait_ge(w_lo, W_END + NSPL)
            pool.iota(iota_n[:, :], pattern=[[1, NC]], base=0, channel_multiplier=0,
                      allow_small_or_imprecise_dtypes=True).then_inc(iota_ready, 1)
            pool.wait_ge(idx_ready, 1)
            pool.wait_ge(xf_stored, 16)
            for e in range(NE):
                if e:
                    pool.wait_ge(misc_done, M0 + MJ * (e - 1) + M_TURN_X + 2)
                pool.indirect_dma_start(
                    out=xg[:, :], out_offset=None, in_=xf_dram,
                    in_offset=bass.IndirectOffsetOnAxis(ap=slot_idx[:, e:e + 1], axis=0)
                ).then_inc(gathered, 16)

        @block.scalar
        def _(act):
            act.wait_ge(zeros_ready, 1)
            zeros = ring[:, :, :].rearrange("p s c -> p (s c)")[:, 0:ZC]
            for z in range(8):
                act.dma_start(table.rearrange("(z p c) o -> z p (c o)", z=8, p=P)[z], zeros).then_inc(table_zero, 16)

            def split_weight(w):
                act.wait_ge(raw_in[w % NRAW], 16 * (w // NRAW + 1))
                act.copy(wh[:, w % NSPL, :], wraw[:, w % NRAW, :]).then_inc(w_hi, 1)

            for ln in range(2):
                act.wait_ge(const_ready, 3)
                act.wait_ge(stats_done, ln + 1)
                act.activation(rstd[:, ln, :], mv[:, ln, :, 1], ACT.Sqrt, bias=eps_ln[0:TN, :]).then_inc(sqrt_done, 1)

            for w in range(NSPL):
                split_weight(w)

            def hi(value, k, job):
                act.wait_ge(evac, job)
                act.copy(mh[:, k, :], tmp[:, k % 2, 0:NC]).then_inc(hi_ready, 1)

            def next_weight(j, w):
                act.wait_ge(pe_done, j + 1)
                split_weight(w + NSPL)

            def exponent(n):
                act.wait_ge(min_ready, n + 1)
                act.activation(tmp2[:, n % 2, :], tmp[:, n % 2, :], ACT.Exp).then_inc(exp_ready, 1)

            for k in range(KT):
                hi(L_Y + k, k, J_Y + k + 1)
            for o in range(KT):
                next_weight(J_Q + o, W_Q + o)
                exponent(o)
            for o in range(KT):
                next_weight(K_JOB[o], W_KV + 2 * o)
                exponent(KT + o)
                next_weight(V_JOB[o], W_KV + 2 * o + 1)
            for h in range(KT):
                hi(L_ATT + h, h, J_ATT + 2 * h + 2)
            for o in range(KT):
                next_weight(J_PROJ + o, W_PROJ + o)
            for o in range(KT):
                next_weight(J_ROOT1 + o, W_ROOT1 + o)

            def relations(base_j, base_w):
                with act.Fori(0, R // 2) as i:
                    for u in range(2):
                        j, w = base_j + u * RJ, base_w + u * KT
                        for k in range(KT):
                            act.wait_ge(evac, i * (2 * RJ) + (j + k + 1))
                            act.copy(mh[:, k, :], tmp[:, k % 2, 0:NC]).then_inc(hi_ready, 1)
                        for o in range(KT):
                            act.wait_ge(pe_done, i * (2 * RJ) + (j + KT + o + 1))
                            nw = w + o + NSPL
                            act.wait_ge(raw_in[nw % NRAW], i * 32 + 16 * (nw // NRAW + 1))
                            act.copy(wh[:, nw % NSPL, :], wraw[:, nw % NRAW, :]).then_inc(w_hi, 1)

            relations(J_REL1, W_REL1)
            for k in range(KT):
                act.wait_ge(h_ready, k + 1)
                act.copy(mh[:, k, :], acc[:, k, :]).then_inc(hi_ready, 1)
            for t in range(NT):
                act.wait_ge(pe_done, J_HN + t + 1)
                act.copy(xh[:, t, :], ps[0:TN, slot(J_HN + t), 0:D]).then_inc(xh_done, 1)
            for o in range(KT):
                next_weight(J_ROOT2 + o, W_ROOT2 + o)
            relations(J_REL2, W_REL2)

            act.wait_ge(stats_done, 3)
            act.activation(rstd3[:, :], mv3[:, :, 1], ACT.Sqrt, bias=eps_ln[0:TN, :]).then_inc(sqrt_done, 1)
            act.wait_ge(pads_zero, 2)
            for k in range(KT):
                act.wait_ge(evac, J_F + k + 1)
                act.copy(fh[:, k, 0:N], acc[:, k, 0:N]).then_inc(fh_ready, 1)
            for h in range(2):
                act.wait_ge(misc_done, h + 1)
                act.activation(ez[:, h * HC:(h + 1) * HC], bank[0:NE, mbank(h), 0:HC], ACT.Exp,
                               scale=-1.0).then_inc(ez_ready, 1)
            act.wait_ge(sg_in, 16)
            act.copy(sgh[:, :], sraw[:, :]).then_inc(sg_hi, 1)
            act.wait_ge(sd_in, 16)
            act.copy(sdh[:, :], draw[:, :]).then_inc(sd_hi, 1)

            with act.Fori(0, NE) as e:
                def shared_half(h):
                    act.wait_ge(shared_done, e * 2 + (h + 1))
                    act.activation(sgate[:, h, :], bank[0:SF, 2 * h, 0:HC], ACT.Silu).then_inc(silu_ready, 1)
                    act.wait_ge(hid_ready, e * (NQ + 2) + (h + 1))
                    act.copy(hsh[:, h * HC:(h + 1) * HC], hs[:, h * HC:(h + 1) * HC]).then_inc(hs_hi, 1)

                shared_half(0)
                shared_half(1)
                act.wait_ge(sg_in, e * 16 + 32)
                act.copy(sgh[:, :], sraw[:, :]).then_inc(sg_hi, 1)
                for q in range(NQ):
                    act.wait_ge(used, e * EC + (chunk["u", q] + 1))
                    act.activation(gate[:, q % 2, :], bank[:, q % 4, 0:QT * CS], ACT.Silu).then_inc(silu_ready, 1)
                act.wait_ge(used, e * EC + EC)
                act.copy(outT[:, :, :].rearrange("p k c -> p (k c)"), bank[:, 4, 0:KT * CS]).then_inc(down_copied, 1)
                for h in range(2):
                    act.wait_ge(misc_evac, e * MJ + (M0 + M_TURN_O + h + 1))
                    act.copy(oeh[:, h * HD:(h + 1) * HD], oe[:, h * HD:(h + 1) * HD]).then_inc(oe_hi, 1)
                act.wait_ge(sd_in, e * 16 + 32)
                act.wait_ge(misc_done, e * MJ + (M0 + M_SH[-1] + 1))
                act.copy(sdh[:, :], draw[:, :]).then_inc(sd_hi, 1)

        @block.vector
        def _(dve):
            steps = [0]

            def then(ins):
                steps[0] += 1
                ins.then_inc(dve_step, 1)
                dve.wait_ge(dve_step, steps[0])

            dve.memset(tmp[:, :, :], 0.0).then_inc(tmp_zero, 1)
            dve.wait_ge(edges_in, 48)
            then(dve.tensor_copy(ef[:, :, :], ecol[:, :, :]))
            then(dve.scalar_tensor_tensor(out=key[:, :], in0=ef[:, 0, :], scalar=float(NC), in1=ef[:, 1, :],
                                          op0=ALU.mult, op1=ALU.add))
            dve.scalar_tensor_tensor(out=key[:, :], in0=ef[:, 2, :], scalar=float(ROWS), in1=key[:, :],
                                     op0=ALU.mult, op1=ALU.add).then_inc(key_ready, 1)
            dve.wait_ge(const_ready, 3)
            dve.wait_ge(key_ready, 1)
            then(dve.tensor_scalar(to_dump[:, :], key[:, :], -1.0, dump_cell[0:TN, 0:1], ALU.mult, ALU.add))

            dve.wait_ge(x_in, 16)
            for ln, (src, dst) in enumerate(((nat, xn), (xn, nat))):
                for t in range(NT):
                    for h in range(2):
                        ins = dve.bn_stats(stats[:, ln, t, h, :], src[:, t, h * HD:(h + 1) * HD])
                then(ins)
                for t in range(NT):
                    ins = dve.bn_aggr(mv[:, ln, t, :], stats[:, ln, t, :, :])
                ins.then_inc(stats_done, 1)
                dve.wait_ge(sqrt_done, ln + 1)
                then(dve.reciprocal(rstd[:, ln, :], rstd[:, ln, :]))
                for t in range(NT):
                    ins = dve.tensor_scalar(dst[:, t, :], src[:, t, :], mv[:, ln, t, 0:1], rstd[:, ln, t:t + 1],
                                            ALU.subtract, ALU.mult)
                if ln == 0:
                    then(ins)
                else:
                    ins.then_inc(yn_ready, 1)
                if ln == 0:
                    dve.wait_ge(keyT_done, 1)
                    dve.tensor_copy(keyT[:, :], ps[0:EB, 3, 0:TN]).then_inc(keyT_ready, 1)
            for t in range(NT):
                ins = dve.tensor_copy(xh[:, t, :], xn[:, t, :])
            then(ins)
            for t in range(NT):
                ins = dve.tensor_tensor(xl[:, t, :], xn[:, t, :], xh[:, t, :].bitcast(F32), ALU.subtract)
            ins.then_inc(xl_ready, 1)

            def split_weight(w):
                dve.wait_ge(w_hi, w + 1)
                dve.tensor_tensor(wl[:, w % NSPL, :], wraw[:, w % NRAW, :], wh[:, w % NSPL, :].bitcast(F32),
                                  ALU.subtract).then_inc(w_lo, 1)

            def lo(n, k):
                dve.wait_ge(hi_ready, n + 1)
                dve.tensor_tensor(ml[:, k, :], tmp[:, k % 2, 0:NC], mh[:, k, :].bitcast(F32),
                                  ALU.subtract).then_inc(lo_ready, 1)

            def group(g):
                dve.wait_ge(row_in[g % 2], 16 * (g // 2 + 1))
                if g >= 2:
                    dve.wait_ge(scattered, 16 * GB * (g - 1))
                b0 = GB * g
                if g >= 1:
                    dve.wait_ge(compared, GB * g)
                for b in range(GB):
                    dve.scalar_tensor_tensor(out=eq[:, b, :], in0=keyrow[:, g % 2, :],
                                             scalar=key[:, b0 + b:b0 + b + 1],
                                             in1=band[0:TN, (GB - 1 - b) * TN:(2 * GB - 1 - b) * TN],
                                             op0=ALU.is_equal, op1=ALU.mult,
                                             accum_out=cnt4[:, g % 2, b:b + 1]).then_inc(compared, 1)
                dve.wait_ge(compared, GB * (g + 1))
                then(dve.tensor_scalar(later4[:, :], cnt4[:, g % 2, :], LATER, None, ALU.is_ge))
                then(dve.tensor_tensor(off4[:, :], later4[:, :], to_dump[:, b0:b0 + GB], ALU.mult))
                dve.tensor_tensor(idx4[:, g % 2, :], off4[:, :], key[:, b0:b0 + GB], ALU.add).then_inc(group_ready, 1)

            groups = [0]

            def next_group():
                if groups[0] < NG:
                    group(groups[0])
                    groups[0] += 1

            def job(j):
                dve.wait_ge(pe_done, j + 1)
                return ps[:, slot(j), :], psh[:, slot(j), :, 0:HC]

            dve.wait_ge(vecs_in, 80)
            dve.wait_ge(tmp_zero, 1)
            for k in range(KT):
                whole, _ = job(J_Y + k)
                if k >= 2:
                    dve.wait_ge(lo_ready, L_Y + k - 1)
                dve.tensor_scalar(node_tiles(tmp[:, k % 2, :]),
                                  whole[:, 0:NT * P].rearrange("p (t c) -> p t c", c=P)[:, :, 0:TN],
                                  vecs[:, 0, k:k + 1], vecs[:, 1, k:k + 1], ALU.mult, ALU.add).then_inc(evac, 1)
                if k:
                    lo(L_Y + k - 1, k - 1)
                if k < NSPL:
                    split_weight(k)
            lo(L_Y + KT - 1, KT - 1)

            def elu(n, j, w, src, low, e, dst):
                dve.tensor_scalar(low, src, 0.0, None, ALU.min).then_inc(min_ready, 1)
                split_weight(w + NSPL)
                next_group()
                dve.wait_ge(exp_ready, n + 1)
                dve.scalar_tensor_tensor(out=dst, in0=src, scalar=0.0, in1=e, op0=ALU.max,
                                         op1=ALU.add).then_inc(evac, 1)

            dve.wait_ge(lo_ready, KT)
            for o in range(KT):
                _, cols = job(J_Q + o)
                elu(o, J_Q + o, W_Q + o, cols, halves(tmp[:, o % 2, 0:NC]), halves(tmp2[:, o % 2, 0:NC]),
                    halves(acc[:, o, :]))

            def product(o):
                j = P_JOB[o]
                whole, _ = job(j)
                dve.wait_ge(const_step, 7)
                for dst, c in ((kv_bd, 0), (ks_bd, 512)):
                    for q in (0, 64):
                        ins = dve.tensor_copy(dst[q:q + 64, o, q:q + 64], whole[q:q + 64, c + q:c + q + 64])
                ins.then_inc(evac, 1)
                next_group()

            for o in range(KT):
                whole, _ = job(K_JOB[o])
                c = [x[0:TN, 0:NT * P].rearrange("p (t c) -> p t c", c=P) for x in
                     (whole, tmp[:, o % 2, :], tmp2[:, o % 2, :])]
                elu(KT + o, K_JOB[o], W_KV + 2 * o, c[0], c[1], c[2], kpc[:, o % 2, :, :])
                whole, _ = job(V_JOB[o])
                dve.tensor_copy(vpc[:, o % 2, :, :],
                                whole[0:TN, 0:NT * P].rearrange("p (t c) -> p t c", c=P)).then_inc(evac, 1)
                split_weight(W_KV + 2 * o + 1 + NSPL)
                if o:
                    product(o - 1)
                else:
                    next_group()
            product(KT - 1)

            for h in range(KT):
                _, den = job(J_ATT + 2 * h)
                dve.tensor_scalar(halves(tmp2[:, h % 2, 0:NC]), den, EPS_Z, None, ALU.add).then_inc(evac, 1)
                dve.wait_ge(evac, J_ATT + 2 * h + 1)
                then(dve.reciprocal(tmp2[:, h % 2, 0:NC], tmp2[:, h % 2, 0:NC]))
                _, num = job(J_ATT + 2 * h + 1)
                if h >= 2:
                    dve.wait_ge(lo_ready, L_ATT + h - 1)
                dve.tensor_tensor(halves(tmp[:, h % 2, 0:NC]), num, halves(tmp2[:, h % 2, 0:NC]),
                                  ALU.mult).then_inc(evac, 1)
                if h:
                    lo(L_ATT + h - 1, h - 1)
                next_group()
            lo(L_ATT + KT - 1, KT - 1)
            while groups[0] < NG:
                next_group()

            for o in range(KT):
                _, cols = job(J_PROJ + o)
                dve.tensor_scalar(halves(acc[:, o, :]), cols, vecs[:, 2, o:o + 1], None, ALU.add).then_inc(evac, 1)
                split_weight(W_PROJ + o + NSPL)
            for n in range(2 * KT):
                whole, _ = job(J_XT + n)
                dve.tensor_copy(node_tiles((mh, ml)[n // KT][:, n % KT, :]),
                                whole[:, 0:NT * P].rearrange("p (t c) -> p t c", c=P)[:, :, 0:TN]).then_inc(evac, 1)
            dve.wait_ge(mix_out, 16)
            for o in range(KT):
                _, cols = job(J_ROOT1 + o)
                dve.tensor_scalar(halves(acc[:, o, :]), cols, vecs[:, 3, o:o + 1], None, ALU.add).then_inc(evac, 1)
                split_weight(W_ROOT1 + o + NSPL)

            def relations(layer, base_j, base_w, base_l):
                with dve.Fori(0, R // 2) as i:
                    for u in range(2):
                        j, w, l = base_j + u * RJ, base_w + u * KT, base_l + u * KT
                        n = layer * R + u
                        dve.wait_ge(cnt_done, i * 2 + (n + 1))
                        dve.tensor_scalar(halves(inv[:, :]), psh[:, 3, :, 0:HC], 1.0, None,
                                          ALU.max).then_inc(inv_step, 1)
                        dve.wait_ge(inv_step, i * 2 + (n + 1))
                        dve.reciprocal(inv[:, :], inv[:, :]).then_inc(inv_ready, 1)
                        dve.wait_ge(inv_ready, i * 2 + (n + 1))

                        def mean_lo(k):
                            dve.wait_ge(hi_ready, i * (2 * KT) + (l + k + 1))
                            dve.tensor_tensor(ml[:, k, :], tmp[:, k % 2, 0:NC], mh[:, k, :].bitcast(F32),
                                              ALU.subtract).then_inc(lo_ready, 1)

                        for k in range(KT):
                            dve.wait_ge(pe_done, i * (2 * RJ) + (j + k + 1))
                            if k >= 2:
                                dve.wait_ge(lo_ready, i * (2 * KT) + (l + k - 1))
                            dve.tensor_tensor(halves(tmp[:, k % 2, 0:NC]), psh[:, slot(j + k), :, 0:HC],
                                              halves(inv[:, :]), ALU.mult).then_inc(evac, 1)
                            if k:
                                mean_lo(k - 1)
                        mean_lo(KT - 1)
                        for o in range(KT):
                            dve.wait_ge(pe_done, i * (2 * RJ) + (j + KT + o + 1))
                            dve.tensor_tensor(halves(acc[:, o, :]), psh[:, slot(j + KT + o), :, 0:HC],
                                              halves(acc[:, o, :]), ALU.add).then_inc(evac, 1)
                            nw = w + o + NSPL
                            dve.wait_ge(w_hi, i * (2 * KT) + (nw + 1))
                            dve.tensor_tensor(wl[:, nw % NSPL, :], wraw[:, nw % NRAW, :],
                                              wh[:, nw % NSPL, :].bitcast(F32), ALU.subtract).then_inc(w_lo, 1)

            relations(0, J_REL1, W_REL1, L_REL1)
            dve.wait_ge(evac, J_HN)
            for k in range(KT):
                dve.tensor_scalar(acc[:, k, :], acc[:, k, :], 0.0, None, ALU.max).then_inc(h_ready, 1)
            for k in range(KT):
                dve.wait_ge(hi_ready, L_H + k + 1)
                dve.tensor_tensor(ml[:, k, :], acc[:, k, :], mh[:, k, :].bitcast(F32),
                                  ALU.subtract).then_inc(lo_ready, 1)
            for t in range(NT):
                whole, _ = job(J_HN + t)
                dve.wait_ge(xh_done, t + 1)
                dve.tensor_tensor(xl[:, t, :], whole[0:TN, 0:D], xh[:, t, :].bitcast(F32),
                                  ALU.subtract).then_inc(evac, 1)
            for o in range(KT):
                _, cols = job(J_ROOT2 + o)
                dve.tensor_scalar(halves(acc[:, o, :]), cols, vecs[:, 4, o:o + 1], None, ALU.add).then_inc(evac, 1)
                split_weight(W_ROOT2 + o + NSPL)
            relations(1, J_REL2, W_REL2, L_REL2)
            dve.wait_ge(mix_in, 16)
            dve.wait_ge(evac, J_X2)
            for k in range(KT):
                dve.tensor_tensor(acc[:, k, :], acc[:, k, :], mixb[:, k, :], ALU.add).then_inc(mix_added, 1)
            dve.wait_ge(xraw_in, 16)
            for t in range(NT):
                whole, _ = job(J_X2 + t)
                dve.tensor_tensor(x2[:, t, :], whole[0:TN, 0:D], x2[:, t, :], ALU.add).then_inc(evac, 1)
            dve.memset(fh[:, :, N:NC].bitcast(F32), 0.0).then_inc(pads_zero, 1)
            dve.memset(fl[:, :, N:NC].bitcast(F32), 0.0).then_inc(pads_zero, 1)

            dve.wait_ge(evac, J_F)
            for t in range(NT):
                for h in range(2):
                    ins = dve.bn_stats(stats3[:, t, h, :], x2[:, t, h * HD:(h + 1) * HD])
            then(ins)
            for t in range(NT):
                ins = dve.bn_aggr(mv3[:, t, :], stats3[:, t, :, :])
            ins.then_inc(stats_done, 1)
            dve.wait_ge(sqrt_done, 3)
            then(dve.reciprocal(rstd3[:, :], rstd3[:, :]))
            for t in range(NT):
                ins = dve.tensor_scalar(xf[:, t, :], x2[:, t, :], mv3[:, t, 0:1], rstd3[:, t:t + 1],
                                        ALU.subtract, ALU.mult)
            ins.then_inc(xf_ready, 1)
            for k in range(KT):
                whole, _ = job(J_F + k)
                dve.tensor_copy(node_tiles(acc[:, k, :]),
                                whole[:, 0:NT * P].rearrange("p (t c) -> p t c", c=P)[:, :, 0:TN]).then_inc(evac, 1)
                if k:
                    dve.wait_ge(fh_ready, k)
                    dve.tensor_tensor(fl[:, k - 1, 0:N], acc[:, k - 1, 0:N], fh[:, k - 1, 0:N].bitcast(F32),
                                      ALU.subtract).then_inc(fl_ready, 1)
            dve.wait_ge(fh_ready, KT)
            dve.tensor_tensor(fl[:, KT - 1, 0:N], acc[:, KT - 1, 0:N], fh[:, KT - 1, 0:N].bitcast(F32),
                              ALU.subtract).then_inc(fl_ready, 1)
            dve.wait_ge(sg_hi, 1)
            dve.tensor_tensor(sgl[:, :], sraw[:, :], sgh[:, :].bitcast(F32), ALU.subtract).then_inc(sg_lo, 1)

            dve.wait_ge(ez_ready, 2)
            dve.tensor_scalar(ez[:, :], ez[:, :], 1.0, None, ALU.add).then_inc(misc_evac, 2)
            dve.wait_ge(misc_evac, 2)
            then(dve.reciprocal(score[:, 0, :], ez[:, :]))
            for r in range(ROUNDS):
                v, cur, nxt = top[:, 8 * r:8 * r + 8], score[:, r % 2, 0:N], score[:, 1 - r % 2, 0:N]
                then(dve.max(v, cur))
                ins = dve.max_index(topi[:, 8 * r:8 * r + 8], v, cur)
                if r < ROUNDS - 1:
                    ins = dve.match_replace(nxt, v, cur, -1.0)
                then(ins)
            dve.memset(top[:, CAP:CS], 0.0).then_inc(top_ready, 1)
            dve.tensor_copy(topf[:, :], topi[:, :]).then_inc(top_ready, 1)
            dve.wait_ge(misc_done, 3)
            dve.tensor_copy(slot_idx[:, :], bank[0:CS, mbank(2), NE:2 * NE]).then_inc(idx_ready, 1)
            dve.tensor_copy(slot_tok[:, :], bank[0:CS, mbank(2), NE:2 * NE])
            dve.tensor_copy(slot_score[:, :], bank[0:CS, mbank(2), 0:NE]).then_inc(misc_evac, 1)
            dve.wait_ge(misc_evac, 3)
            dve.wait_ge(sd_hi, 1)
            dve.tensor_tensor(sdl[:, :], draw[:, :], sdh[:, :].bitcast(F32), ALU.subtract).then_inc(sd_lo, 1)
            dve.wait_ge(iota_ready, 1)

            with dve.Fori(0, NE) as e:
                dve.wait_ge(misc_done, e * MJ + M0)
                dve.tensor_scalar(onehot[:, :], iota_n[:, :], slot_tok[:, bass.ds(e, 1)], None,
                                  ALU.is_equal).then_inc(onehot_ready, 1)

                def shared_half(h):
                    dve.wait_ge(silu_ready, e * (NQ + 2) + (h + 1))
                    dve.tensor_tensor(hs[:, h * HC:(h + 1) * HC], sgate[:, h, :], bank[0:SF, 2 * h + 1, 0:HC],
                                      ALU.mult).then_inc(hid_ready, 1)
                    dve.wait_ge(hs_hi, e * 2 + (h + 1))
                    dve.tensor_tensor(hsl[:, h * HC:(h + 1) * HC], hs[:, h * HC:(h + 1) * HC],
                                      hsh[:, h * HC:(h + 1) * HC].bitcast(F32), ALU.subtract).then_inc(hs_lo, 1)

                def misc(m):
                    dve.wait_ge(misc_done, e * MJ + (M0 + m + 1))

                shared_half(0)
                for h in range(2):
                    misc(M_TURN_X + h)
                    dve.tensor_copy(xgT[:, 3 * h:3 * h + 3, :].rearrange("p k c -> p (k c)"),
                                    bank[:, mbank(M_TURN_X + h), 0:3 * CS]).then_inc(misc_evac, 1)
                shared_half(1)
                dve.wait_ge(sg_hi, e + 2)
                dve.tensor_tensor(sgl[:, :], sraw[:, :], sgh[:, :].bitcast(F32), ALU.subtract).then_inc(sg_lo, 1)
                for q in range(NQ):
                    dve.wait_ge(silu_ready, e * (NQ + 2) + (q + 3))
                    dve.tensor_tensor(hid[:, q, :, :].rearrange("p t c -> p (t c)"), gate[:, q % 2, :],
                                      bank[:, q % 4, QT * CS:2 * QT * CS], ALU.mult).then_inc(hid_ready, 1)

                def add_up(m, n):
                    misc(m)
                    t, h = divmod(n, 2)
                    y = x2[:, t, h * HD:(h + 1) * HD]
                    dve.tensor_tensor(y, bank[0:TN, mbank(m), 0:HD], y, ALU.add).then_inc(misc_evac, 1)

                for n in range(8):
                    add_up(M_SH[n], n)
                for h in range(2):
                    misc(M_TURN_O + h)
                    dve.tensor_scalar(oe[:, h * HD:(h + 1) * HD], bank[0:CS, mbank(M_TURN_O + h), 0:HD],
                                      slot_score[:, bass.ds(e, 1)], None, ALU.mult).then_inc(misc_evac, 1)
                for h in range(2):
                    dve.wait_ge(oe_hi, e * 2 + (h + 1))
                    dve.tensor_tensor(oel[:, h * HD:(h + 1) * HD], oe[:, h * HD:(h + 1) * HD],
                                      oeh[:, h * HD:(h + 1) * HD].bitcast(F32), ALU.subtract).then_inc(oe_lo, 1)
                for n in range(8, 10):
                    add_up(M_SH[n], n)
                dve.wait_ge(sd_hi, e + 2)
                dve.tensor_tensor(sdl[:, :], draw[:, :], sdh[:, :].bitcast(F32), ALU.subtract).then_inc(sd_lo, 1)
                for n in range(10):
                    add_up(M_SCATTER + n, n)

        @block.tensor
        def _(pe):
            def mm3(dst, sh, sl, mvh, mvl, first, last):
                pe.matmul(dst, sh, mvh, start=first, stop=False)
                pe.matmul(dst, sh, mvl, start=False, stop=False)
                return pe.matmul(dst, sl, mvh, start=False, stop=last)

            def turned_job(s, w, wait_k=None):
                for k in range(KT):
                    if wait_k:
                        wait_k(k)
                    for h in range(2):
                        c = slice(h * HC, (h + 1) * HC)
                        last = mm3(psh[:, s, h, 0:HC], piece(wh, w)[:, k, :], piece(wl, w)[:, k, :],
                                   mh[:, k, c], ml[:, k, c], k == 0, k == KT - 1)
                return last

            def free(j):
                if j >= 3:
                    pe.wait_ge(evac, j - 2)

            pe.wait_ge(const_ready, 3)
            pe.wait_ge(key_ready, 1)
            pe.transpose(ps[0:EB, 3, 0:TN], key[:, :], ident[0:TN, 0:TN]).then_inc(keyT_done, 1)

            pe.wait_ge(yn_ready, 1)
            for k in range(KT):
                j = J_Y + k
                free(j)
                for t in range(NT):
                    last = pe.transpose(ps[:, slot(j), t * P:t * P + TN], nat[:, t, k * P:(k + 1) * P],
                                        ident[0:TN, 0:TN])
                last.then_inc(pe_done, 1)

            for o in range(KT):
                j, w = J_Q + o, W_Q + o
                free(j)
                pe.wait_ge(w_lo, w + 1)
                turned_job(slot(j), w, (lambda k: pe.wait_ge(lo_ready, L_Y + k + 1)) if o == 0 else None
                           ).then_inc(pe_done, 1)

            def natural_job(j, w):
                free(j)
                pe.wait_ge(w_lo, w + 1)
                for t in range(NT):
                    c = slice(t * TN, (t + 1) * TN)
                    for k in range(KT):
                        last = mm3(ps[0:TN, slot(j), t * P:(t + 1) * P], mh[:, k, c], ml[:, k, c],
                                   piece(wh, w)[:, k, :], piece(wl, w)[:, k, :], k == 0, k == KT - 1)
                last.then_inc(pe_done, 1)

            def product_job(o):
                j = P_JOB[o]
                free(j)
                pe.wait_ge(evac, V_JOB[o] + 1)
                for c, m in ((0, lambda t: vpc[:, o % 2, t, :]), (512, lambda t: ones[0:TN, :])):
                    for t in range(NT):
                        last = pe.matmul(ps[:, slot(j), c:c + P], kpc[:, o % 2, t, :], m(t),
                                         start=(t == 0), stop=(t == NT - 1))
                last.then_inc(pe_done, 1)

            for o in range(KT):
                natural_job(K_JOB[o], W_KV + 2 * o)
                natural_job(V_JOB[o], W_KV + 2 * o + 1)
                if o:
                    product_job(o - 1)
            product_job(KT - 1)

            for h in range(KT):
                for n, bd in enumerate((ks_bd, kv_bd)):
                    j = J_ATT + 2 * h + n
                    free(j)
                    pe.wait_ge(evac, P_JOB[h] + 1)
                    for c in range(2):
                        last = pe.matmul(psh[:, slot(j), c, 0:HC], bd[:, h, :], acc[:, h, c * HC:(c + 1) * HC],
                                         start=True, stop=True)
                    last.then_inc(pe_done, 1)

            for o in range(KT):
                j, w = J_PROJ + o, W_PROJ + o
                free(j)
                pe.wait_ge(w_lo, w + 1)
                turned_job(slot(j), w, (lambda k: pe.wait_ge(lo_ready, L_ATT + k + 1)) if o == 0 else None
                           ).then_inc(pe_done, 1)

            pe.wait_ge(xl_ready, 1)
            for n in range(2 * KT):
                j = J_XT + n
                free(j)
                for t in range(NT):
                    last = pe.transpose(ps[:, slot(j), t * P:t * P + TN],
                                        (xh, xl)[n // KT][:, t, (n % KT) * P:(n % KT + 1) * P].bitcast(F32),
                                        ident[0:TN, 0:TN])
                last.then_inc(pe_done, 1)

            for o in range(KT):
                j, w = J_ROOT1 + o, W_ROOT1 + o
                free(j)
                pe.wait_ge(w_lo, w + 1)
                if o == 0:
                    pe.wait_ge(evac, J_ROOT1)
                turned_job(slot(j), w).then_inc(pe_done, 1)

            def relations(layer, base_j, base_w, base_l):
                with pe.Fori(0, R // 2) as i:
                    for u in range(2):
                        j, w, l = base_j + u * RJ, base_w + u * KT, base_l + u * KT
                        counts = cbuf[:, u, :].rearrange("p (t n) -> p t n", t=NT)
                        pe.wait_ge(c_in[u], i * 16 + (layer * R // 2 + 1) * 16)
                        if layer or u:
                            pe.wait_ge(inv_step, i * 2 + (layer * R + u))
                        else:
                            pe.wait_ge(inv_step, i * 2)
                        for t in range(NT):
                            for h in range(2):
                                last = pe.matmul(psh[:, 3, h, 0:HC], onesr[0:TN, :],
                                                 counts[:, t, h * HC:(h + 1) * HC], start=(t == 0),
                                                 stop=(t == NT - 1))
                        last.then_inc(cnt_done, 1)
                        for k in range(KT):
                            pe.wait_ge(evac, i * (2 * RJ) + (j + k - 2))
                            for t in range(NT):
                                for h in range(2):
                                    c = counts[:, t, h * HC:(h + 1) * HC]
                                    for x in (xh, xl):
                                        last = pe.matmul(psh[:, slot(j + k), h, 0:HC], x[:, t, k * P:(k + 1) * P], c,
                                                         start=(t == 0 and x is xh),
                                                         stop=(t == NT - 1 and x is xl))
                            last.then_inc(pe_done, 1)
                        for o in range(KT):
                            pe.wait_ge(evac, i * (2 * RJ) + (j + KT + o - 2))
                            pe.wait_ge(w_lo, i * (2 * KT) + (w + o + 1))
                            turned_job(slot(j + KT + o), w + o,
                                       (lambda k: pe.wait_ge(lo_ready, i * (2 * KT) + (l + k + 1))) if o == 0
                                       else None).then_inc(pe_done, 1)

            relations(0, J_REL1, W_REL1, L_REL1)

            def natural_turns(base_j):
                for t in range(NT):
                    j = base_j + t
                    free(j)
                    for k in range(KT):
                        last = pe.transpose(ps[0:TN, slot(j), k * P:(k + 1) * P], acc[:, k, t * TN:(t + 1) * TN],
                                            ident[:, :])
                    last.then_inc(pe_done, 1)

            pe.wait_ge(h_ready, KT)
            natural_turns(J_HN)
            for o in range(KT):
                j, w = J_ROOT2 + o, W_ROOT2 + o
                free(j)
                pe.wait_ge(w_lo, w + 1)
                turned_job(slot(j), w, (lambda k: pe.wait_ge(lo_ready, L_H + k + 1)) if o == 0 else None
                           ).then_inc(pe_done, 1)
            relations(1, J_REL2, W_REL2, L_REL2)
            pe.wait_ge(mix_added, KT)
            natural_turns(J_X2)

            pe.wait_ge(xf_ready, 1)
            for k in range(KT):
                j = J_F + k
                free(j)
                for t in range(NT):
                    last = pe.transpose(ps[:, slot(j), t * P:t * P + TN], xf[:, t, k * P:(k + 1) * P],
                                        ident[0:TN, 0:TN])
                last.then_inc(pe_done, 1)
            pe.wait_ge(gw_in, 16)
            pe.wait_ge(evac, J_END)
            for h in range(2):
                for k in range(KT):
                    last = pe.matmul(bank[0:NE, mbank(h), 0:HC], gw[:, k, :], acc[:, k, h * HC:(h + 1) * HC],
                                     start=(k == 0), stop=(k == KT - 1))
                last.then_inc(misc_done, 1)
            pe.wait_ge(top_ready, 2)
            pe.transpose(bank[0:CS, mbank(2), 0:NE], top[:, :], ident[0:NE, 0:NE])
            pe.transpose(bank[0:CS, mbank(2), NE:2 * NE], topf[:, :], ident[0:NE, 0:NE]).then_inc(misc_done, 1)
            pe.wait_ge(fl_ready, KT)
            pe.wait_ge(pads_zero, 2)

            with pe.Fori(0, NE) as e:
                def misc_free(m):
                    pe.wait_ge(misc_evac, e * MJ + (M0 + m - 2))

                def shared_half(h):
                    for b, o in ((2 * h, 0), (2 * h + 1, 1)):
                        for k in range(KT):
                            c = slice((o * KT + k) * SF, (o * KT + k + 1) * SF)
                            last = mm3(bank[0:SF, b, 0:HC], sgh[:, c], sgl[:, c],
                                       fh[:, k, h * HC:(h + 1) * HC], fl[:, k, h * HC:(h + 1) * HC],
                                       k == 0, k == KT - 1)
                    last.then_inc(shared_done, 1)

                pe.wait_ge(sg_lo, e + 1)
                shared_half(0)
                pe.wait_ge(gathered, e * 16 + 16)
                for h in range(2):
                    misc_free(M_TURN_X + h)
                    for k in range(3):
                        last = pe.transpose(bank[:, mbank(M_TURN_X + h), k * CS:(k + 1) * CS],
                                            xg[:, (3 * h + k) * P:(3 * h + k + 1) * P], ident[0:CS, 0:CS])
                    last.then_inc(misc_done, 1)
                shared_half(1)

                def landed(c):
                    pe.wait_ge(ring_in[c % NRING], e * (16 * EC // NRING) + 16 * (c // NRING + 1))

                def gate_up(q):
                    pe.wait_ge(hid_ready, e * (NQ + 2) + (q // 2 + 1 if q < 4 else q - 1))
                    for o, m in enumerate("gu"):
                        c = chunk[m, q]
                        landed(c)
                        w = ring_slot(c).rearrange("p (k f) -> p k f", k=KT)
                        for t in range(QT):
                            for k in range(KT):
                                last = pe.matmul(bank[:, q % 4, (o * QT + t) * CS:(o * QT + t + 1) * CS],
                                                 w[:, k, t * P:(t + 1) * P], xgT[:, k, :],
                                                 start=(k == 0), stop=(k == KT - 1))
                        last.then_inc(used, 1)

                def down(q):
                    pe.wait_ge(hid_ready, e * (NQ + 2) + (q + 3))
                    c = chunk["d", q]
                    landed(c)
                    w = ring_slot(c).rearrange("p (t d) -> p t d", t=QT)
                    for t in range(QT):
                        for k in range(KT):
                            last = pe.matmul(bank[:, 4, k * CS:(k + 1) * CS], w[:, t, k * P:(k + 1) * P],
                                             hid[:, q, t, :], start=(q == 0 and t == 0 and k == 0),
                                             stop=(q == NQ - 1 and t == QT - 1), skip_group_check=True)
                    last.then_inc(used, 1)

                def shared_down(n):
                    m, (t, h) = M_SH[n], divmod(n, 2)
                    misc_free(m)
                    c, d = slice(t * TN, (t + 1) * TN), slice(h * HD, (h + 1) * HD)
                    mm3(bank[0:TN, mbank(m), 0:HD], hsh[:, c], hsl[:, c], sdh[:, d], sdl[:, d],
                        True, True).then_inc(misc_done, 1)

                pe.wait_ge(misc_evac, e * MJ + (M0 + M_TURN_X + 2))
                gate_up(0)
                pe.wait_ge(down_copied, e)
                for q in range(1, NQ):
                    gate_up(q)
                    down(q - 1)
                pe.wait_ge(hs_lo, e * 2 + 2)
                pe.wait_ge(sd_lo, e + 1)
                for n in range(6):
                    shared_down(n)
                down(NQ - 1)
                for n in range(6, 8):
                    shared_down(n)
                pe.wait_ge(down_copied, e + 1)
                for h in range(2):
                    misc_free(M_TURN_O + h)
                    for k in range(3):
                        last = pe.transpose(bank[0:CS, mbank(M_TURN_O + h), k * P:(k + 1) * P],
                                            outT[:, 3 * h + k, :], ident[:, :])
                    last.then_inc(misc_done, 1)
                for n in range(8, 10):
                    shared_down(n)
                pe.wait_ge(onehot_ready, e + 1)
                pe.wait_ge(oe_lo, e * 2 + 2)
                for n in range(10):
                    m, (t, h) = M_SCATTER + n, divmod(n, 2)
                    misc_free(m)
                    for s, x in enumerate((oeh, oel)):
                        last = pe.matmul(bank[0:TN, mbank(m), 0:HD], onehot[:, t * TN:(t + 1) * TN],
                                         x[:, h * HD:(h + 1) * HD], start=(s == 0), stop=(s == 1))
                    last.then_inc(misc_done, 1)


def _pieces(w):
    i, o = w.shape
    return np.ascontiguousarray(w.reshape(i // P, P, o // P, P).transpose(2, 1, 0, 3)).reshape(o // P, P, i)


def _up_chunks(w):
    return w.reshape(NE, NQ, QT * P, KT, P).transpose(0, 1, 4, 3, 2).reshape(NE * NQ, P, CHUNK)


def _shared_up(w):
    return w.reshape(NE, SF, KT, P).transpose(0, 3, 2, 1).reshape(NE, P, KT * SF)


def _turned_vec(v):
    return np.ascontiguousarray(v.reshape(KT, P).T)


def kernel(**kw):
    import concourse.bacc as _bacc
    from concourse.bass_utils import run_bass_kernel_spmd as _run

    kw = {k: np.asarray(v) for k, v in kw.items()}
    arrays = {
        "x": kw["x"], "src": kw["src"], "dst": kw["dst"], "type": kw["edge_type_8"],
        "gamma": _turned_vec(kw["L0_mix_ln_gamma"]), "beta": _turned_vec(kw["L0_mix_ln_beta"]),
        "b_proj": _turned_vec(kw["L0_mix_b_proj"]),
        "b1": _turned_vec(kw["L0_gnn_b1"]), "b2": _turned_vec(kw["L0_gnn_b2"]),
        "wqkv": _pieces(kw["L0_mix_w_qkv"].T), "wproj": _pieces(kw["L0_mix_w_proj"].T),
        "root1": _pieces(kw["L0_gnn_root1"]), "root2": _pieces(kw["L0_gnn_root2"]),
        "W1": np.concatenate([_pieces(w) for w in kw["L0_gnn_W1"]]),
        "W2": np.concatenate([_pieces(w) for w in kw["L0_gnn_W2"]]),
        "gate_weight": kw["L0_ffn_gate_weight"].T.reshape(KT, P, NE).transpose(1, 0, 2),
        "Wg": _up_chunks(kw["L0_ffn_Wg"]), "Wu": _up_chunks(kw["L0_ffn_Wu"]),
        "Wd": kw["L0_ffn_Wd"].reshape(NE, D, NQ, QT, P).transpose(0, 2, 4, 3, 1).reshape(NE * NQ, P, CHUNK),
        "Ws_gu": np.stack([_shared_up(kw["L0_ffn_Ws_g"]), _shared_up(kw["L0_ffn_Ws_u"])], 2).reshape(NE, P, -1),
        "Ws_d": kw["L0_ffn_Ws_d"].T.reshape(NE, SF, D),
    }
    nc = _bacc.Bacc("TRN2", target_bir_lowering=False, num_devices=1)
    arrays = {"in_" + k: np.ascontiguousarray(v) for k, v in arrays.items()}
    a = {k[3:]: nc.dram_tensor(k, v.shape, mybir.dt.from_np(v.dtype), kind="ExternalInput").ap()
         for k, v in arrays.items()}
    out = nc.dram_tensor("out", (N, D), F32, kind="ExternalOutput").ap()
    build(nc, a, out)
    r = _run(nc, [arrays], core_ids=[0])
    return r.results[0]["out"]
```

```python
from contextlib import ExitStack

import numpy as np
import concourse.bass as bass
from concourse import mybir

F32 = mybir.dt.float32
F32R = mybir.dt.float32r
I32 = mybir.dt.int32
U32 = mybir.dt.uint32
BF16 = mybir.dt.bfloat16
ALU = mybir.AluOpType
ACT = mybir.ActivationFunctionType
AX = mybir.AxisListType

P = 128
N = 625
D = 768
R = 8
E = 10000
NT, TN = 5, 125
KT = D // P
NC, HC = 628, 314
HD = D // 2
NE, CAP = 16, 79
CS = 80
FE, FS = 3072, 1536
EB = E // TN
GB = 4
NG = EB // GB
ROWS = R * NC
TABLE = 128 * 24544
DUMP = N * ROWS
ZC = TABLE // P // 8
LATER = 2048.0
PIECE = KT * P
NRAW, NSPL = 6, 3
NQ, QT = 8, 3
CHUNK = QT * D
HALF = CHUNK // 2
NRING, NR1 = 6, 4
NPC = 4
EC = 3 * NQ
SF = FS // NE
ROUNDS = CS // 8
MJ = 2 + NQ + 2 * NT
EPS_LN = 1e-5
EPS_Z = 1e-6


def build(nc, a, out):
    outer = ExitStack()
    with outer:
        def sb(name, shape, dt=F32, stack=outer):
            return stack.enter_context(nc.sbuf_tensor(name, shape, dt))

        def sem(name):
            return outer.enter_context(nc.semaphore(name))

        table = nc.dram_tensor("edge_table", (TABLE, 1), F32).ap()
        keys_dram = nc.dram_tensor("edge_keys", (EB, TN), F32).ap()
        mix_dram = nc.dram_tensor("mix_spill", (P, KT * NC), F32).ap()
        xf_dram = nc.dram_tensor("ffn_input", (N, D), F32).ap()

        ps = outer.enter_context(nc.psum_tensor("ps", [P, 4, 1024], F32))
        psh = ps.rearrange("p k (h c) -> p k h c", h=2)

        ident = sb("ident", [P, P])
        ones = sb("ones", [P, P])
        onesr = sb("onesr", [P, P], F32R)
        eps_ln = sb("eps_ln", [P, 1])
        vecs = sb("vecs", [P, 5, KT])
        ring = sb("ring", [P, NR1, CHUNK])

        phase_a = ExitStack()
        sa = lambda name, shape, dt=F32: sb(name, shape, dt, phase_a)
        xh = sa("xh", [TN, NT, D], F32R)
        xl = sa("xl", [TN, NT, D], F32R)
        band = sa("band", [P, (2 * GB - 1) * TN])
        ecol = sa("ecol", [TN, 3, EB], I32)
        ef = sa("ef", [TN, 3, EB])
        key = sa("key", [TN, EB])
        to_dump = sa("to_dump", [TN, EB])
        dump_cell = sa("dump_cell", [P, 1])
        keyT = sa("keyT", [EB, TN])
        keyrow = sa("keyrow", [TN, 2, GB * TN])
        eq = sa("eq", [TN, GB, GB * TN], BF16)
        cnt4 = sa("cnt4", [TN, 2, GB])
        later4 = sa("later4", [TN, GB])
        off4 = sa("off4", [TN, GB])
        idx4 = sa("idx4", [TN, 2, GB], I32)
        stats = sa("stats", [TN, 2, NT, 2, 6])
        mv = sa("mv", [TN, 2, NT, 2])
        rstd = sa("rstd", [TN, 2, NT])
        wraw = sa("wraw", [P, NRAW, PIECE])
        wh = sa("wh", [P, NSPL, PIECE], F32R)
        wl = sa("wl", [P, NSPL, PIECE], F32R)
        tmp = sa("tmp", [P, 2, 640])
        tmp2 = sa("tmp2", [P, 2, 640])
        inv = sa("inv", [P, NC])
        acc = sa("acc", [P, KT, NC])
        kv_bd = sa("kv_bd", [P, KT, P])
        ks_bd = sa("ks_bd", [P, KT, P])
        early = ExitStack()
        nat = sb("nat", [TN, NT, D], F32, early)
        kpc = sb("kpc", [TN, 2, NT, P], F32, early)
        vpc = sb("vpc", [TN, 2, NT, P], F32, early)
        early.close()
        cbuf = sa("cbuf", [TN, 2, NT * NC], F32R)
        sa("behind_cbuf", [TN, 160])
        early = ExitStack()
        xn = sb("xn", [TN, NT, D], F32, early)
        early.close()
        mh = sa("mh", [P, KT, NC], F32R)
        ml = sa("ml", [P, KT, NC], F32R)
        phase_a.close()
        phase_b = outer.enter_context(ExitStack())
        sbb = lambda name, shape, dt=F32: sb(name, shape, dt, phase_b)
        x2 = sbb("x2", [TN, NT, D])
        early = ExitStack()
        mixb = sb("mixb", [P, KT, NC], F32, early)
        early.close()
        early = ExitStack()
        xf = sb("xf", [TN, NT, D], F32, early)
        early.close()
        ring2 = sbb("ring2", [P, NRING - NR1, CHUNK])
        early = ExitStack()
        xft = sb("xft", [P, KT, NC], F32, early)
        early.close()
        hid_h = sbb("hid_h", [P, NQ, QT, CS], F32R)
        hid_l = sbb("hid_l", [P, NQ, QT, CS], F32R)
        eh = sbb("eh", [P, NPC, HALF], F32R)
        el = sbb("el", [P, NPC, HALF], F32R)
        fh = sbb("fh", [P, KT, NC], F32R)
        fl = sbb("fl", [P, KT, NC], F32R)
        sraw = sbb("sraw", [P, 2 * KT * SF])
        sgh = sbb("sgh", [P, 2 * KT * SF], F32R)
        sgl = sbb("sgl", [P, 2 * KT * SF], F32R)
        draw = sbb("draw", [SF, D])
        sdh = sbb("sdh", [SF, D], F32R)
        sdl = sbb("sdl", [SF, D], F32R)
        hs = sbb("hs", [SF, NC])
        hsh = sbb("hsh", [SF, NC], F32R)
        hsl = sbb("hsl", [SF, NC], F32R)
        early = ExitStack()
        ez = sb("ez", [NE, NC], F32, early)
        score = sb("score", [NE, 2, NC], F32, early)
        early.close()
        hid = sbb("hid", [CS, 2, QT * P])
        xg = sbb("xg", [CS, D])
        oe = sbb("oe", [CS, D])
        oeh = sbb("oeh", [CS, D], F32R)
        oel = sbb("oel", [CS, D], F32R)
        xg_h = sbb("xg_h", [P, KT, CS], F32R)
        xg_l = sbb("xg_l", [P, KT, CS], F32R)
        onehot = sbb("onehot", [CS, NC], F32R)
        iota_n = sbb("iota_n", [CS, NC])
        gw = sbb("gw", [P, KT, NE])
        top = sbb("top", [NE, CS])
        topi = sbb("topi", [NE, CS], U32)
        topf = sbb("topf", [NE, CS])
        slot_score = sbb("slot_score", [CS, NE])
        slot_tok = sbb("slot_tok", [CS, NE])
        slot_idx = sbb("slot_idx", [CS, NE], I32)
        stats3 = sbb("stats3", [TN, NT, 2, 6])
        mv3 = sbb("mv3", [TN, NT, 2])
        rstd3 = sbb("rstd3", [TN, NT])

        x_in = sem("x_in"); edges_in = sem("edges_in"); vecs_in = sem("vecs_in")
        const_step = sem("const_step"); const_ready = sem("const_ready")
        zeros_ready = sem("zeros_ready"); table_zero = sem("table_zero")
        dve_step = sem("dve_step"); sqrt_done = sem("sqrt_done"); tmp_zero = sem("tmp_zero"); stats_done = sem("stats_done")
        yn_ready = sem("yn_ready"); key_ready = sem("key_ready"); keyT_done = sem("keyT_done")
        keyT_ready = sem("keyT_ready"); keys_stored = sem("keys_stored")
        row_in = [sem("row_in0"), sem("row_in1")]
        compared = sem("compared"); group_ready = sem("group_ready"); scattered = sem("scattered")
        raw_in = [sem(f"raw_in{i}") for i in range(NRAW)]
        w_hi = sem("w_hi"); w_lo = sem("w_lo")
        c_in = [sem("c_in0"), sem("c_in1")]
        pe_done = sem("pe_done"); evac = sem("evac")
        hi_ready = sem("hi_ready"); lo_ready = sem("lo_ready")
        xh_done = sem("xh_done"); xl_ready = sem("xl_ready")
        min_ready = sem("min_ready"); exp_ready = sem("exp_ready"); recip_step = sem("recip_step")
        cnt_done = sem("cnt_done"); inv_step = sem("inv_step"); inv_ready = sem("inv_ready")
        h_ready = sem("h_ready"); mix_out = sem("mix_out"); mix_in = sem("mix_in")
        xraw_in = sem("xraw_in"); mix_added = sem("mix_added"); out_done = sem("out_done")

        used = sem("used")
        half_hi = sem("half_hi"); half_lo = sem("half_lo"); turn_hi = sem("turn_hi"); oe_ready = sem("oe_ready")
        ring_in = [sem(f"ring_in{n}") for n in range(NRING)]
        xf_ready = sem("xf_ready"); xf_stored = sem("xf_stored"); gw_in = sem("gw_in")
        fh_ready = sem("fh_ready"); fl_ready = sem("fl_ready"); pads_zero = sem("pads_zero")
        ez_ready = sem("ez_ready"); top_ready = sem("top_ready"); idx_ready = sem("idx_ready")
        iota_ready = sem("iota_ready"); gathered = sem("gathered")
        sg_in = sem("sg_in"); sd_in = sem("sd_in")
        sg_hi = sem("sg_hi"); sg_lo = sem("sg_lo"); sd_hi = sem("sd_hi"); sd_lo = sem("sd_lo")
        shared_done = sem("shared_done"); silu_ready = sem("silu_ready"); hid_ready = sem("hid_ready")
        hs_hi = sem("hs_hi"); hs_lo = sem("hs_lo"); onehot_ready = sem("onehot_ready")
        down_copied = sem("down_copied"); oe_hi = sem("oe_hi"); oe_lo = sem("oe_lo")
        misc_done = sem("misc_done"); misc_evac = sem("misc_evac")

        J_Y = 0
        J_Q = J_Y + KT
        J_KV = J_Q + KT
        K_JOB = [J_KV] + [J_KV + 2 + 3 * (o - 1) for o in range(1, KT)]
        V_JOB = [j + 1 for j in K_JOB]
        P_JOB = [J_KV + 4 + 3 * o for o in range(KT - 1)] + [J_KV + 3 * KT - 1]
        J_ATT = J_KV + 3 * KT
        J_PROJ = J_ATT + 2 * KT
        J_XT = J_PROJ + KT
        J_ROOT1 = J_XT + 2 * KT
        J_REL1 = J_ROOT1 + KT
        RJ = 2 * KT
        J_HN = J_REL1 + R * RJ
        J_ROOT2 = J_HN + NT
        J_REL2 = J_ROOT2 + KT
        J_X2 = J_REL2 + R * RJ
        J_F = J_X2 + NT
        J_END = J_F + KT
        W_Q, W_KV = 0, KT
        W_PROJ = W_KV + 2 * KT
        W_ROOT1 = W_PROJ + KT
        W_REL1 = W_ROOT1 + KT
        W_ROOT2 = W_REL1 + R * KT
        W_REL2 = W_ROOT2 + KT
        W_END = W_REL2 + R * KT
        L_Y, L_ATT = 0, KT
        L_REL1 = 2 * KT
        L_H = L_REL1 + R * KT
        L_REL2 = L_H + KT

        def slot(j):
            return j % 3

        def piece(t, w):
            return t[:, w % NSPL, :].rearrange("p (k m) -> p k m", k=KT)

        def w_src(w):
            if w < W_KV:
                return a["wqkv"][w]
            if w < W_PROJ:
                o, v = divmod(w - W_KV, 2)
                return a["wqkv"][KT * (1 + v) + o]
            if w < W_ROOT1:
                return a["wproj"][w - W_PROJ]
            if w < W_REL1:
                return a["root1"][w - W_ROOT1]
            if w < W_REL2:
                return a["root2"][w - W_ROOT2]
            return a["wproj"][w - W_END]

        def halves(t):
            return t.rearrange("p (h c) -> p h c", h=2)

        def node_tiles(t):
            return t[:, 0:N].rearrange("p (t c) -> p t c", t=NT)

        bank = ps.rearrange("p k (h c) -> p (k h) c", h=2)
        M0 = 6
        M_HIDDEN = 0
        M_TOKENS = NQ
        M_Y = M_TOKENS + 2
        HJ = NQ + 2

        def mbank(m):
            return 6 + m % 2

        order = [("g", 0), ("u", 0), ("g", 1), ("u", 1), ("turn", 0)]
        for q in range(2, NQ):
            order += [("g", q), ("u", q), ("turn", q - 1), ("d", q - 2)]
        order += [("turn", NQ - 1), ("d", NQ - 2), ("d", NQ - 1)]
        chunks = [x for x in order if x[0] != "turn"]
        chunk = {x: c for c, x in enumerate(chunks)}

        def ring_slot(c):
            c %= NRING
            return ring[:, c, :] if c < NR1 else ring2[:, c - NR1, :]

        block = outer.enter_context(nc.Block())

        @block.sync
        def _(sp):
            sp.dma_start(nat[:, :, :], a["x"].rearrange("(t p) d -> p t d", p=TN)).then_inc(x_in, 16)
            for n, e in enumerate(("type", "dst", "src")):
                sp.dma_start(ecol[:, n, :], a[e].rearrange("(p b) -> p b", b=EB)).then_inc(edges_in, 16)
            for n, v in enumerate(("gamma", "beta", "b_proj", "b1", "b2")):
                sp.dma_start(vecs[:, n, :], a[v]).then_inc(vecs_in, 16)

            def load_piece(w):
                if w >= NRAW:
                    sp.wait_ge(w_lo, w - NRAW + 1)
                sp.dma_start(wraw[:, w % NRAW, :], w_src(w)).then_inc(raw_in[w % NRAW], 16)

            def load_row(g):
                if g >= 2:
                    sp.wait_ge(group_ready, g - 1)
                src = keys_dram[g * GB:(g + 1) * GB, :].rearrange("b c -> (b c)").unsqueeze(0)
                sp.dma_start(keyrow[:, g % 2, :], src.broadcast_to([TN, GB * TN])).then_inc(row_in[g % 2], 16)

            for w in range(NRAW):
                load_piece(w)
            def first_chunk(c):
                m, q = chunks[c]
                sp.dma_start(ring_slot(c), a["W" + m][q]).then_inc(ring_in[c % NRING], 16)

            sp.wait_ge(keyT_ready, 1)
            sp.dma_start(keys_dram, keyT[:, :]).then_inc(keys_stored, 16)
            sp.wait_ge(keys_stored, 16)
            load_row(0)
            load_row(1)
            for w in range(NRAW, W_REL1):
                g = w - NRAW + 2
                if g < NG:
                    load_row(g)
                load_piece(w)
            sp.wait_ge(table_zero, 8 * 16)
            for c in range(NR1):
                first_chunk(c)
            sp.wait_ge(evac, J_PROJ + KT)
            sp.dma_start(mix_dram, acc[:, :, :].rearrange("p k n -> p (k n)")).then_inc(mix_out, 16)

            def relations(wt, base_j, base_w):
                with sp.Fori(0, R // 2) as i:
                    for u in range(2):
                        sp.wait_ge(pe_done, i * (2 * RJ) + (base_j + (u - 2) * RJ + KT))
                        src = table[0:DUMP, :].rearrange("(t p r n) o -> p r t (n o)", t=NT, p=TN, r=R)
                        sp.dma_start(cbuf[:, u, :].bitcast(F32).rearrange("p (t n) -> p t n", t=NT),
                                     src[:, bass.ds(i * 2 + u, 1), :, :].rearrange("p r t n -> p (r t) n")
                                     ).then_inc(c_in[u], 16)
                        for o in range(KT):
                            sp.wait_ge(w_lo, i * (2 * KT) + (base_w + u * KT + o - NRAW + 1))
                            sp.dma_start(wraw[:, o, :], wt[bass.ds(i * (2 * KT) + (u * KT + o), 1)].rearrange(
                                "a p f -> (a p) f")).then_inc(raw_in[o], 16)

            sp.wait_ge(scattered, 16 * EB)
            relations(a["W1"], J_REL1, W_REL1)
            for w in range(W_ROOT2, W_REL2):
                load_piece(w)
            relations(a["W2"], J_REL2, W_REL2)
            for w in range(W_END, W_END + NSPL):
                load_piece(w)
            sp.wait_ge(pe_done, J_X2 - KT)
            sp.wait_ge(mix_out, 16)
            sp.dma_start(mixb[:, :, :].rearrange("p k n -> p (k n)"), mix_dram).then_inc(mix_in, 16)
            sp.dma_start(x2[:, :, :], a["x"].rearrange("(t p) d -> p t d", p=TN)).then_inc(xraw_in, 16)
            sp.wait_ge(pe_done, J_X2)
            sp.wait_ge(w_lo, W_END + NSPL)
            sp.dma_start(gw[:, :, :], a["gate_weight"]).then_inc(gw_in, 16)

            def load_shared(e):
                sp.dma_start(sraw[:, :], a["Ws_gu"][bass.ds(e, 1)].rearrange("a p f -> (a p) f")
                             ).then_inc(sg_in, 16)

            def load_shared_down(e):
                sp.dma_start(draw[:, :], a["Ws_d"][bass.ds(e, 1)].rearrange("a p f -> (a p) f")
                             ).then_inc(sd_in, 16)

            load_shared(0)
            load_shared_down(0)
            sp.wait_ge(xf_ready, 1)
            sp.dma_start(xf_dram.rearrange("(t p) d -> p t d", p=TN), xf[:, :, :]).then_inc(xf_stored, 16)
            sp.wait_ge(xf_stored, 16)
            sp.wait_ge(pe_done, J_END)
            for c in range(NR1, NRING):
                first_chunk(c)
            sp.wait_ge(sg_lo, 1)
            load_shared(1)
            for c in range(NRING, EC):
                sp.wait_ge(half_lo, 2 * (c - NRING + 1))
                first_chunk(c)
                if c == NRING + 8:
                    sp.wait_ge(sg_lo, 2)
                    load_shared(2)
                    sp.wait_ge(sd_lo, 1)
                    load_shared_down(1)
            with sp.Fori(1, NE) as e:
                for c, (m, q) in enumerate(chunks):
                    sp.wait_ge(half_lo, e * (2 * EC) + 2 * (c - NRING + 1))
                    sp.dma_start(ring_slot(c), a["W" + m][bass.ds(e * NQ + q, 1)].rearrange("a p f -> (a p) f")
                                 ).then_inc(ring_in[c % NRING], 16)
                    if c == NRING + 8:
                        sp.wait_ge(sg_lo, e + 2)
                        load_shared((e + 2) % NE)
                        sp.wait_ge(sd_lo, e + 1)
                        load_shared_down((e + 1) % NE)
            for c in range(NPC // 2):
                sp.wait_ge(half_lo, 2 * (NE * EC + c - NRING + 1))
                first_chunk(c)
            sp.wait_ge(sg_in, 16 * (NE + 2))
            sp.wait_ge(sd_in, 16 * (NE + 1))
            sp.wait_ge(misc_evac, M0 + MJ * NE)
            sp.dma_start(out.rearrange("(t p) d -> p t d", p=TN), x2[:, :, :]).then_inc(out_done, 16)
            sp.wait_ge(out_done, 16)

        @block.gpsimd
        def _(pool):
            zeros = ring[:, :, :].rearrange("p s c -> p (s c)")[:, 0:ZC]
            pool.memset(zeros, 0.0).then_inc(zeros_ready, 1)
            pool.memset(ident[:, :], 0.0).then_inc(const_step, 1)
            pool.memset(band[:, :], 1.0).then_inc(const_step, 1)
            pool.memset(ones[:, :], 1.0).then_inc(const_step, 1)
            pool.memset(onesr[:, :].bitcast(F32), 1.0).then_inc(const_step, 1)
            pool.memset(eps_ln[:, :], EPS_LN).then_inc(const_step, 1)
            pool.memset(kv_bd[:, :, :], 0.0).then_inc(const_step, 1)
            pool.memset(ks_bd[:, :, :], 0.0).then_inc(const_step, 1)
            pool.wait_ge(const_step, 7)
            pool.affine_select(out=ident[:, :], in_=ident[:, :], compare_op=ALU.not_equal, fill=1.0, base=0,
                               pattern=[[-1, P]], channel_multiplier=1).then_inc(const_ready, 1)
            pool.affine_select(out=band[:, :], in_=band[:, :], compare_op=ALU.is_ge, fill=LATER,
                               base=(GB - 1) * TN, pattern=[[-1, (2 * GB - 1) * TN]],
                               channel_multiplier=1).then_inc(const_ready, 1)
            pool.iota(dump_cell[:, :], pattern=[[0, 1]], base=DUMP, channel_multiplier=1,
                      allow_small_or_imprecise_dtypes=True).then_inc(const_ready, 1)
            pool.wait_ge(table_zero, 8 * 16)
            for g in range(NG):
                pool.wait_ge(group_ready, g + 1)
                if g >= 1:
                    pool.wait_ge(scattered, 16 * GB * g)
                for b in range(GB):
                    pool.indirect_dma_start(
                        out=table, out_offset=bass.IndirectOffsetOnAxis(ap=idx4[:, g % 2, b:b + 1], axis=0),
                        in_=cnt4[:, g % 2, b:b + 1], in_offset=None, compute_op=ALU.add
                    ).then_inc(scattered, 16)
            pool.wait_ge(pe_done, J_X2)
            pool.wait_ge(lo_ready, L_REL2 + R * KT)
            pool.wait_ge(w_lo, W_END + NSPL)
            pool.iota(iota_n[:, :], pattern=[[1, NC]], base=0, channel_multiplier=0,
                      allow_small_or_imprecise_dtypes=True).then_inc(iota_ready, 1)
            pool.wait_ge(idx_ready, 1)
            pool.wait_ge(xf_stored, 16)
            for n in range(NE + 1):
                e = min(n, NE - 1)
                if n:
                    pool.wait_ge(misc_done, M0 if n == 1 else M0 + MJ * (n - 2) + M_TOKENS + 2)
                pool.indirect_dma_start(
                    out=xg[:, :], out_offset=None, in_=xf_dram,
                    in_offset=bass.IndirectOffsetOnAxis(ap=slot_idx[:, e:e + 1], axis=0)
                ).then_inc(gathered, 16)

        @block.scalar
        def _(act):
            act.wait_ge(zeros_ready, 1)
            zeros = ring[:, :, :].rearrange("p s c -> p (s c)")[:, 0:ZC]
            for z in range(8):
                act.dma_start(table.rearrange("(z p c) o -> z p (c o)", z=8, p=P)[z], zeros).then_inc(table_zero, 16)

            def split_weight(w):
                act.wait_ge(raw_in[w % NRAW], 16 * (w // NRAW + 1))
                act.copy(wh[:, w % NSPL, :], wraw[:, w % NRAW, :]).then_inc(w_hi, 1)

            for ln in range(2):
                act.wait_ge(const_ready, 3)
                act.wait_ge(stats_done, ln + 1)
                act.activation(rstd[:, ln, :], mv[:, ln, :, 1], ACT.Sqrt, bias=eps_ln[0:TN, :]).then_inc(sqrt_done, 1)

            for w in range(NSPL):
                split_weight(w)

            def hi(value, k, job):
                act.wait_ge(evac, job)
                act.copy(mh[:, k, :], tmp[:, k % 2, 0:NC]).then_inc(hi_ready, 1)

            def next_weight(j, w):
                act.wait_ge(pe_done, j + 1)
                split_weight(w + NSPL)

            def exponent(n):
                act.wait_ge(min_ready, n + 1)
                act.activation(tmp2[:, n % 2, :], tmp[:, n % 2, :], ACT.Exp).then_inc(exp_ready, 1)

            for k in range(KT):
                hi(L_Y + k, k, J_Y + k + 1)
            for o in range(KT):
                next_weight(J_Q + o, W_Q + o)
                exponent(o)
            for o in range(KT):
                next_weight(K_JOB[o], W_KV + 2 * o)
                exponent(KT + o)
                next_weight(V_JOB[o], W_KV + 2 * o + 1)
            for h in range(KT):
                hi(L_ATT + h, h, J_ATT + 2 * h + 2)
            for o in range(KT):
                next_weight(J_PROJ + o, W_PROJ + o)
            for o in range(KT):
                next_weight(J_ROOT1 + o, W_ROOT1 + o)

            def relations(base_j, base_w):
                with act.Fori(0, R // 2) as i:
                    for u in range(2):
                        j, w = base_j + u * RJ, base_w + u * KT
                        for k in range(KT):
                            act.wait_ge(evac, i * (2 * RJ) + (j + k + 1))
                            act.copy(mh[:, k, :], tmp[:, k % 2, 0:NC]).then_inc(hi_ready, 1)
                        for o in range(KT):
                            act.wait_ge(pe_done, i * (2 * RJ) + (j + KT + o + 1))
                            nw = w + o + NSPL
                            act.wait_ge(raw_in[nw % NRAW], i * 32 + 16 * (nw // NRAW + 1))
                            act.copy(wh[:, nw % NSPL, :], wraw[:, nw % NRAW, :]).then_inc(w_hi, 1)

            relations(J_REL1, W_REL1)
            for k in range(KT):
                act.wait_ge(h_ready, k + 1)
                act.copy(mh[:, k, :], acc[:, k, :]).then_inc(hi_ready, 1)
            for t in range(NT):
                act.wait_ge(pe_done, J_HN + t + 1)
                act.copy(xh[:, t, :], ps[0:TN, slot(J_HN + t), 0:D]).then_inc(xh_done, 1)
            for o in range(KT):
                next_weight(J_ROOT2 + o, W_ROOT2 + o)
            relations(J_REL2, W_REL2)

            act.wait_ge(stats_done, 3)
            act.activation(rstd3[:, :], mv3[:, :, 1], ACT.Sqrt, bias=eps_ln[0:TN, :]).then_inc(sqrt_done, 1)
            act.wait_ge(pads_zero, 3)
            for k in range(KT):
                act.wait_ge(evac, J_F + k + 1)
                act.copy(fh[:, k, 0:N], xft[:, k, 0:N]).then_inc(fh_ready, 1)
            for h in range(2):
                act.wait_ge(misc_done, h + 1)
                act.activation(ez[:, h * HC:(h + 1) * HC], bank[0:NE, mbank(h), 0:HC], ACT.Exp,
                               scale=-1.0).then_inc(ez_ready, 1)
            act.wait_ge(sg_in, 16)
            act.copy(sgh[:, :], sraw[:, :]).then_inc(sg_hi, 1)

            def half_of_chunk(n):
                return ring_slot(n // 2)[:, (n % 2) * HALF:(n % 2 + 1) * HALF]

            for n in range(NPC):
                act.wait_ge(ring_in[n // 2], 16)
                act.copy(eh[:, n, :], half_of_chunk(n)).then_inc(half_hi, 1)

            def turned(count, dst, m):
                act.wait_ge(misc_done, count)
                act.copy(dst, bank[:, mbank(m), 0:QT * CS]).then_inc(turn_hi, 1)

            def tokens_hi(h, count):
                turned(count, xg_h[:, 3 * h:3 * h + 3, :].rearrange("p k c -> p (k c)"), M_TOKENS + h)

            def shared_silu(h, count):
                act.wait_ge(shared_done, count)
                act.activation(hs[:, h * HC:(h + 1) * HC], bank[0:SF, 2 * h, 0:HC], ACT.Silu
                               ).then_inc(silu_ready, 1)

            for h in range(2):
                shared_silu(h, h + 1)
            for h in range(2):
                tokens_hi(h, M0 - 2 + h + 1)

            with act.Fori(0, NE) as e:
                act.wait_ge(misc_done, e * MJ + M0)
                for h in range(2):
                    act.wait_ge(hid_ready, e * HJ + (h + 1))
                    act.copy(hsh[:, h * HC:(h + 1) * HC], hs[:, h * HC:(h + 1) * HC]).then_inc(hs_hi, 1)
                for m, q in order:
                    if m == "turn":
                        turned(e * MJ + (M0 + M_HIDDEN + q + 1),
                               hid_h[:, q, :, :].rearrange("p t c -> p (t c)"), M_HIDDEN + q)
                        if q == 0:
                            act.wait_ge(sd_in, e * 16 + 16)
                            act.copy(sdh[:, :], draw[:, :]).then_inc(sd_hi, 1)
                        if q == 1:
                            act.wait_ge(sg_in, e * 16 + 32)
                            act.copy(sgh[:, :], sraw[:, :]).then_inc(sg_hi, 1)
                        continue
                    for n in (2 * chunk[m, q], 2 * chunk[m, q] + 1):
                        act.wait_ge(used, e * (2 * EC) + (n + 1))
                        c = (n + NPC) // 2
                        act.wait_ge(ring_in[c % NRING], e * (16 * EC // NRING) + 16 * (c // NRING + 1))
                        act.copy(eh[:, n % NPC, :], half_of_chunk(n + NPC)).then_inc(half_hi, 1)
                    if m == "u":
                        act.activation(hid[:, q % 2, :], bank[0:CS, 2 * q % 4, 0:QT * P], ACT.Silu
                                       ).then_inc(silu_ready, 1)
                for h in range(2):
                    act.wait_ge(oe_ready, e * 2 + (h + 1))
                    act.copy(oeh[:, h * HD:(h + 1) * HD], oe[:, h * HD:(h + 1) * HD]).then_inc(oe_hi, 1)
                shared_silu(0, e * 2 + 3)
                for h in range(2):
                    tokens_hi(h, e * MJ + (M0 + M_TOKENS + h + 1))
                shared_silu(1, e * 2 + 4)

        @block.vector
        def _(dve):
            steps = [0]

            def then(ins):
                steps[0] += 1
                ins.then_inc(dve_step, 1)
                dve.wait_ge(dve_step, steps[0])

            dve.memset(tmp[:, :, :], 0.0).then_inc(tmp_zero, 1)
            dve.wait_ge(edges_in, 48)
            then(dve.tensor_copy(ef[:, :, :], ecol[:, :, :]))
            then(dve.scalar_tensor_tensor(out=key[:, :], in0=ef[:, 0, :], scalar=float(NC), in1=ef[:, 1, :],
                                          op0=ALU.mult, op1=ALU.add))
            dve.scalar_tensor_tensor(out=key[:, :], in0=ef[:, 2, :], scalar=float(ROWS), in1=key[:, :],
                                     op0=ALU.mult, op1=ALU.add).then_inc(key_ready, 1)
            dve.wait_ge(const_ready, 3)
            dve.wait_ge(key_ready, 1)
            then(dve.tensor_scalar(to_dump[:, :], key[:, :], -1.0, dump_cell[0:TN, 0:1], ALU.mult, ALU.add))

            dve.wait_ge(x_in, 16)
            for ln, (src, dst) in enumerate(((nat, xn), (xn, nat))):
                for t in range(NT):
                    for h in range(2):
                        ins = dve.bn_stats(stats[:, ln, t, h, :], src[:, t, h * HD:(h + 1) * HD])
                then(ins)
                for t in range(NT):
                    ins = dve.bn_aggr(mv[:, ln, t, :], stats[:, ln, t, :, :])
                ins.then_inc(stats_done, 1)
                dve.wait_ge(sqrt_done, ln + 1)
                then(dve.reciprocal(rstd[:, ln, :], rstd[:, ln, :]))
                for t in range(NT):
                    ins = dve.tensor_scalar(dst[:, t, :], src[:, t, :], mv[:, ln, t, 0:1], rstd[:, ln, t:t + 1],
                                            ALU.subtract, ALU.mult)
                if ln == 0:
                    then(ins)
                else:
                    ins.then_inc(yn_ready, 1)
                if ln == 0:
                    dve.wait_ge(keyT_done, 1)
                    dve.tensor_copy(keyT[:, :], ps[0:EB, 3, 0:TN]).then_inc(keyT_ready, 1)
            for t in range(NT):
                ins = dve.tensor_copy(xh[:, t, :], xn[:, t, :])
            then(ins)
            for t in range(NT):
                ins = dve.tensor_tensor(xl[:, t, :], xn[:, t, :], xh[:, t, :].bitcast(F32), ALU.subtract)
            ins.then_inc(xl_ready, 1)

            def split_weight(w):
                dve.wait_ge(w_hi, w + 1)
                dve.tensor_tensor(wl[:, w % NSPL, :], wraw[:, w % NRAW, :], wh[:, w % NSPL, :].bitcast(F32),
                                  ALU.subtract).then_inc(w_lo, 1)

            def lo(n, k):
                dve.wait_ge(hi_ready, n + 1)
                dve.tensor_tensor(ml[:, k, :], tmp[:, k % 2, 0:NC], mh[:, k, :].bitcast(F32),
                                  ALU.subtract).then_inc(lo_ready, 1)

            def group(g):
                dve.wait_ge(row_in[g % 2], 16 * (g // 2 + 1))
                if g >= 2:
                    dve.wait_ge(scattered, 16 * GB * (g - 1))
                b0 = GB * g
                if g >= 1:
                    dve.wait_ge(compared, GB * g)
                for b in range(GB):
                    dve.scalar_tensor_tensor(out=eq[:, b, :], in0=keyrow[:, g % 2, :],
                                             scalar=key[:, b0 + b:b0 + b + 1],
                                             in1=band[0:TN, (GB - 1 - b) * TN:(2 * GB - 1 - b) * TN],
                                             op0=ALU.is_equal, op1=ALU.mult,
                                             accum_out=cnt4[:, g % 2, b:b + 1]).then_inc(compared, 1)
                dve.wait_ge(compared, GB * (g + 1))
                then(dve.tensor_scalar(later4[:, :], cnt4[:, g % 2, :], LATER, None, ALU.is_ge))
                then(dve.tensor_tensor(off4[:, :], later4[:, :], to_dump[:, b0:b0 + GB], ALU.mult))
                dve.tensor_tensor(idx4[:, g % 2, :], off4[:, :], key[:, b0:b0 + GB], ALU.add).then_inc(group_ready, 1)

            groups = [0]

            def next_group():
                if groups[0] < NG:
                    group(groups[0])
                    groups[0] += 1

            def job(j):
                dve.wait_ge(pe_done, j + 1)
                return ps[:, slot(j), :], psh[:, slot(j), :, 0:HC]

            dve.wait_ge(vecs_in, 80)
            dve.wait_ge(tmp_zero, 1)
            for k in range(KT):
                whole, _ = job(J_Y + k)
                if k >= 2:
                    dve.wait_ge(lo_ready, L_Y + k - 1)
                dve.tensor_scalar(node_tiles(tmp[:, k % 2, :]),
                                  whole[:, 0:NT * P].rearrange("p (t c) -> p t c", c=P)[:, :, 0:TN],
                                  vecs[:, 0, k:k + 1], vecs[:, 1, k:k + 1], ALU.mult, ALU.add).then_inc(evac, 1)
                if k:
                    lo(L_Y + k - 1, k - 1)
                if k < NSPL:
                    split_weight(k)
            lo(L_Y + KT - 1, KT - 1)

            def elu(n, j, w, src, low, e, dst):
                dve.tensor_scalar(low, src, 0.0, None, ALU.min).then_inc(min_ready, 1)
                split_weight(w + NSPL)
                next_group()
                dve.wait_ge(exp_ready, n + 1)
                dve.scalar_tensor_tensor(out=dst, in0=src, scalar=0.0, in1=e, op0=ALU.max,
                                         op1=ALU.add).then_inc(evac, 1)

            dve.wait_ge(lo_ready, KT)
            for o in range(KT):
                _, cols = job(J_Q + o)
                elu(o, J_Q + o, W_Q + o, cols, halves(tmp[:, o % 2, 0:NC]), halves(tmp2[:, o % 2, 0:NC]),
                    halves(acc[:, o, :]))

            def product(o):
                j = P_JOB[o]
                whole, _ = job(j)
                dve.wait_ge(const_step, 7)
                for dst, c in ((kv_bd, 0), (ks_bd, 512)):
                    for q in (0, 64):
                        ins = dve.tensor_copy(dst[q:q + 64, o, q:q + 64], whole[q:q + 64, c + q:c + q + 64])
                ins.then_inc(evac, 1)
                next_group()

            for o in range(KT):
                whole, _ = job(K_JOB[o])
                c = [x[0:TN, 0:NT * P].rearrange("p (t c) -> p t c", c=P) for x in
                     (whole, tmp[:, o % 2, :], tmp2[:, o % 2, :])]
                elu(KT + o, K_JOB[o], W_KV + 2 * o, c[0], c[1], c[2], kpc[:, o % 2, :, :])
                whole, _ = job(V_JOB[o])
                dve.tensor_copy(vpc[:, o % 2, :, :],
                                whole[0:TN, 0:NT * P].rearrange("p (t c) -> p t c", c=P)).then_inc(evac, 1)
                split_weight(W_KV + 2 * o + 1 + NSPL)
                if o:
                    product(o - 1)
                else:
                    next_group()
            product(KT - 1)

            for h in range(KT):
                _, den = job(J_ATT + 2 * h)
                dve.tensor_scalar(halves(tmp2[:, h % 2, 0:NC]), den, EPS_Z, None, ALU.add).then_inc(evac, 1)
                dve.wait_ge(evac, J_ATT + 2 * h + 1)
                then(dve.reciprocal(tmp2[:, h % 2, 0:NC], tmp2[:, h % 2, 0:NC]))
                _, num = job(J_ATT + 2 * h + 1)
                if h >= 2:
                    dve.wait_ge(lo_ready, L_ATT + h - 1)
                dve.tensor_tensor(halves(tmp[:, h % 2, 0:NC]), num, halves(tmp2[:, h % 2, 0:NC]),
                                  ALU.mult).then_inc(evac, 1)
                if h:
                    lo(L_ATT + h - 1, h - 1)
                next_group()
            lo(L_ATT + KT - 1, KT - 1)
            while groups[0] < NG:
                next_group()

            for o in range(KT):
                _, cols = job(J_PROJ + o)
                dve.tensor_scalar(halves(acc[:, o, :]), cols, vecs[:, 2, o:o + 1], None, ALU.add).then_inc(evac, 1)
                split_weight(W_PROJ + o + NSPL)
            for n in range(2 * KT):
                whole, _ = job(J_XT + n)
                dve.tensor_copy(node_tiles((mh, ml)[n // KT][:, n % KT, :]),
                                whole[:, 0:NT * P].rearrange("p (t c) -> p t c", c=P)[:, :, 0:TN]).then_inc(evac, 1)
            dve.wait_ge(mix_out, 16)
            for o in range(KT):
                _, cols = job(J_ROOT1 + o)
                dve.tensor_scalar(halves(acc[:, o, :]), cols, vecs[:, 3, o:o + 1], None, ALU.add).then_inc(evac, 1)
                split_weight(W_ROOT1 + o + NSPL)

            def relations(layer, base_j, base_w, base_l):
                with dve.Fori(0, R // 2) as i:
                    for u in range(2):
                        j, w, l = base_j + u * RJ, base_w + u * KT, base_l + u * KT
                        n = layer * R + u
                        dve.wait_ge(cnt_done, i * 2 + (n + 1))
                        dve.tensor_scalar(halves(inv[:, :]), psh[:, 3, :, 0:HC], 1.0, None,
                                          ALU.max).then_inc(inv_step, 1)
                        dve.wait_ge(inv_step, i * 2 + (n + 1))
                        dve.reciprocal(inv[:, :], inv[:, :]).then_inc(inv_ready, 1)
                        dve.wait_ge(inv_ready, i * 2 + (n + 1))

                        def mean_lo(k):
                            dve.wait_ge(hi_ready, i * (2 * KT) + (l + k + 1))
                            dve.tensor_tensor(ml[:, k, :], tmp[:, k % 2, 0:NC], mh[:, k, :].bitcast(F32),
                                              ALU.subtract).then_inc(lo_ready, 1)

                        for k in range(KT):
                            dve.wait_ge(pe_done, i * (2 * RJ) + (j + k + 1))
                            if k >= 2:
                                dve.wait_ge(lo_ready, i * (2 * KT) + (l + k - 1))
                            dve.tensor_tensor(halves(tmp[:, k % 2, 0:NC]), psh[:, slot(j + k), :, 0:HC],
                                              halves(inv[:, :]), ALU.mult).then_inc(evac, 1)
                            if k:
                                mean_lo(k - 1)
                        mean_lo(KT - 1)
                        for o in range(KT):
                            dve.wait_ge(pe_done, i * (2 * RJ) + (j + KT + o + 1))
                            dve.tensor_tensor(halves(acc[:, o, :]), psh[:, slot(j + KT + o), :, 0:HC],
                                              halves(acc[:, o, :]), ALU.add).then_inc(evac, 1)
                            nw = w + o + NSPL
                            dve.wait_ge(w_hi, i * (2 * KT) + (nw + 1))
                            dve.tensor_tensor(wl[:, nw % NSPL, :], wraw[:, nw % NRAW, :],
                                              wh[:, nw % NSPL, :].bitcast(F32), ALU.subtract).then_inc(w_lo, 1)

            relations(0, J_REL1, W_REL1, L_REL1)
            dve.wait_ge(evac, J_HN)
            for k in range(KT):
                dve.tensor_scalar(acc[:, k, :], acc[:, k, :], 0.0, None, ALU.max).then_inc(h_ready, 1)
            for k in range(KT):
                dve.wait_ge(hi_ready, L_H + k + 1)
                dve.tensor_tensor(ml[:, k, :], acc[:, k, :], mh[:, k, :].bitcast(F32),
                                  ALU.subtract).then_inc(lo_ready, 1)
            for t in range(NT):
                whole, _ = job(J_HN + t)
                dve.wait_ge(xh_done, t + 1)
                dve.tensor_tensor(xl[:, t, :], whole[0:TN, 0:D], xh[:, t, :].bitcast(F32),
                                  ALU.subtract).then_inc(evac, 1)
            for o in range(KT):
                _, cols = job(J_ROOT2 + o)
                dve.tensor_scalar(halves(acc[:, o, :]), cols, vecs[:, 4, o:o + 1], None, ALU.add).then_inc(evac, 1)
                split_weight(W_ROOT2 + o + NSPL)
            relations(1, J_REL2, W_REL2, L_REL2)
            dve.wait_ge(mix_in, 16)
            dve.wait_ge(evac, J_X2)
            for k in range(KT):
                dve.tensor_tensor(acc[:, k, :], acc[:, k, :], mixb[:, k, :], ALU.add).then_inc(mix_added, 1)
            dve.wait_ge(xraw_in, 16)
            for t in range(NT):
                whole, _ = job(J_X2 + t)
                dve.tensor_tensor(x2[:, t, :], whole[0:TN, 0:D], x2[:, t, :], ALU.add).then_inc(evac, 1)
            dve.memset(fh[:, :, N:NC].bitcast(F32), 0.0).then_inc(pads_zero, 1)
            dve.memset(fl[:, :, N:NC].bitcast(F32), 0.0).then_inc(pads_zero, 1)
            dve.memset(xft[:, :, N:NC], 0.0).then_inc(pads_zero, 1)

            dve.wait_ge(evac, J_F)
            for t in range(NT):
                for h in range(2):
                    ins = dve.bn_stats(stats3[:, t, h, :], x2[:, t, h * HD:(h + 1) * HD])
            then(ins)
            for t in range(NT):
                ins = dve.bn_aggr(mv3[:, t, :], stats3[:, t, :, :])
            ins.then_inc(stats_done, 1)
            dve.wait_ge(sqrt_done, 3)
            then(dve.reciprocal(rstd3[:, :], rstd3[:, :]))
            for t in range(NT):
                ins = dve.tensor_scalar(xf[:, t, :], x2[:, t, :], mv3[:, t, 0:1], rstd3[:, t:t + 1],
                                        ALU.subtract, ALU.mult)
            ins.then_inc(xf_ready, 1)
            for k in range(KT):
                whole, _ = job(J_F + k)
                dve.tensor_copy(node_tiles(xft[:, k, :]),
                                whole[:, 0:NT * P].rearrange("p (t c) -> p t c", c=P)[:, :, 0:TN]).then_inc(evac, 1)
                if k:
                    dve.wait_ge(fh_ready, k)
                    dve.tensor_tensor(fl[:, k - 1, 0:N], xft[:, k - 1, 0:N], fh[:, k - 1, 0:N].bitcast(F32),
                                      ALU.subtract).then_inc(fl_ready, 1)
            dve.wait_ge(fh_ready, KT)
            dve.tensor_tensor(fl[:, KT - 1, 0:N], xft[:, KT - 1, 0:N], fh[:, KT - 1, 0:N].bitcast(F32),
                              ALU.subtract).then_inc(fl_ready, 1)
            dve.wait_ge(sg_hi, 1)
            dve.tensor_tensor(sgl[:, :], sraw[:, :], sgh[:, :].bitcast(F32), ALU.subtract).then_inc(sg_lo, 1)

            dve.wait_ge(ez_ready, 2)
            dve.tensor_scalar(ez[:, :], ez[:, :], 1.0, None, ALU.add).then_inc(misc_evac, 2)
            dve.wait_ge(misc_evac, 2)
            then(dve.reciprocal(score[:, 0, :], ez[:, :]))
            for r in range(ROUNDS):
                v, cur, nxt = top[:, 8 * r:8 * r + 8], score[:, r % 2, 0:N], score[:, 1 - r % 2, 0:N]
                then(dve.max(v, cur))
                ins = dve.max_index(topi[:, 8 * r:8 * r + 8], v, cur)
                if r < ROUNDS - 1:
                    ins = dve.match_replace(nxt, v, cur, -1.0)
                then(ins)
            dve.memset(top[:, CAP:CS], 0.0).then_inc(top_ready, 1)
            dve.tensor_copy(topf[:, :], topi[:, :]).then_inc(top_ready, 1)
            dve.wait_ge(misc_done, 3)
            dve.tensor_copy(slot_score[:, :], bank[0:CS, mbank(2), 0:NE]).then_inc(misc_evac, 1)
            dve.wait_ge(misc_done, 4)
            dve.tensor_copy(slot_idx[:, :], bank[0:CS, mbank(3), 0:NE]).then_inc(idx_ready, 1)
            dve.tensor_copy(slot_tok[:, :], bank[0:CS, mbank(3), 0:NE]).then_inc(misc_evac, 1)
            dve.wait_ge(misc_evac, 4)
            dve.wait_ge(iota_ready, 1)

            def half_of_chunk(n):
                return ring_slot(n // 2)[:, (n % 2) * HALF:(n % 2 + 1) * HALF]

            for n in range(NPC):
                dve.wait_ge(half_hi, n + 1)
                dve.tensor_tensor(el[:, n, :], half_of_chunk(n), eh[:, n, :].bitcast(F32),
                                  ALU.subtract).then_inc(half_lo, 1)

            def turned(count, dst, hi, m):
                dve.wait_ge(turn_hi, count)
                dve.tensor_tensor(dst, bank[:, mbank(m), 0:QT * CS], hi.bitcast(F32),
                                  ALU.subtract).then_inc(misc_evac, 1)

            def tokens_lo(h, count):
                x = [t[:, 3 * h:3 * h + 3, :].rearrange("p k c -> p (k c)") for t in (xg_l, xg_h)]
                turned(count, x[0], x[1], M_TOKENS + h)

            def shared_hidden(h, count):
                x = hs[:, h * HC:(h + 1) * HC]
                dve.wait_ge(silu_ready, count)
                dve.tensor_tensor(x, x, bank[0:SF, 2 * h + 1, 0:HC], ALU.mult).then_inc(hid_ready, 1)

            for h in range(2):
                shared_hidden(h, h + 1)
            for h in range(2):
                tokens_lo(h, h + 1)

            with dve.Fori(0, NE) as e:
                dve.wait_ge(misc_done, e * MJ + M0)
                dve.tensor_scalar(onehot[:, :], iota_n[:, :], slot_tok[:, bass.ds(e, 1)], None,
                                  ALU.is_equal).then_inc(onehot_ready, 1)
                for h in range(2):
                    dve.wait_ge(hs_hi, e * 2 + (h + 1))
                    dve.tensor_tensor(hsl[:, h * HC:(h + 1) * HC], hs[:, h * HC:(h + 1) * HC],
                                      hsh[:, h * HC:(h + 1) * HC].bitcast(F32), ALU.subtract).then_inc(hs_lo, 1)
                for m, q in order:
                    if m == "turn":
                        x = [t[:, q, :, :].rearrange("p t c -> p (t c)") for t in (hid_l, hid_h)]
                        turned(e * (2 + NQ) + (q + 3), x[0], x[1], M_HIDDEN + q)
                        if q == 0:
                            dve.wait_ge(sd_hi, e + 1)
                            dve.tensor_tensor(sdl[:, :], draw[:, :], sdh[:, :].bitcast(F32),
                                              ALU.subtract).then_inc(sd_lo, 1)
                        if q == 1:
                            dve.wait_ge(sg_hi, e + 2)
                            dve.tensor_tensor(sgl[:, :], sraw[:, :], sgh[:, :].bitcast(F32),
                                              ALU.subtract).then_inc(sg_lo, 1)
                        continue
                    for n in (2 * chunk[m, q], 2 * chunk[m, q] + 1):
                        dve.wait_ge(half_hi, e * (2 * EC) + (n + NPC + 1))
                        dve.tensor_tensor(el[:, n % NPC, :], half_of_chunk(n + NPC),
                                          eh[:, n % NPC, :].bitcast(F32), ALU.subtract).then_inc(half_lo, 1)
                        if m == "d" and q == NQ - 1:
                            h = n % 2
                            dve.tensor_scalar(oe[:, h * HD:(h + 1) * HD], bank[0:CS, 4 + h, 0:HD],
                                              slot_score[:, bass.ds(e, 1)], None, ALU.mult).then_inc(oe_ready, 1)
                    if m == "u":
                        dve.wait_ge(silu_ready, e * HJ + (q + 3))
                        dve.tensor_tensor(hid[:, q % 2, :], hid[:, q % 2, :], bank[0:CS, (2 * q + 1) % 4, 0:QT * P],
                                          ALU.mult).then_inc(hid_ready, 1)
                for h in range(2):
                    dve.wait_ge(oe_hi, e * 2 + (h + 1))
                    dve.tensor_tensor(oel[:, h * HD:(h + 1) * HD], oe[:, h * HD:(h + 1) * HD],
                                      oeh[:, h * HD:(h + 1) * HD].bitcast(F32), ALU.subtract).then_inc(oe_lo, 1)
                shared_hidden(0, e * HJ + (HJ + 1))
                for h in range(2):
                    tokens_lo(h, e * (2 + NQ) + (NQ + 2 + h + 1))
                shared_hidden(1, e * HJ + (HJ + 2))
                for n in range(2 * NT):
                    h, t = divmod(n, NT)
                    y = x2[:, t, h * HD:(h + 1) * HD]
                    dve.wait_ge(misc_done, e * MJ + (M0 + M_Y + n + 1))
                    dve.tensor_tensor(y, bank[0:TN, mbank(M_Y + n), 0:HD], y, ALU.add).then_inc(misc_evac, 1)

        @block.tensor
        def _(pe):
            def mm3(dst, sh, sl, mvh, mvl, first, last):
                pe.matmul(dst, sh, mvh, start=first, stop=False)
                pe.matmul(dst, sh, mvl, start=False, stop=False)
                return pe.matmul(dst, sl, mvh, start=False, stop=last)

            def turned_job(s, w, wait_k=None):
                for k in range(KT):
                    if wait_k:
                        wait_k(k)
                    for h in range(2):
                        c = slice(h * HC, (h + 1) * HC)
                        last = mm3(psh[:, s, h, 0:HC], piece(wh, w)[:, k, :], piece(wl, w)[:, k, :],
                                   mh[:, k, c], ml[:, k, c], k == 0, k == KT - 1)
                return last

            def free(j):
                if j >= 3:
                    pe.wait_ge(evac, j - 2)

            pe.wait_ge(const_ready, 3)
            pe.wait_ge(key_ready, 1)
            pe.transpose(ps[0:EB, 3, 0:TN], key[:, :], ident[0:TN, 0:TN]).then_inc(keyT_done, 1)

            pe.wait_ge(yn_ready, 1)
            for k in range(KT):
                j = J_Y + k
                free(j)
                for t in range(NT):
                    last = pe.transpose(ps[:, slot(j), t * P:t * P + TN], nat[:, t, k * P:(k + 1) * P],
                                        ident[0:TN, 0:TN])
                last.then_inc(pe_done, 1)

            for o in range(KT):
                j, w = J_Q + o, W_Q + o
                free(j)
                pe.wait_ge(w_lo, w + 1)
                turned_job(slot(j), w, (lambda k: pe.wait_ge(lo_ready, L_Y + k + 1)) if o == 0 else None
                           ).then_inc(pe_done, 1)

            def natural_job(j, w):
                free(j)
                pe.wait_ge(w_lo, w + 1)
                for t in range(NT):
                    c = slice(t * TN, (t + 1) * TN)
                    for k in range(KT):
                        last = mm3(ps[0:TN, slot(j), t * P:(t + 1) * P], mh[:, k, c], ml[:, k, c],
                                   piece(wh, w)[:, k, :], piece(wl, w)[:, k, :], k == 0, k == KT - 1)
                last.then_inc(pe_done, 1)

            def product_job(o):
                j = P_JOB[o]
                free(j)
                pe.wait_ge(evac, V_JOB[o] + 1)
                for c, m in ((0, lambda t: vpc[:, o % 2, t, :]), (512, lambda t: ones[0:TN, :])):
                    for t in range(NT):
                        last = pe.matmul(ps[:, slot(j), c:c + P], kpc[:, o % 2, t, :], m(t),
                                         start=(t == 0), stop=(t == NT - 1))
                last.then_inc(pe_done, 1)

            for o in range(KT):
                natural_job(K_JOB[o], W_KV + 2 * o)
                natural_job(V_JOB[o], W_KV + 2 * o + 1)
                if o:
                    product_job(o - 1)
            product_job(KT - 1)

            for h in range(KT):
                for n, bd in enumerate((ks_bd, kv_bd)):
                    j = J_ATT + 2 * h + n
                    free(j)
                    pe.wait_ge(evac, P_JOB[h] + 1)
                    for c in range(2):
                        last = pe.matmul(psh[:, slot(j), c, 0:HC], bd[:, h, :], acc[:, h, c * HC:(c + 1) * HC],
                                         start=True, stop=True)
                    last.then_inc(pe_done, 1)

            for o in range(KT):
                j, w = J_PROJ + o, W_PROJ + o
                free(j)
                pe.wait_ge(w_lo, w + 1)
                turned_job(slot(j), w, (lambda k: pe.wait_ge(lo_ready, L_ATT + k + 1)) if o == 0 else None
                           ).then_inc(pe_done, 1)

            pe.wait_ge(xl_ready, 1)
            for n in range(2 * KT):
                j = J_XT + n
                free(j)
                for t in range(NT):
                    last = pe.transpose(ps[:, slot(j), t * P:t * P + TN],
                                        (xh, xl)[n // KT][:, t, (n % KT) * P:(n % KT + 1) * P].bitcast(F32),
                                        ident[0:TN, 0:TN])
                last.then_inc(pe_done, 1)

            for o in range(KT):
                j, w = J_ROOT1 + o, W_ROOT1 + o
                free(j)
                pe.wait_ge(w_lo, w + 1)
                if o == 0:
                    pe.wait_ge(evac, J_ROOT1)
                turned_job(slot(j), w).then_inc(pe_done, 1)

            def relations(layer, base_j, base_w, base_l):
                with pe.Fori(0, R // 2) as i:
                    for u in range(2):
                        j, w, l = base_j + u * RJ, base_w + u * KT, base_l + u * KT
                        counts = cbuf[:, u, :].rearrange("p (t n) -> p t n", t=NT)
                        pe.wait_ge(c_in[u], i * 16 + (layer * R // 2 + 1) * 16)
                        if layer or u:
                            pe.wait_ge(inv_step, i * 2 + (layer * R + u))
                        else:
                            pe.wait_ge(inv_step, i * 2)
                        for t in range(NT):
                            for h in range(2):
                                last = pe.matmul(psh[:, 3, h, 0:HC], onesr[0:TN, :],
                                                 counts[:, t, h * HC:(h + 1) * HC], start=(t == 0),
                                                 stop=(t == NT - 1))
                        last.then_inc(cnt_done, 1)
                        for k in range(KT):
                            pe.wait_ge(evac, i * (2 * RJ) + (j + k - 2))
                            for t in range(NT):
                                for h in range(2):
                                    c = counts[:, t, h * HC:(h + 1) * HC]
                                    for x in (xh, xl):
                                        last = pe.matmul(psh[:, slot(j + k), h, 0:HC], x[:, t, k * P:(k + 1) * P], c,
                                                         start=(t == 0 and x is xh),
                                                         stop=(t == NT - 1 and x is xl))
                            last.then_inc(pe_done, 1)
                        for o in range(KT):
                            pe.wait_ge(evac, i * (2 * RJ) + (j + KT + o - 2))
                            pe.wait_ge(w_lo, i * (2 * KT) + (w + o + 1))
                            turned_job(slot(j + KT + o), w + o,
                                       (lambda k: pe.wait_ge(lo_ready, i * (2 * KT) + (l + k + 1))) if o == 0
                                       else None).then_inc(pe_done, 1)

            relations(0, J_REL1, W_REL1, L_REL1)

            def natural_turns(base_j):
                for t in range(NT):
                    j = base_j + t
                    free(j)
                    for k in range(KT):
                        last = pe.transpose(ps[0:TN, slot(j), k * P:(k + 1) * P], acc[:, k, t * TN:(t + 1) * TN],
                                            ident[:, :])
                    last.then_inc(pe_done, 1)

            pe.wait_ge(h_ready, KT)
            natural_turns(J_HN)
            for o in range(KT):
                j, w = J_ROOT2 + o, W_ROOT2 + o
                free(j)
                pe.wait_ge(w_lo, w + 1)
                turned_job(slot(j), w, (lambda k: pe.wait_ge(lo_ready, L_H + k + 1)) if o == 0 else None
                           ).then_inc(pe_done, 1)
            relations(1, J_REL2, W_REL2, L_REL2)
            pe.wait_ge(mix_added, KT)
            natural_turns(J_X2)

            pe.wait_ge(xf_ready, 1)
            for k in range(KT):
                j = J_F + k
                free(j)
                for t in range(NT):
                    last = pe.transpose(ps[:, slot(j), t * P:t * P + TN], xf[:, t, k * P:(k + 1) * P],
                                        ident[0:TN, 0:TN])
                last.then_inc(pe_done, 1)
            pe.wait_ge(gw_in, 16)
            pe.wait_ge(evac, J_END)
            for h in range(2):
                for k in range(KT):
                    last = pe.matmul(bank[0:NE, mbank(h), 0:HC], gw[:, k, :], xft[:, k, h * HC:(h + 1) * HC],
                                     start=(k == 0), stop=(k == KT - 1))
                last.then_inc(misc_done, 1)

            def shared_half(h):
                for b, o in ((2 * h, 0), (2 * h + 1, 1)):
                    for k in range(KT):
                        c = slice((o * KT + k) * SF, (o * KT + k + 1) * SF)
                        last = mm3(bank[0:SF, b, 0:HC], sgh[:, c], sgl[:, c],
                                   fh[:, k, h * HC:(h + 1) * HC], fl[:, k, h * HC:(h + 1) * HC],
                                   k == 0, k == KT - 1)
                last.then_inc(shared_done, 1)

            def tokens_turned(landed):
                pe.wait_ge(gathered, landed)
                for h in range(2):
                    for k in range(3):
                        last = pe.transpose(bank[:, mbank(M_TOKENS + h), k * CS:(k + 1) * CS],
                                            xg[:, (3 * h + k) * P:(3 * h + k + 1) * P], ident[0:CS, 0:CS])
                    last.then_inc(misc_done, 1)

            pe.wait_ge(fl_ready, KT)
            pe.wait_ge(sg_lo, 1)
            shared_half(0)
            shared_half(1)
            pe.wait_ge(top_ready, 2)
            pe.wait_ge(misc_evac, 2)
            pe.transpose(bank[0:CS, mbank(2), 0:NE], top[:, :], ident[0:NE, 0:NE]).then_inc(misc_done, 1)
            pe.transpose(bank[0:CS, mbank(3), 0:NE], topf[:, :], ident[0:NE, 0:NE]).then_inc(misc_done, 1)
            pe.wait_ge(misc_evac, 4)
            tokens_turned(16)

            with pe.Fori(0, NE) as e:
                def misc_free(m):
                    pe.wait_ge(misc_evac, e * MJ + (M0 + m - 1))

                def chunk_halves(m, q, product):
                    for n in (2 * chunk[m, q], 2 * chunk[m, q] + 1):
                        pe.wait_ge(half_lo, e * (2 * EC) + (n + 1))
                        w = [t[:, n % NPC, :].rearrange("p (k f) -> p k f", k=3) for t in (eh, el)]
                        product(n % 2, *w).then_inc(used, 1)

                for m, q in order:
                    if m == "turn":
                        pe.wait_ge(hid_ready, e * HJ + (q + 3))
                        misc_free(M_HIDDEN + q)
                        for t in range(QT):
                            last = pe.transpose(bank[:, mbank(M_HIDDEN + q), t * CS:(t + 1) * CS],
                                                hid[:, q % 2, t * P:(t + 1) * P], ident[0:CS, 0:CS])
                        last.then_inc(misc_done, 1)
                    elif m == "d":
                        pe.wait_ge(misc_evac, e * MJ + (M0 + M_HIDDEN + q + 1))

                        def product(half, wh_, wl_):
                            for t in range(QT):
                                last = mm3(bank[0:CS, 4 + half, 0:HD], hid_h[:, q, t, :], hid_l[:, q, t, :],
                                           wh_[:, t, :], wl_[:, t, :], q == 0 and t == 0,
                                           q == NQ - 1 and t == QT - 1)
                            return last

                        chunk_halves(m, q, product)
                    else:
                        if m == "g":
                            if q == 0:
                                pe.wait_ge(misc_evac, e * MJ + M0)
                            pe.wait_ge(hid_ready, e * HJ + (q + 1))

                        def product(half, wh_, wl_):
                            for k in range(3):
                                kk = 3 * half + k
                                last = mm3(bank[0:CS, (2 * q + (m == "u")) % 4, 0:QT * P], xg_h[:, kk, :],
                                           xg_l[:, kk, :], wh_[:, k, :], wl_[:, k, :], kk == 0, kk == KT - 1)
                            return last

                        chunk_halves(m, q, product)
                pe.wait_ge(sg_lo, e + 2)
                shared_half(0)
                misc_free(M_TOKENS + 1)
                tokens_turned(e * 16 + 32)
                shared_half(1)
                pe.wait_ge(hs_lo, e * 2 + 2)
                pe.wait_ge(sd_lo, e + 1)
                pe.wait_ge(onehot_ready, e + 1)
                for n in range(2 * NT):
                    h, t = divmod(n, NT)
                    m = M_Y + n
                    misc_free(m)
                    c, d = slice(t * TN, (t + 1) * TN), slice(h * HD, (h + 1) * HD)
                    dst = bank[0:TN, mbank(m), 0:HD]
                    mm3(dst, hsh[:, c], hsl[:, c], sdh[:, d], sdl[:, d], True, False)
                    if t == 0:
                        pe.wait_ge(oe_lo, e * 2 + (h + 1))
                    pe.matmul(dst, onehot[:, c], oeh[:, d], start=False, stop=False)
                    pe.matmul(dst, onehot[:, c], oel[:, d], start=False, stop=True).then_inc(misc_done, 1)


def _pieces(w):
    i, o = w.shape
    return np.ascontiguousarray(w.reshape(i // P, P, o // P, P).transpose(2, 1, 0, 3)).reshape(o // P, P, i)


def _up_chunks(w):
    return w.reshape(NE, NQ, QT * P, KT, P).transpose(0, 1, 4, 3, 2).reshape(NE * NQ, P, CHUNK)


def _shared_up(w):
    return w.reshape(NE, SF, KT, P).transpose(0, 3, 2, 1).reshape(NE, P, KT * SF)


def _turned_vec(v):
    return np.ascontiguousarray(v.reshape(KT, P).T)


def kernel(**kw):
    import concourse.bacc as _bacc
    from concourse.bass_utils import run_bass_kernel_spmd as _run

    kw = {k: np.asarray(v) for k, v in kw.items()}
    arrays = {
        "x": kw["x"], "src": kw["src"], "dst": kw["dst"], "type": kw["edge_type_8"],
        "gamma": _turned_vec(kw["L0_mix_ln_gamma"]), "beta": _turned_vec(kw["L0_mix_ln_beta"]),
        "b_proj": _turned_vec(kw["L0_mix_b_proj"]),
        "b1": _turned_vec(kw["L0_gnn_b1"]), "b2": _turned_vec(kw["L0_gnn_b2"]),
        "wqkv": _pieces(kw["L0_mix_w_qkv"].T), "wproj": _pieces(kw["L0_mix_w_proj"].T),
        "root1": _pieces(kw["L0_gnn_root1"]), "root2": _pieces(kw["L0_gnn_root2"]),
        "W1": np.concatenate([_pieces(w) for w in kw["L0_gnn_W1"]]),
        "W2": np.concatenate([_pieces(w) for w in kw["L0_gnn_W2"]]),
        "gate_weight": kw["L0_ffn_gate_weight"].T.reshape(KT, P, NE).transpose(1, 0, 2),
        "Wg": _up_chunks(kw["L0_ffn_Wg"]), "Wu": _up_chunks(kw["L0_ffn_Wu"]),
        "Wd": kw["L0_ffn_Wd"].reshape(NE, 2, HD, NQ, QT, P).transpose(0, 3, 5, 1, 4, 2).reshape(NE * NQ, P, CHUNK),
        "Ws_gu": np.stack([_shared_up(kw["L0_ffn_Ws_g"]), _shared_up(kw["L0_ffn_Ws_u"])], 2).reshape(NE, P, -1),
        "Ws_d": kw["L0_ffn_Ws_d"].T.reshape(NE, SF, D),
    }
    nc = _bacc.Bacc("TRN2", target_bir_lowering=False, num_devices=1)
    arrays = {"in_" + k: np.ascontiguousarray(v) for k, v in arrays.items()}
    a = {k[3:]: nc.dram_tensor(k, v.shape, mybir.dt.from_np(v.dtype), kind="ExternalInput").ap()
         for k, v in arrays.items()}
    out = nc.dram_tensor("out", (N, D), F32, kind="ExternalOutput").ap()
    build(nc, a, out)
    r = _run(nc, [arrays], core_ids=[0])
    return r.results[0]["out"]
```

```python
from contextlib import ExitStack

import numpy as np
import concourse.bass as bass
from concourse import mybir

F32 = mybir.dt.float32
F32R = mybir.dt.float32r
I32 = mybir.dt.int32
U32 = mybir.dt.uint32
BF16 = mybir.dt.bfloat16
ALU = mybir.AluOpType
ACT = mybir.ActivationFunctionType

P = 128
N = 625
D = 768
R = 8
E = 10000
NT, TN = 5, 125
KT = D // P
NC, HC = 628, 314
HD = D // 2
NE, CAP = 16, 79
CS = 80
FE, FS = 3072, 1536
EB = E // TN
GB = 4
NG = EB // GB
ROWS = R * NC
TABLE = 128 * 24544
DUMP = N * ROWS
ZC = TABLE // P // 8
LATER = 2048.0
PIECE = KT * P
NRAW, NSPL = 6, 4
QT = 3
NQ = FE // (QT * P)
CHUNK = QT * D
HALF = CHUNK // 2
NRING, NR1 = 6, 4
NPC = 4
EC = 3 * NQ
SF = P
NSL = FS // SF
UN = 4
US = NSL * UN // NE
ROUNDS = CS // 8
MJ = 2 + NQ + 2 * NT
EPS_LN = 1e-5
EPS_Z = 1e-6


def build(nc, a, out):
    outer = ExitStack()
    with outer:
        def sb(name, shape, dt=F32, stack=outer):
            return stack.enter_context(nc.sbuf_tensor(name, shape, dt))

        def sem(name):
            return outer.enter_context(nc.semaphore(name))

        table = nc.dram_tensor("edge_table", (TABLE, 1), F32).ap()
        keys_dram = nc.dram_tensor("edge_keys", (EB, TN), F32).ap()
        xf_dram = nc.dram_tensor("ffn_input", (N, D), F32).ap()

        ps = outer.enter_context(nc.psum_tensor("ps", [P, 4, 1024], F32))
        psh = ps.rearrange("p k (h c) -> p k h c", h=2)

        ident = sb("ident", [P, P])
        ones = sb("ones", [P, P])
        onesr = sb("onesr", [P, P], F32R)
        eps_ln = sb("eps_ln", [P, 1])
        vecs = sb("vecs", [P, 5, KT])
        ring = sb("ring", [P, NR1, CHUNK])
        ring_start = ring.rearrange("p s c -> p (s c)")
        sum1 = ring_start[:, 0:KT * NC].rearrange("p (k n) -> p k n", k=KT)
        c = KT * NC
        xn = ring_start[0:TN, c:c + NT * D].rearrange("p (t d) -> p t d", t=NT)
        c += NT * D
        band = ring_start[:, c:c + (2 * GB - 1) * TN]
        c += (2 * GB - 1) * TN
        ef = ring_start[0:TN, c:c + 3 * EB].rearrange("p (n b) -> p n b", n=3)
        c += 3 * EB
        to_dump = ring_start[0:TN, c:c + EB]

        phase_a = ExitStack()
        sa = lambda name, shape, dt=F32: sb(name, shape, dt, phase_a)
        xh = sa("xh", [TN, NT, D], F32R)
        xl = sa("xl", [TN, NT, D], F32R)
        ecol = sa("ecol", [TN, 3, EB], I32)
        key = sa("key", [TN, EB])
        dump_cell = sa("dump_cell", [P, 1])
        keyT = sa("keyT", [EB, TN])
        keyrow = sa("keyrow", [TN, 2, GB * TN])
        eq = sa("eq", [TN, GB, GB * TN], BF16)
        cnt4 = sa("cnt4", [TN, 2, GB])
        later4 = sa("later4", [TN, GB])
        off4 = sa("off4", [TN, GB])
        idx4 = sa("idx4", [TN, 2, GB], I32)
        stats = sa("stats", [TN, 2, NT, 2, 6])
        mv = sa("mv", [TN, 2, NT, 2])
        rstd = sa("rstd", [TN, 2, NT])
        wraw = sa("wraw", [P, NRAW, PIECE])
        wh = sa("wh", [P, NSPL, PIECE], F32R)
        wl = sa("wl", [P, NSPL, PIECE], F32R)
        tmp = sa("tmp", [P, 2, 640])
        tmp2 = sa("tmp2", [P, 2, 640])
        inv = sa("inv", [P, NC])
        acc = sa("acc", [P, KT, NC])
        kv_bd = sa("kv_bd", [P, KT, P])
        ks_bd = sa("ks_bd", [P, KT, P])
        early = ExitStack()
        nat = sb("nat", [TN, NT, D], F32, early)
        kpc = sb("kpc", [TN, 2, NT, P], F32, early)
        vpc = sb("vpc", [TN, 2, NT, P], F32, early)
        early.close()
        cbuf = sa("cbuf", [TN, 2, NT * NC], F32R)
        sa("behind_cbuf", [TN, 4 * NT * P - 2 * NT * NC + NT * D])
        mh = sa("mh", [P, KT, NC], F32R)
        ml = sa("ml", [P, KT, NC], F32R)
        phase_a.close()
        phase_b = outer.enter_context(ExitStack())
        sbb = lambda name, shape, dt=F32: sb(name, shape, dt, phase_b)
        x2 = sbb("x2", [TN, NT, D])
        early = ExitStack()
        xf = sb("xf", [TN, NT, D], F32, early)
        early.close()
        ring2 = sbb("ring2", [P, NRING - NR1, CHUNK])
        hid_h = sbb("hid_h", [P, 2, QT, CS], F32R)
        hid_l = sbb("hid_l", [P, 2, QT, CS], F32R)
        sdh = sbb("sdh", [SF, D], F32R)
        sdl = sbb("sdl", [SF, D], F32R)
        oe = sbb("oe", [CS, D])
        oeh = sbb("oeh", [CS, D], F32R)
        eh = sbb("eh", [P, NPC, HALF], F32R)
        el = sbb("el", [P, NPC, HALF], F32R)
        fh = sbb("fh", [P, KT, NC], F32R)
        fl = sbb("fl", [P, KT, NC], F32R)
        sraw = sbb("sraw", [P, 2 * KT * SF])
        sgh = sbb("sgh", [P, 2 * KT * SF], F32R)
        sgl = sbb("sgl", [P, 2 * KT * SF], F32R)
        draw = sbb("draw", [SF, D])
        hs = sbb("hs", [SF, NC])
        hsh = sbb("hsh", [SF, NC], F32R)
        hsl = sbb("hsl", [SF, NC], F32R)
        early = ExitStack()
        ez = sb("ez", [NE, NC], F32, early)
        score = sb("score", [NE, 2, NC], F32, early)
        early.close()
        hid = sbb("hid", [CS, 2, QT * P])
        xg = sbb("xg", [CS, D])
        oel = sbb("oel", [CS, D], F32R)
        xg_h = sbb("xg_h", [P, KT, CS], F32R)
        xg_l = sbb("xg_l", [P, KT, CS], F32R)
        onehot = sbb("onehot", [CS, NC], F32R)
        iota_n = sbb("iota_n", [CS, NC])
        gw = sbb("gw", [P, KT, NE])
        gwh = sbb("gwh", [P, KT, NE], F32R)
        gwl = sbb("gwl", [P, KT, NE], F32R)
        top = sbb("top", [NE, CS])
        topi = sbb("topi", [NE, CS], U32)
        topf = sbb("topf", [NE, CS])
        slot_score = sbb("slot_score", [CS, NE])
        slot_tok = sbb("slot_tok", [CS, NE])
        slot_idx = sbb("slot_idx", [CS, NE], I32)
        stats3 = sbb("stats3", [TN, NT, 2, 6])
        mv3 = sbb("mv3", [TN, NT, 2])
        rstd3 = sbb("rstd3", [TN, NT])

        x_in = [sem(f"x_in{t}") for t in range(NT)]; edges_in = sem("edges_in"); vecs_in = sem("vecs_in")
        const_step = sem("const_step"); const_ready = sem("const_ready")
        zeros_ready = sem("zeros_ready"); table_zero = sem("table_zero")
        dve_step = sem("dve_step"); sqrt_done = sem("sqrt_done"); tmp_zero = sem("tmp_zero"); stats_done = sem("stats_done")
        yn_ready = sem("yn_ready"); key_ready = sem("key_ready"); v_copied = sem("v_copied"); xt_hi = sem("xt_hi"); keyT_done = sem("keyT_done")
        keyT_ready = sem("keyT_ready"); keys_stored = sem("keys_stored")
        row_in = [sem("row_in0"), sem("row_in1")]
        compared = sem("compared"); group_ready = sem("group_ready"); scattered = sem("scattered")
        raw_in = [sem(f"raw_in{i}") for i in range(NRAW)]
        w_hi = sem("w_hi"); w_lo = sem("w_lo")
        c_in = [sem("c_in0"), sem("c_in1")]
        pe_done = sem("pe_done"); evac = sem("evac")
        hi_ready = sem("hi_ready"); lo_ready = sem("lo_ready")
        xh_done = sem("xh_done"); xl_ready = sem("xl_ready")
        min_ready = sem("min_ready"); exp_ready = sem("exp_ready")
        cnt_done = sem("cnt_done"); inv_step = sem("inv_step"); inv_ready = sem("inv_ready")
        h_ready = sem("h_ready")
        xraw_in = sem("xraw_in"); out_done = sem("out_done")

        used = sem("used")
        half_hi = sem("half_hi"); half_lo = sem("half_lo"); turn_hi = sem("turn_hi"); oe_ready = sem("oe_ready")
        ring_in = [sem(f"ring_in{n}") for n in range(NRING)]
        xf_ready = sem("xf_ready"); xf_stored = sem("xf_stored"); gw_in = sem("gw_in")
        fh_ready = sem("fh_ready"); gw_hi = sem("gw_hi"); gw_lo = sem("gw_lo"); pads_zero = sem("pads_zero")
        ez_ready = sem("ez_ready"); top_ready = sem("top_ready"); idx_ready = sem("idx_ready")
        iota_ready = sem("iota_ready"); gathered = sem("gathered")
        sg_in = sem("sg_in"); sd_in = sem("sd_in")
        sg_hi = sem("sg_hi"); sg_lo = sem("sg_lo"); sd_hi = sem("sd_hi"); sd_lo = sem("sd_lo")
        shared_done = sem("shared_done"); silu_ready = sem("silu_ready"); hid_ready = sem("hid_ready")
        hs_hi = sem("hs_hi"); hs_lo = sem("hs_lo"); onehot_ready = sem("onehot_ready")
        oe_hi = sem("oe_hi"); oe_lo = sem("oe_lo")
        misc_done = sem("misc_done"); misc_evac = sem("misc_evac")

        J_Y = 0
        J_Q = J_Y + KT
        J_KV = J_Q + KT
        A_JOB = [J_KV] + [J_KV + 2 + 5 * (o - 1) for o in range(1, KT)]
        B_JOB = [J_KV + 1] + [A_JOB[o] + 2 for o in range(1, KT)]
        J_XT = B_JOB[-1] + 1
        J_MIXED = J_XT + KT
        mixed = ["root", "den", "num", "root", "product", "root", "den", "num", "root", "root", "root"]
        P_JOB = [A_JOB[o + 1] + 1 for o in range(KT - 1)] + [J_MIXED + 4]
        DEN_JOB = [A_JOB[o + 1] + 3 for o in range(KT - 2)] + [J_MIXED + 1, J_MIXED + 6]
        NUM_JOB = [j + 1 for j in DEN_JOB]
        ROOT1_JOB = [J_MIXED + n for n, x in enumerate(mixed) if x == "root"]
        J_PROJ = J_MIXED + len(mixed)
        J_REL1 = J_PROJ + KT
        RJ = 2 * KT
        J_HN = J_REL1 + R * RJ
        J_ROOT2 = J_HN + NT
        J_REL2 = J_ROOT2 + KT
        J_X2 = J_REL2 + R * RJ
        J_F = J_X2 + NT
        J_END = J_F + KT
        W_Q, W_KV = 0, KT
        W_ROOT1 = W_KV + 2 * KT
        W_PROJ = W_ROOT1 + KT
        W_REL1 = W_PROJ + KT
        W_ROOT2 = W_REL1 + R * KT
        W_REL2 = W_ROOT2 + KT
        W_END = W_REL2 + R * KT
        L_Y, L_ATT = 0, KT
        L_REL1 = 2 * KT
        L_H = L_REL1 + R * KT
        L_REL2 = L_H + KT

        Q_GROUPS, SECOND_GROUPS, ROOT_GROUPS, PROJ_GROUPS = (0, 1, 4, 5), (1, 2, 3, 4, 5), (1, 2, 3, 4), (0,)
        split_behind = [W_Q + o + NSPL + 1 for o in Q_GROUPS]
        for o in range(KT):
            split_behind += [W_KV + 2 * o + NSPL] + [W_KV + 2 * o + NSPL + 2] * (o in SECOND_GROUPS)
        split_behind += [W_ROOT1 + o + NSPL + 1 for o in ROOT_GROUPS]
        split_behind += [W_PROJ + o + NSPL + 1 for o in PROJ_GROUPS]
        assert len(split_behind) == NG

        def slot(j):
            return j % 3

        def piece(t, w):
            return t[:, w % NSPL, :].rearrange("p (k m) -> p k m", k=KT)

        def w_src(w):
            if w < W_KV:
                return a["wq"][w]
            if w < W_ROOT1:
                return a["wkv"][w - W_KV]
            if w < W_PROJ:
                return a["root1"][w - W_ROOT1]
            if w < W_REL1:
                return a["wproj"][w - W_PROJ]
            if w < W_REL2:
                return a["root2"][w - W_ROOT2]
            return a["wproj"][w - W_END]

        def halves(t):
            return t.rearrange("p (h c) -> p h c", h=2)

        def tiles_of(w, n):
            return w[:, 0:NT * P].rearrange("p (t c) -> p t c", c=P)[:, :, 0:n]

        def node_tiles(t):
            return t[:, 0:N].rearrange("p (t c) -> p t c", t=NT)

        bank = ps.rearrange("p k (h c) -> p (k h) c", h=2)
        M0 = 6
        M_HIDDEN = 0
        M_TOKENS = NQ
        M_Y = M_TOKENS + 2
        HJ = UN * NQ + 2 * US

        def with_slice(u):
            return u < US

        def makes_slice(u, final):
            return (u + 1) % UN < US and not (final and u == UN - 1)

        def experts(engine, expert):
            with engine.Fori(0, NE // UN - 1) as i:
                for u in range(UN):
                    expert(i, u, False)
            for u in range(UN):
                expert(NE // UN - 1, u, True)

        def made(u):
            return min(u, US - 1)

        def hjobs(u):
            return u * NQ + 2 * made(u)

        def kv_tiles(j, count, c):
            return ps[0:TN, slot(j), 0:count * 2 * P].rearrange("p (t c) -> p t c", c=2 * P)[:, :, c:c + P]

        def half_slice(t, n):
            return t[:, n * KT * SF:(n + 1) * KT * SF]

        def mbank(m):
            return 6 + m % 2

        order = [("g", 0), ("u", 0), ("g", 1), ("u", 1), ("turn", 0)]
        for q in range(2, NQ):
            order += [("g", q), ("u", q), ("turn", q - 1), ("d", q - 2)]
        order += [("turn", NQ - 1), ("d", NQ - 2), ("tokens", 0), ("d", NQ - 1)]
        chunks = [x for x in order if x[0] in "gud"]
        chunk = {x: c for c, x in enumerate(chunks)}

        def ring_slot(c):
            c %= NRING
            return ring[:, c, :] if c < NR1 else ring2[:, c - NR1, :]

        block = outer.enter_context(nc.Block())

        @block.sync
        def _(sp):
            for t in range(NT):
                sp.dma_start(nat[:, t, :], a["x"][t * TN:(t + 1) * TN, :]).then_inc(x_in[t], 16)
            for n, e in enumerate(("type", "dst", "src")):
                sp.dma_start(ecol[:, n, :], a[e].rearrange("(p b) -> p b", b=EB)).then_inc(edges_in, 16)
            for n, v in enumerate(("gamma", "beta", "b_proj", "b1", "b2")):
                sp.dma_start(vecs[:, n, :], a[v]).then_inc(vecs_in, 16)

            def load_piece(w):
                if w >= NRAW:
                    sp.wait_ge(w_lo, w - NRAW + 1)
                sp.dma_start(wraw[:, w % NRAW, :], w_src(w)).then_inc(raw_in[w % NRAW], 16)

            def load_row(g):
                if g >= 2:
                    sp.wait_ge(group_ready, g - 1)
                src = keys_dram[g * GB:(g + 1) * GB, :].rearrange("b c -> (b c)").unsqueeze(0)
                sp.dma_start(keyrow[:, g % 2, :], src.broadcast_to([TN, GB * TN])).then_inc(row_in[g % 2], 16)

            for w in range(NRAW):
                load_piece(w)
            def first_chunk(c):
                m, q = chunks[c]
                sp.dma_start(ring_slot(c), a["W" + m][q]).then_inc(ring_in[c % NRING], 16)

            sp.wait_ge(keyT_ready, 1)
            sp.dma_start(keys_dram, keyT[:, :]).then_inc(keys_stored, 16)
            sp.wait_ge(keys_stored, 16)
            load_row(0)
            load_row(1)

            rows = 2
            for w in range(NRAW, W_REL1):
                while rows < NG and split_behind[rows - 2] + NRAW <= w:
                    load_row(rows)
                    rows += 1
                load_piece(w)
            for g in range(rows, NG):
                load_row(g)

            def relations(wt, base_j, base_w):
                with sp.Fori(0, R // 2) as i:
                    for u in range(2):
                        sp.wait_ge(pe_done, i * (2 * RJ) + (base_j + (u - 2) * RJ + KT))
                        src = table[0:DUMP, :].rearrange("(t p r n) o -> p r t (n o)", t=NT, p=TN, r=R)
                        sp.dma_start(cbuf[:, u, :].bitcast(F32).rearrange("p (t n) -> p t n", t=NT),
                                     src[:, bass.ds(i * 2 + u, 1), :, :].rearrange("p r t n -> p (r t) n")
                                     ).then_inc(c_in[u], 16)
                        for o in range(KT):
                            sp.wait_ge(w_lo, i * (2 * KT) + (base_w + u * KT + o - NRAW + 1))
                            sp.dma_start(wraw[:, o, :], wt[bass.ds(i * (2 * KT) + (u * KT + o), 1)].rearrange(
                                "a p f -> (a p) f")).then_inc(raw_in[o], 16)

            sp.wait_ge(scattered, 16 * EB)
            relations(a["W1"], J_REL1, W_REL1)
            for w in range(W_ROOT2, W_REL2):
                load_piece(w)
            relations(a["W2"], J_REL2, W_REL2)
            for w in range(W_END, W_END + NSPL):
                load_piece(w)
            sp.wait_ge(evac, J_REL2)
            for c in range(NR1):
                first_chunk(c)
            sp.wait_ge(pe_done, J_X2 - KT)
            sp.dma_start(x2[:, :, :], a["x"].rearrange("(t p) d -> p t d", p=TN)).then_inc(xraw_in, 16)
            sp.wait_ge(pe_done, J_X2)
            sp.wait_ge(w_lo, W_END + NSPL)
            sp.dma_start(gw[:, :, :], a["gate_weight"]).then_inc(gw_in, 16)

            def load_shared(e):
                sp.dma_start(sraw[:, :], a["Ws_gu"][bass.ds(e, 1)].rearrange("a p f -> (a p) f")
                             ).then_inc(sg_in, 16)

            def load_shared_down(e):
                sp.dma_start(draw[:, :], a["Ws_d"][bass.ds(e, 1)].rearrange("a p f -> (a p) f")
                             ).then_inc(sd_in, 16)

            sp.wait_ge(pe_done, J_F)
            load_shared(0)
            load_shared_down(0)
            sp.wait_ge(xf_ready, 1)
            sp.dma_start(xf_dram.rearrange("(t p) d -> p t d", p=TN), xf[:, :, :]).then_inc(xf_stored, 16)
            sp.wait_ge(xf_stored, 16)
            sp.wait_ge(pe_done, J_END)
            for c in range(NR1, NRING):
                first_chunk(c)
            sp.wait_ge(sg_lo, 2)
            load_shared(1)

            def expert(i, u, final):
                for c in range(EC):
                    sp.wait_ge(half_lo, i * (UN * 2 * EC) + (u * 2 * EC + 2 * (c + 1)))
                    m, q = chunks[(c + NRING) % EC]
                    n = u + (c + NRING) // EC
                    e = i * UN + n if n < UN else (i * UN + UN) % NE
                    sp.dma_start(ring_slot(c), a["W" + m][bass.ds(e * NQ + q, 1)].rearrange("a p f -> (a p) f")
                                 ).then_inc(ring_in[c % NRING], 16)
                    if c == 15 and makes_slice(u, final) and not (final and u == US - 2):
                        sp.wait_ge(sg_lo, i * (2 * US) + (2 * made(u) + 4))
                        load_shared(i * US + (made(u) + 2))
                    if c == 8 and with_slice(u) and not (final and u == US - 1):
                        sp.wait_ge(sd_lo, i * US + (u + 1))
                        load_shared_down(i * US + (u + 1))

            experts(sp, expert)
            for n in range(NRING):
                sp.wait_ge(ring_in[n], 16 * (NE * EC // NRING + 1))
            sp.wait_ge(sg_in, 16 * NSL)
            sp.wait_ge(sd_in, 16 * NSL)
            sp.wait_ge(misc_evac, M0 + MJ * NE)
            sp.dma_start(out.rearrange("(t p) d -> p t d", p=TN), x2[:, :, :]).then_inc(out_done, 16)
            sp.wait_ge(out_done, 16)

        @block.gpsimd
        def _(pool):
            zeros = ring_start[:, 0:ZC]
            pool.memset(zeros, 0.0).then_inc(zeros_ready, 1)
            pool.memset(ident[:, :], 0.0).then_inc(const_step, 1)
            pool.memset(band[:, :], 1.0).then_inc(const_step, 1)
            pool.memset(ones[:, :], 1.0).then_inc(const_step, 1)
            pool.memset(onesr[:, :].bitcast(F32), 1.0).then_inc(const_step, 1)
            pool.memset(eps_ln[:, :], EPS_LN).then_inc(const_step, 1)
            pool.memset(kv_bd[:, :, :], 0.0).then_inc(const_step, 1)
            pool.memset(ks_bd[:, :, :], 0.0).then_inc(const_step, 1)
            pool.wait_ge(const_step, 7)
            pool.affine_select(out=ident[:, :], in_=ident[:, :], compare_op=ALU.not_equal, fill=1.0, base=0,
                               pattern=[[-1, P]], channel_multiplier=1).then_inc(const_ready, 1)
            pool.affine_select(out=band[:, :], in_=band[:, :], compare_op=ALU.is_ge, fill=LATER,
                               base=(GB - 1) * TN, pattern=[[-1, (2 * GB - 1) * TN]],
                               channel_multiplier=1).then_inc(const_ready, 1)
            pool.iota(dump_cell[:, :], pattern=[[0, 1]], base=DUMP, channel_multiplier=1,
                      allow_small_or_imprecise_dtypes=True).then_inc(const_ready, 1)
            pool.wait_ge(table_zero, 8 * 16)
            for g in range(NG):
                pool.wait_ge(group_ready, g + 1)
                if g >= 1:
                    pool.wait_ge(scattered, 16 * GB * g)
                for b in range(GB):
                    pool.indirect_dma_start(
                        out=table, out_offset=bass.IndirectOffsetOnAxis(ap=idx4[:, g % 2, b:b + 1], axis=0),
                        in_=cnt4[:, g % 2, b:b + 1], in_offset=None, compute_op=ALU.add
                    ).then_inc(scattered, 16)
            pool.wait_ge(pe_done, J_X2)
            pool.wait_ge(lo_ready, L_REL2 + R * KT)
            pool.wait_ge(w_lo, W_END + NSPL)
            pool.iota(iota_n[:, :], pattern=[[1, NC]], base=0, channel_multiplier=0,
                      allow_small_or_imprecise_dtypes=True).then_inc(iota_ready, 1)
            pool.wait_ge(idx_ready, 1)
            pool.wait_ge(xf_stored, 16)
            for n in range(NE + 1):
                e = min(n, NE - 1)
                if n:
                    pool.wait_ge(misc_done, M0 if n == 1 else M0 + MJ * (n - 2) + M_TOKENS + 2)
                pool.indirect_dma_start(
                    out=xg[:, :], out_offset=None, in_=xf_dram,
                    in_offset=bass.IndirectOffsetOnAxis(ap=slot_idx[:, e:e + 1], axis=0)
                ).then_inc(gathered, 16)

        @block.scalar
        def _(act):
            def split_weight(w):
                act.wait_ge(raw_in[w % NRAW], 16 * (w // NRAW + 1))
                act.copy(wh[:, w % NSPL, :], wraw[:, w % NRAW, :]).then_inc(w_hi, 1)

            def clear(z):
                act.dma_start(table.rearrange("(z p c) o -> z p (c o)", z=8, p=P)[z], ring_start[:, 0:ZC]
                              ).then_inc(table_zero, 16)

            for ln in range(2):
                act.wait_ge(const_ready, 3)
                act.wait_ge(stats_done, ln + 1)
                act.activation(rstd[:, ln, :], mv[:, ln, :, 1], ACT.Sqrt, bias=eps_ln[0:TN, :]).then_inc(sqrt_done, 1)
                if ln == 0:
                    for w in range(NSPL):
                        split_weight(w)
                    act.wait_ge(zeros_ready, 1)
                    for z in range(3):
                        clear(z)

            def next_weight(j, w):
                act.wait_ge(pe_done, j + 1)
                split_weight(w + NSPL)

            def exponent(n, low, src, e, reader=None):
                if reader is not None:
                    act.wait_ge(evac, reader + 1)
                act.activation(low, src, ACT.Relu, scale=-1.0).then_inc(min_ready, 1)
                act.wait_ge(min_ready, n + 1)
                act.activation(e, low, ACT.Exp, scale=-1.0).then_inc(exp_ready, 1)

            for k in range(KT):
                act.wait_ge(evac, J_Y + k + 1)
                act.copy(mh[:, k, :], tmp[:, k % 2, 0:NC]).then_inc(hi_ready, 1)
                if k % 2 == 0:
                    clear(3 + k // 2)
            for o in range(KT):
                next_weight(J_Q + o, W_Q + o)
                if o < 2:
                    clear(6 + o)
                    act.wait_ge(lo_ready, L_Y + KT)
                exponent(o, halves(tmp[:, o % 2, 0:NC]), psh[:, slot(J_Q + o), :, 0:HC],
                         halves(tmp2[:, o % 2, 0:NC]), J_Q + o - 2 if o >= 2 else None)
            for t in range(NT):
                act.copy(xh[:, t, :], xn[:, t, :]).then_inc(xh_done, 1)
            for o in range(KT):
                for n, (j, t0, t1) in enumerate(((A_JOB[o], 0, 4), (B_JOB[o], 4, NT))):
                    act.wait_ge(pe_done, j + 1)
                    low, e = [x[0:TN, o % 2, t0 * P:t1 * P].rearrange("p (t c) -> p t c", c=P)
                              for x in (tmp, tmp2)]
                    exponent(KT + 2 * o + n, low, kv_tiles(j, t1 - t0, 0), e,
                             B_JOB[o - 2] if o >= 2 else J_Q + KT - 2 + o)
                    act.copy(vpc[:, o % 2, t0:t1, :], kv_tiles(j, t1 - t0, P)).then_inc(v_copied, 1)
                next_weight(B_JOB[o], W_KV + 2 * o)
                next_weight(B_JOB[o], W_KV + 2 * o + 1)
            for k in range(KT):
                act.wait_ge(pe_done, J_XT + k + 1)
                act.copy(node_tiles(mh[:, k, :]), tiles_of(ps[:, slot(J_XT + k), :], TN)).then_inc(xt_hi, 1)
            for o in range(KT):
                next_weight(ROOT1_JOB[o], W_ROOT1 + o)
            for h in range(KT):
                act.wait_ge(evac, NUM_JOB[h] + 1)
                act.copy(mh[:, h, :], acc[:, h, :]).then_inc(hi_ready, 1)
            for o in range(KT):
                next_weight(J_PROJ + o, W_PROJ + o)

            def relations(base_j, base_w):
                with act.Fori(0, R // 2) as i:
                    for u in range(2):
                        j, w = base_j + u * RJ, base_w + u * KT
                        for k in range(KT):
                            act.wait_ge(evac, i * (2 * RJ) + (j + k + 1))
                            act.copy(mh[:, k, :], tmp[:, k % 2, 0:NC]).then_inc(hi_ready, 1)
                        for o in range(KT):
                            act.wait_ge(pe_done, i * (2 * RJ) + (j + KT + o + 1))
                            nw = w + o + NSPL
                            act.wait_ge(raw_in[nw % NRAW], i * 32 + 16 * (nw // NRAW + 1))
                            act.copy(wh[:, nw % NSPL, :], wraw[:, nw % NRAW, :]).then_inc(w_hi, 1)

            relations(J_REL1, W_REL1)
            for k in range(KT):
                act.wait_ge(h_ready, k + 1)
                act.copy(mh[:, k, :], sum1[:, k, :]).then_inc(hi_ready, 1)
            for t in range(NT):
                act.wait_ge(pe_done, J_HN + t + 1)
                act.copy(xh[:, t, :], ps[0:TN, slot(J_HN + t), 0:D]).then_inc(xh_done, 1)
            for o in range(KT):
                next_weight(J_ROOT2 + o, W_ROOT2 + o)
            relations(J_REL2, W_REL2)

            act.wait_ge(stats_done, 3)
            act.activation(rstd3[:, :], mv3[:, :, 1], ACT.Sqrt, bias=eps_ln[0:TN, :]).then_inc(sqrt_done, 1)
            act.wait_ge(gw_in, 16)
            act.copy(gwh[:, :, :], gw[:, :, :]).then_inc(gw_hi, 1)
            for k in range(KT):
                act.wait_ge(pe_done, J_F + k + 1)
                act.copy(node_tiles(fh[:, k, :]),
                         ps[:, slot(J_F + k), 0:NT * P].rearrange("p (t c) -> p t c", c=P)[:, :, 0:TN]
                         ).then_inc(fh_ready, 1)
            for h in range(2):
                act.wait_ge(misc_done, h + 1)
                act.activation(ez[:, h * HC:(h + 1) * HC], bank[0:NE, mbank(h), 0:HC], ACT.Exp,
                               scale=-1.0).then_inc(ez_ready, 1)
            act.wait_ge(sg_in, 16)
            for n in range(2):
                act.copy(half_slice(sgh, n), half_slice(sraw, n)).then_inc(sg_hi, 1)

            def half_of_chunk(n):
                return ring_slot(n // 2)[:, (n % 2) * HALF:(n % 2 + 1) * HALF]

            for n in range(NPC):
                act.wait_ge(ring_in[n // 2], 16)
                act.copy(eh[:, n, :], half_of_chunk(n)).then_inc(half_hi, 1)

            def turned(count, dst, m):
                act.wait_ge(misc_done, count)
                act.copy(dst, bank[:, mbank(m), 0:QT * CS]).then_inc(turn_hi, 1)

            def tokens_hi(h, count):
                turned(count, xg_h[:, 3 * h:3 * h + 3, :].rearrange("p k c -> p (k c)"), M_TOKENS + h)

            def shared_silu(h, count):
                act.wait_ge(shared_done, count)
                act.activation(hs[:, h * HC:(h + 1) * HC], bank[0:SF, 2 * h, 0:HC], ACT.Silu
                               ).then_inc(silu_ready, 1)

            for h in range(2):
                shared_silu(h, h + 1)
            for h in range(2):
                tokens_hi(h, M0 - 2 + h + 1)

            def expert(i, u, final):
                def at(each, n):
                    return i * (UN * each) + (u * each + n)

                def output_hi(h):
                    act.wait_ge(oe_ready, at(2, h + 1))
                    act.copy(oeh[:, h * HD:(h + 1) * HD], oe[:, h * HD:(h + 1) * HD]).then_inc(oe_hi, 1)

                act.wait_ge(misc_done, at(MJ, M0))
                for h in range(2 if with_slice(u) else 0):
                    act.wait_ge(hid_ready, i * HJ + (hjobs(u) + h + 1))
                    act.copy(hsh[:, h * HC:(h + 1) * HC], hs[:, h * HC:(h + 1) * HC]).then_inc(hs_hi, 1)
                for m, q in order:
                    if m == "tokens":
                        for h in range(2):
                            tokens_hi(h, at(MJ, M0 + M_TOKENS + h + 1))
                        continue
                    if m == "turn":
                        turned(at(MJ, M0 + M_HIDDEN + q + 1),
                               hid_h[:, q % 2, :, :].rearrange("p t c -> p (t c)"), M_HIDDEN + q)
                        if q == 0 and with_slice(u):
                            act.wait_ge(sd_in, i * (16 * US) + 16 * (u + 1))
                            act.copy(sdh[:, :], draw[:, :]).then_inc(sd_hi, 1)
                        if q in (2, 4) and makes_slice(u, final):
                            n = q // 2 - 1
                            act.wait_ge(sg_in, i * (16 * US) + 16 * (made(u) + 2))
                            act.copy(half_slice(sgh, n), half_slice(sraw, n)).then_inc(sg_hi, 1)
                        continue
                    for n in (2 * chunk[m, q], 2 * chunk[m, q] + 1):
                        act.wait_ge(used, at(2 * EC, n + 1))
                        if n == 2 * EC - 1:
                            output_hi(1)
                        c = (n + NPC) // 2
                        act.wait_ge(ring_in[c % NRING], at(16 * EC // NRING, 16 * (c // NRING + 1)))
                        act.copy(eh[:, n % NPC, :], half_of_chunk(n + NPC)).then_inc(half_hi, 1)
                        if n == 2 * EC - 2:
                            output_hi(0)
                    if m == "u":
                        act.activation(hid[:, q % 2, :], bank[0:CS, 2 * q % 4, 0:QT * P], ACT.Silu
                                       ).then_inc(silu_ready, 1)
                for h in range(2 if makes_slice(u, final) else 0):
                    shared_silu(h, i * (2 * US) + (2 * made(u) + h + 3))

            experts(act, expert)

        @block.vector
        def _(dve):
            steps = [0]

            def then(ins):
                steps[0] += 1
                ins.then_inc(dve_step, 1)
                dve.wait_ge(dve_step, steps[0])

            dve.memset(tmp[:, :, :], 0.0).then_inc(tmp_zero, 1)

            for ln, (src, dst) in enumerate(((nat, xn), (xn, nat))):
                for t in range(NT):
                    if ln == 0:
                        dve.wait_ge(x_in[t], 16)
                    for h in range(2):
                        ins = dve.bn_stats(stats[:, ln, t, h, :], src[:, t, h * HD:(h + 1) * HD])
                then(ins)
                for t in range(NT):
                    ins = dve.bn_aggr(mv[:, ln, t, :], stats[:, ln, t, :, :])
                ins.then_inc(stats_done, 1)
                if ln == 0:
                    dve.wait_ge(edges_in, 48)
                    then(dve.tensor_copy(ef[:, :, :], ecol[:, :, :]))
                    then(dve.scalar_tensor_tensor(out=key[:, :], in0=ef[:, 0, :], scalar=float(NC),
                                                  in1=ef[:, 1, :], op0=ALU.mult, op1=ALU.add))
                    dve.scalar_tensor_tensor(out=key[:, :], in0=ef[:, 2, :], scalar=float(ROWS), in1=key[:, :],
                                             op0=ALU.mult, op1=ALU.add).then_inc(key_ready, 1)
                    dve.wait_ge(const_ready, 3)
                    dve.wait_ge(key_ready, 1)
                    then(dve.tensor_scalar(to_dump[:, :], key[:, :], -1.0, dump_cell[0:TN, 0:1],
                                           ALU.mult, ALU.add))
                dve.wait_ge(sqrt_done, ln + 1)
                then(dve.reciprocal(rstd[:, ln, :], rstd[:, ln, :]))
                for t in range(NT):
                    ins = dve.tensor_scalar(dst[:, t, :], src[:, t, :], mv[:, ln, t, 0:1], rstd[:, ln, t:t + 1],
                                            ALU.subtract, ALU.mult)
                if ln == 0:
                    then(ins)
                    dve.wait_ge(keyT_done, 1)
                    dve.tensor_copy(keyT[:, :], ps[0:EB, 3, 0:TN]).then_inc(keyT_ready, 1)
                else:
                    ins.then_inc(yn_ready, 1)

            def split_weight(w):
                dve.wait_ge(w_hi, w + 1)
                dve.tensor_tensor(wl[:, w % NSPL, :], wraw[:, w % NRAW, :], wh[:, w % NSPL, :].bitcast(F32),
                                  ALU.subtract).then_inc(w_lo, 1)

            def lo(n, k):
                dve.wait_ge(hi_ready, n + 1)
                dve.tensor_tensor(ml[:, k, :], tmp[:, k % 2, 0:NC], mh[:, k, :].bitcast(F32),
                                  ALU.subtract).then_inc(lo_ready, 1)

            def group(g):
                dve.wait_ge(row_in[g % 2], 16 * (g // 2 + 1))
                if g >= 2:
                    dve.wait_ge(scattered, 16 * GB * (g - 1))
                b0 = GB * g
                if g >= 1:
                    dve.wait_ge(compared, GB * g)
                for b in range(GB):
                    dve.scalar_tensor_tensor(out=eq[:, b, :], in0=keyrow[:, g % 2, :],
                                             scalar=key[:, b0 + b:b0 + b + 1],
                                             in1=band[0:TN, (GB - 1 - b) * TN:(2 * GB - 1 - b) * TN],
                                             op0=ALU.is_equal, op1=ALU.mult,
                                             accum_out=cnt4[:, g % 2, b:b + 1]).then_inc(compared, 1)
                dve.wait_ge(compared, GB * (g + 1))
                then(dve.tensor_scalar(later4[:, :], cnt4[:, g % 2, :], LATER, None, ALU.is_ge))
                then(dve.tensor_tensor(off4[:, :], later4[:, :], to_dump[:, b0:b0 + GB], ALU.mult))
                dve.tensor_tensor(idx4[:, g % 2, :], off4[:, :], key[:, b0:b0 + GB], ALU.add).then_inc(group_ready, 1)

            groups = [0]

            def next_group():
                group(groups[0])
                groups[0] += 1

            def job(j):
                dve.wait_ge(pe_done, j + 1)
                return ps[:, slot(j), :], psh[:, slot(j), :, 0:HC]

            dve.wait_ge(vecs_in, 80)
            dve.wait_ge(tmp_zero, 1)
            for k in range(KT):
                whole, _ = job(J_Y + k)
                if k >= 2:
                    dve.wait_ge(lo_ready, L_Y + k - 1)
                dve.tensor_scalar(node_tiles(tmp[:, k % 2, :]),
                                  whole[:, 0:NT * P].rearrange("p (t c) -> p t c", c=P)[:, :, 0:TN],
                                  vecs[:, 0, k:k + 1], vecs[:, 1, k:k + 1], ALU.mult, ALU.add).then_inc(evac, 1)
                if k:
                    lo(L_Y + k - 1, k - 1)
                if k < NSPL:
                    split_weight(k)
            lo(L_Y + KT - 1, KT - 1)

            for o in range(KT):
                _, cols = job(J_Q + o)
                split_weight(W_Q + o + NSPL)
                if o in Q_GROUPS:
                    next_group()
                dve.wait_ge(exp_ready, o + 1)
                dve.scalar_tensor_tensor(out=halves(acc[:, o, :]), in0=cols, scalar=0.0,
                                         in1=halves(tmp2[:, o % 2, 0:NC]), op0=ALU.max, op1=ALU.add
                                         ).then_inc(evac, 1)

            def product(o):
                j = P_JOB[o]
                whole, _ = job(j)
                dve.wait_ge(const_step, 7)
                for dst, c in ((kv_bd, 0), (ks_bd, 512)):
                    for q in (0, 64):
                        ins = dve.tensor_copy(dst[q:q + 64, o, q:q + 64], whole[q:q + 64, c + q:c + q + 64])
                ins.then_inc(evac, 1)

            def natural_elu(o, n):
                j, t0, t1 = ((A_JOB[o], 0, 4), (B_JOB[o], 4, NT))[n]
                job(j)
                e = tmp2[0:TN, o % 2, t0 * P:t1 * P].rearrange("p (t c) -> p t c", c=P)
                src = kv_tiles(j, t1 - t0, 0)
                if n == 0:
                    next_group()
                dve.wait_ge(exp_ready, KT + 2 * o + n + 1)
                dve.wait_ge(v_copied, 2 * o + n + 1)
                dve.scalar_tensor_tensor(out=kpc[:, o % 2, t0:t1, :], in0=src, scalar=0.0, in1=e, op0=ALU.max,
                                         op1=ALU.add).then_inc(evac, 1)

            def attend(h):
                _, den = job(DEN_JOB[h])
                if h:
                    dve.wait_ge(evac, NUM_JOB[h - 1] + 1)
                dve.tensor_scalar(halves(inv[:, :]), den, EPS_Z, None, ALU.add).then_inc(evac, 1)
                dve.wait_ge(evac, DEN_JOB[h] + 1)
                then(dve.reciprocal(inv[:, :], inv[:, :]))
                _, num = job(NUM_JOB[h])
                dve.tensor_tensor(halves(acc[:, h, :]), num, halves(inv[:, :]), ALU.mult).then_inc(evac, 1)

            def attention_lo(k):
                dve.wait_ge(hi_ready, L_ATT + k + 1)
                dve.tensor_tensor(ml[:, k, :], acc[:, k, :], mh[:, k, :].bitcast(F32),
                                  ALU.subtract).then_inc(lo_ready, 1)

            for o in range(KT):
                natural_elu(o, 0)
                if o:
                    product(o - 1)
                natural_elu(o, 1)
                split_weight(W_KV + 2 * o + NSPL)
                split_weight(W_KV + 2 * o + 1 + NSPL)
                if 0 < o < KT - 1:
                    attend(o - 1)
                if o in SECOND_GROUPS:
                    next_group()
            for k in range(KT):
                dve.wait_ge(xt_hi, k + 1)
                dve.tensor_tensor(node_tiles(ml[:, k, :]), tiles_of(ps[:, slot(J_XT + k), :], TN),
                                  node_tiles(mh[:, k, :]).bitcast(F32), ALU.subtract).then_inc(evac, 1)
            dve.wait_ge(table_zero, 8 * 16)
            for o in range(KT):
                _, cols = job(ROOT1_JOB[o])
                dve.tensor_scalar(halves(sum1[:, o, :]), cols, vecs[:, 3, o:o + 1], None, ALU.add).then_inc(evac, 1)
                split_weight(W_ROOT1 + o + NSPL)
                if o == 0:
                    attend(KT - 2)
                elif o == 1:
                    product(KT - 1)
                elif o == 2:
                    attend(KT - 1)
                if o in ROOT_GROUPS:
                    next_group()
            for k in range(KT):
                attention_lo(k)
            for o in range(KT):
                _, cols = job(J_PROJ + o)
                dve.tensor_scalar(halves(acc[:, o, :]), cols, vecs[:, 2, o:o + 1], None, ALU.add).then_inc(evac, 1)
                split_weight(W_PROJ + o + NSPL)
                if o in PROJ_GROUPS:
                    next_group()
                if o < NT:
                    dve.wait_ge(xh_done, o + 1)
                    dve.tensor_tensor(xl[:, o, :], xn[:, o, :], xh[:, o, :].bitcast(F32),
                                      ALU.subtract).then_inc(xl_ready, 1)

            def relations(layer, base_j, base_w, base_l):
                total = (sum1, acc)[layer]
                with dve.Fori(0, R // 2) as i:
                    for u in range(2):
                        j, w, l = base_j + u * RJ, base_w + u * KT, base_l + u * KT
                        n = layer * R + u
                        dve.wait_ge(cnt_done, i * 2 + (n + 1))
                        dve.tensor_scalar(halves(inv[:, :]), psh[:, 3, :, 0:HC], 1.0, None,
                                          ALU.max).then_inc(inv_step, 1)
                        dve.wait_ge(inv_step, i * 2 + (n + 1))
                        dve.reciprocal(inv[:, :], inv[:, :]).then_inc(inv_ready, 1)
                        dve.wait_ge(inv_ready, i * 2 + (n + 1))

                        def mean_lo(k):
                            dve.wait_ge(hi_ready, i * (2 * KT) + (l + k + 1))
                            dve.tensor_tensor(ml[:, k, :], tmp[:, k % 2, 0:NC], mh[:, k, :].bitcast(F32),
                                              ALU.subtract).then_inc(lo_ready, 1)

                        for k in range(KT):
                            dve.wait_ge(pe_done, i * (2 * RJ) + (j + k + 1))
                            if k >= 2:
                                dve.wait_ge(lo_ready, i * (2 * KT) + (l + k - 1))
                            dve.tensor_tensor(halves(tmp[:, k % 2, 0:NC]), psh[:, slot(j + k), :, 0:HC],
                                              halves(inv[:, :]), ALU.mult).then_inc(evac, 1)
                            if k:
                                mean_lo(k - 1)
                        mean_lo(KT - 1)
                        for o in range(KT):
                            dve.wait_ge(pe_done, i * (2 * RJ) + (j + KT + o + 1))
                            dve.tensor_tensor(halves(total[:, o, :]), psh[:, slot(j + KT + o), :, 0:HC],
                                              halves(total[:, o, :]), ALU.add).then_inc(evac, 1)
                            nw = w + o + NSPL
                            dve.wait_ge(w_hi, i * (2 * KT) + (nw + 1))
                            dve.tensor_tensor(wl[:, nw % NSPL, :], wraw[:, nw % NRAW, :],
                                              wh[:, nw % NSPL, :].bitcast(F32), ALU.subtract).then_inc(w_lo, 1)

            relations(0, J_REL1, W_REL1, L_REL1)
            dve.wait_ge(evac, J_HN)
            for k in range(KT):
                dve.tensor_scalar(sum1[:, k, :], sum1[:, k, :], 0.0, None, ALU.max).then_inc(h_ready, 1)
            for k in range(KT):
                dve.wait_ge(hi_ready, L_H + k + 1)
                dve.tensor_tensor(ml[:, k, :], sum1[:, k, :], mh[:, k, :].bitcast(F32),
                                  ALU.subtract).then_inc(lo_ready, 1)
            for t in range(NT):
                whole, _ = job(J_HN + t)
                dve.wait_ge(xh_done, NT + t + 1)
                dve.tensor_tensor(xl[:, t, :], whole[0:TN, 0:D], xh[:, t, :].bitcast(F32),
                                  ALU.subtract).then_inc(evac, 1)
            for o in range(KT):
                _, cols = job(J_ROOT2 + o)
                dve.scalar_tensor_tensor(out=halves(acc[:, o, :]), in0=cols, scalar=vecs[:, 4, o:o + 1],
                                         in1=halves(acc[:, o, :]), op0=ALU.add, op1=ALU.add).then_inc(evac, 1)
                split_weight(W_ROOT2 + o + NSPL)
            relations(1, J_REL2, W_REL2, L_REL2)
            dve.wait_ge(xraw_in, 16)
            for t in range(NT):
                whole, _ = job(J_X2 + t)
                dve.tensor_tensor(x2[:, t, :], whole[0:TN, 0:D], x2[:, t, :], ALU.add).then_inc(evac, 1)
            dve.memset(fh[:, :, N:NC].bitcast(F32), 0.0).then_inc(pads_zero, 1)
            dve.memset(fl[:, :, N:NC].bitcast(F32), 0.0).then_inc(pads_zero, 1)

            dve.wait_ge(evac, J_F)
            for t in range(NT):
                for h in range(2):
                    ins = dve.bn_stats(stats3[:, t, h, :], x2[:, t, h * HD:(h + 1) * HD])
            then(ins)
            for t in range(NT):
                ins = dve.bn_aggr(mv3[:, t, :], stats3[:, t, :, :])
            ins.then_inc(stats_done, 1)
            dve.wait_ge(sqrt_done, 3)
            then(dve.reciprocal(rstd3[:, :], rstd3[:, :]))
            for t in range(NT):
                ins = dve.tensor_scalar(xf[:, t, :], x2[:, t, :], mv3[:, t, 0:1], rstd3[:, t:t + 1],
                                        ALU.subtract, ALU.mult)
            ins.then_inc(xf_ready, 1)
            dve.wait_ge(gw_hi, 1)
            dve.tensor_tensor(gwl[:, :, :], gw[:, :, :], gwh[:, :, :].bitcast(F32), ALU.subtract).then_inc(gw_lo, 1)
            for k in range(KT):
                dve.wait_ge(fh_ready, k + 1)
                dve.tensor_tensor(node_tiles(fl[:, k, :]),
                                  ps[:, slot(J_F + k), 0:NT * P].rearrange("p (t c) -> p t c", c=P)[:, :, 0:TN],
                                  node_tiles(fh[:, k, :]).bitcast(F32), ALU.subtract).then_inc(evac, 1)
            for n in range(2):
                dve.wait_ge(sg_hi, n + 1)
                dve.tensor_tensor(half_slice(sgl, n), half_slice(sraw, n), half_slice(sgh, n).bitcast(F32),
                                  ALU.subtract).then_inc(sg_lo, 1)

            dve.wait_ge(ez_ready, 2)
            dve.tensor_scalar(ez[:, :], ez[:, :], 1.0, None, ALU.add).then_inc(misc_evac, 2)
            dve.wait_ge(misc_evac, 2)
            then(dve.reciprocal(score[:, 0, :], ez[:, :]))
            for r in range(ROUNDS):
                v, cur, nxt = top[:, 8 * r:8 * r + 8], score[:, r % 2, 0:N], score[:, 1 - r % 2, 0:N]
                then(dve.max(v, cur))
                ins = dve.max_index(topi[:, 8 * r:8 * r + 8], v, cur)
                if r < ROUNDS - 1:
                    ins = dve.match_replace(nxt, v, cur, -1.0)
                then(ins)
            dve.memset(top[:, CAP:CS], 0.0).then_inc(top_ready, 1)
            dve.tensor_copy(topf[:, :], topi[:, :]).then_inc(top_ready, 1)
            dve.wait_ge(misc_done, 3)
            dve.tensor_copy(slot_score[:, :], bank[0:CS, mbank(2), 0:NE]).then_inc(misc_evac, 1)
            dve.wait_ge(misc_done, 4)
            dve.tensor_copy(slot_idx[:, :], bank[0:CS, mbank(3), 0:NE]).then_inc(idx_ready, 1)
            dve.tensor_copy(slot_tok[:, :], bank[0:CS, mbank(3), 0:NE]).then_inc(misc_evac, 1)
            dve.wait_ge(misc_evac, 4)
            dve.wait_ge(iota_ready, 1)

            def half_of_chunk(n):
                return ring_slot(n // 2)[:, (n % 2) * HALF:(n % 2 + 1) * HALF]

            for n in range(NPC):
                dve.wait_ge(half_hi, n + 1)
                dve.tensor_tensor(el[:, n, :], half_of_chunk(n), eh[:, n, :].bitcast(F32),
                                  ALU.subtract).then_inc(half_lo, 1)

            def turned(count, dst, hi, m):
                dve.wait_ge(turn_hi, count)
                dve.tensor_tensor(dst, bank[:, mbank(m), 0:QT * CS], hi.bitcast(F32),
                                  ALU.subtract).then_inc(misc_evac, 1)

            def tokens_lo(h, count):
                x = [t[:, 3 * h:3 * h + 3, :].rearrange("p k c -> p (k c)") for t in (xg_l, xg_h)]
                turned(count, x[0], x[1], M_TOKENS + h)

            def shared_hidden(h, count):
                x = hs[:, h * HC:(h + 1) * HC]
                dve.wait_ge(silu_ready, count)
                dve.tensor_tensor(x, x, bank[0:SF, 2 * h + 1, 0:HC], ALU.mult).then_inc(hid_ready, 1)

            for h in range(2):
                shared_hidden(h, h + 1)
            for h in range(2):
                tokens_lo(h, h + 1)

            def expert(i, u, final):
                def at(each, n):
                    return i * (UN * each) + (u * each + n)

                def output_lo(h):
                    dve.wait_ge(oe_hi, at(2, h + 1))
                    dve.tensor_tensor(oel[:, h * HD:(h + 1) * HD], oe[:, h * HD:(h + 1) * HD],
                                      oeh[:, h * HD:(h + 1) * HD].bitcast(F32), ALU.subtract).then_inc(oe_lo, 1)

                def half_chunk_lo(n):
                    dve.wait_ge(half_hi, at(2 * EC, n + NPC + 1))
                    dve.tensor_tensor(el[:, n % NPC, :], half_of_chunk(n + NPC),
                                      eh[:, n % NPC, :].bitcast(F32), ALU.subtract).then_inc(half_lo, 1)

                dve.wait_ge(misc_done, at(MJ, M0))
                dve.tensor_scalar(onehot[:, :], iota_n[:, :], slot_tok[:, bass.ds(i * UN + u, 1)], None,
                                  ALU.is_equal).then_inc(onehot_ready, 1)
                for h in range(2 if with_slice(u) else 0):
                    dve.wait_ge(hs_hi, i * (2 * US) + (2 * u + h + 1))
                    dve.tensor_tensor(hsl[:, h * HC:(h + 1) * HC], hs[:, h * HC:(h + 1) * HC],
                                      hsh[:, h * HC:(h + 1) * HC].bitcast(F32), ALU.subtract).then_inc(hs_lo, 1)
                for m, q in order:
                    if m == "tokens":
                        for h in range(2):
                            tokens_lo(h, at(2 + NQ, NQ + 2 + h + 1))
                        continue
                    if m == "turn":
                        x = [t[:, q % 2, :, :].rearrange("p t c -> p (t c)") for t in (hid_l, hid_h)]
                        turned(at(2 + NQ, q + 3), x[0], x[1], M_HIDDEN + q)
                        if q == 0 and with_slice(u):
                            dve.wait_ge(sd_hi, i * US + (u + 1))
                            dve.tensor_tensor(sdl[:, :], draw[:, :], sdh[:, :].bitcast(F32),
                                              ALU.subtract).then_inc(sd_lo, 1)
                        if q in (2, 4) and makes_slice(u, final):
                            n = q // 2 - 1
                            dve.wait_ge(sg_hi, i * (2 * US) + (2 * made(u) + n + 3))
                            dve.tensor_tensor(half_slice(sgl, n), half_slice(sraw, n),
                                              half_slice(sgh, n).bitcast(F32), ALU.subtract).then_inc(sg_lo, 1)
                        continue
                    for n in (2 * chunk[m, q], 2 * chunk[m, q] + 1):
                        if n == 2 * EC - 1:
                            output_lo(0)
                        if m == "d" and q == NQ - 1:
                            h = n % 2
                            dve.wait_ge(used, at(2 * EC, n + 1))
                            dve.tensor_scalar(oe[:, h * HD:(h + 1) * HD], bank[0:CS, 4 + h, 0:HD],
                                              slot_score[:, bass.ds(i * UN + u, 1)], None, ALU.mult
                                              ).then_inc(oe_ready, 1)
                        if n == 2 * EC - 1:
                            output_lo(1)
                        if n < 2 * EC - 1 or makes_slice(u, final):
                            half_chunk_lo(n)
                    if m == "u":
                        dve.wait_ge(silu_ready, i * HJ + (hjobs(u) + q + 3))
                        dve.tensor_tensor(hid[:, q % 2, :], hid[:, q % 2, :], bank[0:CS, (2 * q + 1) % 4, 0:QT * P],
                                          ALU.mult).then_inc(hid_ready, 1)
                for h in range(2 if makes_slice(u, final) else 0):
                    shared_hidden(h, i * HJ + (hjobs(u) + NQ + h + 3))
                for n in range(2 * NT):
                    h, t = divmod(n, NT)
                    y = x2[:, t, h * HD:(h + 1) * HD]
                    dve.wait_ge(misc_done, at(MJ, M0 + M_Y + n + 1))
                    dve.tensor_tensor(y, bank[0:TN, mbank(M_Y + n), 0:HD], y, ALU.add).then_inc(misc_evac, 1)
                    if n == 3 and not makes_slice(u, final):
                        half_chunk_lo(2 * EC - 1)

            experts(dve, expert)

        @block.tensor
        def _(pe):
            def mm3(dst, sh, sl, mvh, mvl, first, last):
                pe.matmul(dst, sh, mvh, start=first, stop=False)
                pe.matmul(dst, sh, mvl, start=False, stop=False)
                return pe.matmul(dst, sl, mvh, start=False, stop=last)

            def turned_job(s, w, wait_k=None):
                for k in range(KT):
                    if wait_k:
                        wait_k(k)
                    for h in range(2):
                        c = slice(h * HC, (h + 1) * HC)
                        last = mm3(psh[:, s, h, 0:HC], piece(wh, w)[:, k, :], piece(wl, w)[:, k, :],
                                   mh[:, k, c], ml[:, k, c], k == 0, k == KT - 1)
                return last

            def free(j):
                if j >= 3:
                    pe.wait_ge(evac, j - 2)

            pe.wait_ge(const_ready, 3)
            pe.wait_ge(key_ready, 1)
            pe.transpose(ps[0:EB, 3, 0:TN], key[:, :], ident[0:TN, 0:TN]).then_inc(keyT_done, 1)

            pe.wait_ge(yn_ready, 1)
            for k in range(KT):
                j = J_Y + k
                free(j)
                for t in range(NT):
                    last = pe.transpose(ps[:, slot(j), t * P:t * P + TN], nat[:, t, k * P:(k + 1) * P],
                                        ident[0:TN, 0:TN])
                last.then_inc(pe_done, 1)

            for o in range(KT):
                j, w = J_Q + o, W_Q + o
                free(j)
                pe.wait_ge(w_lo, w + 1)
                turned_job(slot(j), w, (lambda k: pe.wait_ge(lo_ready, L_Y + k + 1)) if o == 0 else None
                           ).then_inc(pe_done, 1)

            def natural_job(o, j, tiles):
                free(j)
                w = W_KV + 2 * o
                for n, t in enumerate(tiles):
                    c = slice(t * TN, (t + 1) * TN)
                    for k in range(KT):
                        half, kk = divmod(k, KT // 2)
                        if t == 0 and kk == 0:
                            pe.wait_ge(w_lo, w + half + 1)
                        wh_, wl_ = [x[:, (w + half) % NSPL, kk * 2 * P:(kk + 1) * 2 * P] for x in (wh, wl)]
                        last = mm3(ps[0:TN, slot(j), n * 2 * P:(n + 1) * 2 * P], mh[:, k, c], ml[:, k, c],
                                   wh_, wl_, k == 0, k == KT - 1)
                last.then_inc(pe_done, 1)

            def product_job(o):
                j = P_JOB[o]
                free(j)
                pe.wait_ge(evac, B_JOB[o] + 1)
                for c, m in ((0, lambda t: vpc[:, o % 2, t, :]), (512, lambda t: ones[0:TN, :])):
                    for t in range(NT):
                        last = pe.matmul(ps[:, slot(j), c:c + P], kpc[:, o % 2, t, :], m(t),
                                         start=(t == 0), stop=(t == NT - 1))
                last.then_inc(pe_done, 1)

            def attention_jobs(h):
                for j, bd in ((DEN_JOB[h], ks_bd), (NUM_JOB[h], kv_bd)):
                    free(j)
                    pe.wait_ge(evac, P_JOB[h] + 1)
                    for c in range(2):
                        last = pe.matmul(psh[:, slot(j), c, 0:HC], bd[:, h, :], acc[:, h, c * HC:(c + 1) * HC],
                                         start=True, stop=True)
                    last.then_inc(pe_done, 1)

            for o in range(KT):
                natural_job(o, A_JOB[o], range(0, 4))
                if o:
                    product_job(o - 1)
                natural_job(o, B_JOB[o], range(4, NT))
                if 0 < o < KT - 1:
                    attention_jobs(o - 1)

            for k in range(KT):
                j = J_XT + k
                free(j)
                for t in range(NT):
                    last = pe.transpose(ps[:, slot(j), t * P:t * P + TN], xn[:, t, k * P:(k + 1) * P],
                                        ident[0:TN, 0:TN])
                last.then_inc(pe_done, 1)

            for o in range(KT):
                j, w = ROOT1_JOB[o], W_ROOT1 + o
                free(j)
                pe.wait_ge(w_lo, w + 1)
                turned_job(slot(j), w, (lambda k: pe.wait_ge(evac, J_XT + k + 1)) if o == 0 else None
                           ).then_inc(pe_done, 1)
                if o == 0:
                    attention_jobs(KT - 2)
                elif o == 1:
                    product_job(KT - 1)
                elif o == 2:
                    attention_jobs(KT - 1)

            for o in range(KT):
                j, w = J_PROJ + o, W_PROJ + o
                free(j)
                pe.wait_ge(w_lo, w + 1)
                turned_job(slot(j), w, (lambda k: pe.wait_ge(lo_ready, L_ATT + k + 1)) if o == 0 else None
                           ).then_inc(pe_done, 1)
            pe.wait_ge(xl_ready, NT)

            def relations(layer, base_j, base_w, base_l):
                with pe.Fori(0, R // 2) as i:
                    for u in range(2):
                        j, w, l = base_j + u * RJ, base_w + u * KT, base_l + u * KT
                        counts = cbuf[:, u, :].rearrange("p (t n) -> p t n", t=NT)
                        pe.wait_ge(c_in[u], i * 16 + (layer * R // 2 + 1) * 16)
                        if layer or u:
                            pe.wait_ge(inv_step, i * 2 + (layer * R + u))
                        else:
                            pe.wait_ge(inv_step, i * 2)
                        for t in range(NT):
                            for h in range(2):
                                last = pe.matmul(psh[:, 3, h, 0:HC], onesr[0:TN, :],
                                                 counts[:, t, h * HC:(h + 1) * HC], start=(t == 0),
                                                 stop=(t == NT - 1))
                        last.then_inc(cnt_done, 1)
                        for k in range(KT):
                            pe.wait_ge(evac, i * (2 * RJ) + (j + k - 2))
                            for t in range(NT):
                                for h in range(2):
                                    c = counts[:, t, h * HC:(h + 1) * HC]
                                    for x in (xh, xl):
                                        last = pe.matmul(psh[:, slot(j + k), h, 0:HC], x[:, t, k * P:(k + 1) * P], c,
                                                         start=(t == 0 and x is xh),
                                                         stop=(t == NT - 1 and x is xl))
                            last.then_inc(pe_done, 1)
                        for o in range(KT):
                            pe.wait_ge(evac, i * (2 * RJ) + (j + KT + o - 2))
                            pe.wait_ge(w_lo, i * (2 * KT) + (w + o + 1))
                            turned_job(slot(j + KT + o), w + o,
                                       (lambda k: pe.wait_ge(lo_ready, i * (2 * KT) + (l + k + 1))) if o == 0
                                       else None).then_inc(pe_done, 1)

            relations(0, J_REL1, W_REL1, L_REL1)

            def natural_turns(base_j, total):
                for t in range(NT):
                    j = base_j + t
                    free(j)
                    for k in range(KT):
                        last = pe.transpose(ps[0:TN, slot(j), k * P:(k + 1) * P], total[:, k, t * TN:(t + 1) * TN],
                                            ident[:, :])
                    last.then_inc(pe_done, 1)

            pe.wait_ge(h_ready, KT)
            natural_turns(J_HN, sum1)
            for o in range(KT):
                j, w = J_ROOT2 + o, W_ROOT2 + o
                free(j)
                pe.wait_ge(w_lo, w + 1)
                turned_job(slot(j), w, (lambda k: pe.wait_ge(lo_ready, L_H + k + 1)) if o == 0 else None
                           ).then_inc(pe_done, 1)
            relations(1, J_REL2, W_REL2, L_REL2)
            pe.wait_ge(evac, J_X2)
            natural_turns(J_X2, acc)

            def logits(k):
                pe.wait_ge(evac, J_F + k + 1)
                for h in range(2):
                    c = slice(h * HC, (h + 1) * HC)
                    last = mm3(bank[0:NE, mbank(h), 0:HC], gwh[:, k, :], gwl[:, k, :], fh[:, k, c], fl[:, k, c],
                               k == 0, k == KT - 1)
                    if k == KT - 1:
                        last.then_inc(misc_done, 1)

            pe.wait_ge(xf_ready, 1)
            for k in range(KT):
                j = J_F + k
                free(j)
                for t in range(NT):
                    last = pe.transpose(ps[:, slot(j), t * P:t * P + TN], xf[:, t, k * P:(k + 1) * P],
                                        ident[0:TN, 0:TN])
                last.then_inc(pe_done, 1)
                if k == 0:
                    pe.wait_ge(gw_lo, 1)
                    pe.wait_ge(pads_zero, 2)
                else:
                    logits(k - 1)
            logits(KT - 1)

            def shared_half(h):
                for b, o in ((2 * h, 0), (2 * h + 1, 1)):
                    for k in range(KT):
                        c = slice((o * KT + k) * SF, (o * KT + k + 1) * SF)
                        last = mm3(bank[0:SF, b, 0:HC], sgh[:, c], sgl[:, c],
                                   fh[:, k, h * HC:(h + 1) * HC], fl[:, k, h * HC:(h + 1) * HC],
                                   k == 0, k == KT - 1)
                last.then_inc(shared_done, 1)

            def tokens_turned(landed):
                pe.wait_ge(gathered, landed)
                for h in range(2):
                    for k in range(3):
                        last = pe.transpose(bank[:, mbank(M_TOKENS + h), k * CS:(k + 1) * CS],
                                            xg[:, (3 * h + k) * P:(3 * h + k + 1) * P], ident[0:CS, 0:CS])
                    last.then_inc(misc_done, 1)

            pe.wait_ge(sg_lo, 2)
            shared_half(0)
            shared_half(1)
            pe.wait_ge(top_ready, 2)
            pe.wait_ge(misc_evac, 2)
            pe.transpose(bank[0:CS, mbank(2), 0:NE], top[:, :], ident[0:NE, 0:NE]).then_inc(misc_done, 1)
            pe.transpose(bank[0:CS, mbank(3), 0:NE], topf[:, :], ident[0:NE, 0:NE]).then_inc(misc_done, 1)
            pe.wait_ge(misc_evac, 4)
            tokens_turned(16)

            def expert(i, u, final):
                def at(each, n):
                    return i * (UN * each) + (u * each + n)

                def misc_free(m):
                    pe.wait_ge(misc_evac, at(MJ, M0 + m - 1))

                def chunk_halves(m, q, product):
                    for n in (2 * chunk[m, q], 2 * chunk[m, q] + 1):
                        pe.wait_ge(half_lo, at(2 * EC, n + 1))
                        w = [t[:, n % NPC, :].rearrange("p (k f) -> p k f", k=3) for t in (eh, el)]
                        product(n % 2, *w).then_inc(used, 1)

                for m, q in order:
                    if m == "turn":
                        pe.wait_ge(hid_ready, i * HJ + (hjobs(u) + q + 3))
                        misc_free(M_HIDDEN + q)
                        for t in range(QT):
                            last = pe.transpose(bank[:, mbank(M_HIDDEN + q), t * CS:(t + 1) * CS],
                                                hid[:, q % 2, t * P:(t + 1) * P], ident[0:CS, 0:CS])
                        last.then_inc(misc_done, 1)
                    elif m == "tokens":
                        misc_free(M_TOKENS + 1)
                        tokens_turned(at(16, 32))
                    elif m == "d":
                        pe.wait_ge(misc_evac, at(MJ, M0 + M_HIDDEN + q + 1))

                        def product(half, wh_, wl_):
                            for t in range(QT):
                                last = mm3(bank[0:CS, 4 + half, 0:HD], hid_h[:, q % 2, t, :], hid_l[:, q % 2, t, :],
                                           wh_[:, t, :], wl_[:, t, :], q == 0 and t == 0,
                                           q == NQ - 1 and t == QT - 1)
                            return last

                        chunk_halves(m, q, product)
                    else:
                        if m == "g":
                            pe.wait_ge(hid_ready, i * HJ + (hjobs(u) + q + 1))

                        def product(half, wh_, wl_):
                            for k in range(3):
                                kk = 3 * half + k
                                last = mm3(bank[0:CS, (2 * q + (m == "u")) % 4, 0:QT * P], xg_h[:, kk, :],
                                           xg_l[:, kk, :], wh_[:, k, :], wl_[:, k, :], kk == 0, kk == KT - 1)
                            return last

                        chunk_halves(m, q, product)
                if makes_slice(u, final):
                    pe.wait_ge(sg_lo, i * (2 * US) + (2 * made(u) + 4))
                    shared_half(0)
                    shared_half(1)
                if with_slice(u):
                    pe.wait_ge(hs_lo, i * (2 * US) + 2 * (u + 1))
                    pe.wait_ge(sd_lo, i * US + (u + 1))
                pe.wait_ge(onehot_ready, at(1, 1))
                for n in range(2 * NT):
                    h, t = divmod(n, NT)
                    m = M_Y + n
                    misc_free(m)
                    c, d = slice(t * TN, (t + 1) * TN), slice(h * HD, (h + 1) * HD)
                    dst = bank[0:TN, mbank(m), 0:HD]
                    if with_slice(u):
                        mm3(dst, hsh[:, c], hsl[:, c], sdh[:, d], sdl[:, d], True, False)
                    if t == 0:
                        pe.wait_ge(oe_lo, at(2, h + 1))
                    pe.matmul(dst, onehot[:, c], oeh[:, d], start=not with_slice(u), stop=False)
                    pe.matmul(dst, onehot[:, c], oel[:, d], start=False, stop=True).then_inc(misc_done, 1)

            pe.wait_ge(misc_evac, M0)
            experts(pe, expert)


def _pieces(w):
    i, o = w.shape
    return np.ascontiguousarray(w.reshape(i // P, P, o // P, P).transpose(2, 1, 0, 3)).reshape(o // P, P, i)


def _kv_pieces(w):
    w = w[:, D:].reshape(2, KT // 2, P, 2, KT, P)
    return w.transpose(4, 0, 2, 1, 3, 5).reshape(2 * KT, P, D)


def _up_chunks(w):
    return w.reshape(NE, NQ, QT * P, KT, P).transpose(0, 1, 4, 3, 2).reshape(NE * NQ, P, CHUNK)


def _shared_up(w):
    return w.reshape(NSL, SF, KT, P).transpose(0, 3, 2, 1).reshape(NSL, P, KT * SF)


def _turned_vec(v):
    return np.ascontiguousarray(v.reshape(KT, P).T)


def kernel(**kw):
    import concourse.bacc as _bacc
    from concourse.bass_utils import run_bass_kernel_spmd as _run

    kw = {k: np.asarray(v) for k, v in kw.items()}
    arrays = {
        "x": kw["x"], "src": kw["src"], "dst": kw["dst"], "type": kw["edge_type_8"],
        "gamma": _turned_vec(kw["L0_mix_ln_gamma"]), "beta": _turned_vec(kw["L0_mix_ln_beta"]),
        "b_proj": _turned_vec(kw["L0_mix_b_proj"]),
        "b1": _turned_vec(kw["L0_gnn_b1"]), "b2": _turned_vec(kw["L0_gnn_b2"]),
        "wq": _pieces(kw["L0_mix_w_qkv"].T[:, :D]), "wkv": _kv_pieces(kw["L0_mix_w_qkv"].T), "wproj": _pieces(kw["L0_mix_w_proj"].T),
        "root1": _pieces(kw["L0_gnn_root1"]), "root2": _pieces(kw["L0_gnn_root2"]),
        "W1": np.concatenate([_pieces(w) for w in kw["L0_gnn_W1"]]),
        "W2": np.concatenate([_pieces(w) for w in kw["L0_gnn_W2"]]),
        "gate_weight": kw["L0_ffn_gate_weight"].T.reshape(KT, P, NE).transpose(1, 0, 2),
        "Wg": _up_chunks(kw["L0_ffn_Wg"]), "Wu": _up_chunks(kw["L0_ffn_Wu"]),
        "Wd": kw["L0_ffn_Wd"].reshape(NE, 2, HD, NQ, QT, P).transpose(0, 3, 5, 1, 4, 2).reshape(NE * NQ, P, CHUNK),
        "Ws_gu": np.stack([_shared_up(kw["L0_ffn_Ws_g"]), _shared_up(kw["L0_ffn_Ws_u"])], 2).reshape(NSL, P, -1),
        "Ws_d": kw["L0_ffn_Ws_d"].T.reshape(NSL, SF, D),
    }
    nc = _bacc.Bacc("TRN2", target_bir_lowering=False, num_devices=1)
    arrays = {"in_" + k: np.ascontiguousarray(v) for k, v in arrays.items()}
    a = {k[3:]: nc.dram_tensor(k, v.shape, mybir.dt.from_np(v.dtype), kind="ExternalInput").ap()
         for k, v in arrays.items()}
    out = nc.dram_tensor("out", (N, D), F32, kind="ExternalOutput").ap()
    build(nc, a, out)
    r = _run(nc, [arrays], core_ids=[0])
    return r.results[0]["out"]
```
